# Optimizing a Trainium2 kernel written in Bass

```python
import numpy as np
import jax
import jax.numpy as jnp

def _softmax(x, axis=-1):
    return jax.nn.softmax(x, axis=axis)

def _gelu(x):
    return jax.nn.gelu(x, approximate=True)

def _silu(x):
    return jax.nn.silu(x)

def _sigmoid(x):
    return jax.nn.sigmoid(x)

def _layernorm(x, axis=-1, eps=1e-05):
    m = jnp.mean(x, axis=axis, keepdims=True)
    v = jnp.var(x, axis=axis, keepdims=True)
    return (x - m) / jnp.sqrt(v + eps)

def _scatter_add(tgt, idx, src, axis=0):
    return tgt.at[idx].add(src)

def _segment_sum(src, seg, n):
    return jax.ops.segment_sum(src, seg, n)
kernel_name = 'mk_macaron_d2_jaxref_r8_85de09'

def setup_inputs(seed: int=0):
    np.random.seed(seed)
    _w = jnp.asarray

    def _L0_attn_setup():
        import jax, jax.numpy as jnp
        import numpy as np
        from math import sqrt
        D_MODEL = 128
        NUM_HEADS = 16
        MASK_VAL = -100000000.0

        def _proj_heads(x, w, h):
            d = w.shape[0] // h
            w = w.reshape(h, d, w.shape[1])
            return jnp.einsum('bsi,hdi->bhsd', x, w)
        key = jax.random.key(seed)
        k1, k2, k3, k4, k5 = jax.random.split(key, 5)
        scale = 1.0 / sqrt(D_MODEL)
        return {'in_features': jax.random.normal(k1, (2, 256, D_MODEL), dtype=jnp.float32), 'q_proj_weight': jax.random.normal(k2, (D_MODEL, D_MODEL), dtype=jnp.float32) * scale, 'k_proj_weight': jax.random.normal(k3, (D_MODEL, D_MODEL), dtype=jnp.float32) * scale, 'v_proj_weight': jax.random.normal(k4, (D_MODEL, D_MODEL), dtype=jnp.float32) * scale, 'o_proj_weight': jax.random.normal(k5, (D_MODEL, D_MODEL), dtype=jnp.float32) * scale}
    _L0_attn_in = _L0_attn_setup()

    def _L0_ffn_setup():
        import jax, jax.numpy as jnp
        import numpy as np
        E = 16
        K = 4
        NG = 4
        TG = 2
        SCALE = 2.5
        NORM_TOPK = True
        H = 128
        I = 64
        SH_I = I * 2
        B, S = (2, 256)
        key = jax.random.key(seed)
        ks = jax.random.split(key, 9)

        def w(k, shape, fan_in):
            return jax.random.normal(k, shape, jnp.float32) * (1.0 / np.sqrt(fan_in))
        return {'hidden_states': jax.random.normal(ks[0], (B, S, H), jnp.float32), 'gate_w': w(ks[1], (E, H), H), 'gate_bias': jnp.zeros((E,), jnp.float32), 'Wg': w(ks[2], (E, I, H), H), 'Wu': w(ks[3], (E, I, H), H), 'Wd': w(ks[4], (E, H, I), I), 'Ws_g': w(ks[5], (SH_I, H), H), 'Ws_u': w(ks[6], (SH_I, H), H), 'Ws_d': w(ks[7], (H, SH_I), SH_I)}
    _L0_ffn_in = _L0_ffn_setup()

    def _L1_attn_setup():
        import jax, jax.numpy as jnp
        import numpy as np
        B, S, D = (4, 512, 128)
        C = 8.0
        key = jax.random.key(seed)
        k_x, k_wa, k_wx, k_ba, k_bx, k_lam = jax.random.split(key, 6)
        x = jax.random.normal(k_x, (B, S, D), dtype=jnp.float32)
        std = 1.0 / np.sqrt(D)
        Wa = jax.random.normal(k_wa, (D, D), dtype=jnp.float32) * std
        Wx = jax.random.normal(k_wx, (D, D), dtype=jnp.float32) * std
        ba = jax.random.normal(k_ba, (D,), dtype=jnp.float32) * 0.02
        bx = jax.random.normal(k_bx, (D,), dtype=jnp.float32) * 0.02
        u = jax.random.uniform(k_lam, (D,), dtype=jnp.float32, minval=0.9, maxval=0.999)
        Lam = -jnp.log(jnp.power(u, -1.0 / C) - 1.0)
        return {'x': x, 'Wa': Wa, 'Wx': Wx, 'ba': ba, 'bx': bx, 'Lam': Lam}
    _L1_attn_in = _L1_attn_setup()

    def _L1_ffn_setup():
        import jax, jax.numpy as jnp
        import numpy as np
        key = jax.random.key(seed)
        ks = jax.random.split(key, 5)
        B, Sq, M, E, H = (4, 256, 128, 8, 512)
        x = jax.random.normal(ks[0], (B, Sq, M), dtype=jnp.float32)
        wg = jax.random.normal(ks[1], (M, E), dtype=jnp.float32) * (1.0 / np.sqrt(M))
        w1 = jax.random.normal(ks[2], (E, M, H), dtype=jnp.float32) * (1.0 / np.sqrt(M))
        b1 = jnp.zeros((E, H), dtype=jnp.float32)
        w2 = jax.random.normal(ks[3], (E, H, M), dtype=jnp.float32) * (1.0 / np.sqrt(H))
        b2 = jnp.zeros((E, M), dtype=jnp.float32)
        return {'x': x, 'wg': wg, 'w1': w1, 'b1': b1, 'w2': w2, 'b2': b2}
    _L1_ffn_in = _L1_ffn_setup()
    _d = {'L0_attn_in_features': _L0_attn_in['in_features'], 'L0_attn_q_proj_weight': _L0_attn_in['q_proj_weight'], 'L0_attn_k_proj_weight': _L0_attn_in['k_proj_weight'], 'L0_attn_v_proj_weight': _L0_attn_in['v_proj_weight'], 'L0_attn_o_proj_weight': _L0_attn_in['o_proj_weight'], 'L0_ffn_gate_w': _L0_ffn_in['gate_w'], 'L0_ffn_gate_bias': _L0_ffn_in['gate_bias'], 'L0_ffn_Wg': _L0_ffn_in['Wg'], 'L0_ffn_Wu': _L0_ffn_in['Wu'], 'L0_ffn_Wd': _L0_ffn_in['Wd'], 'L0_ffn_Ws_g': _L0_ffn_in['Ws_g'], 'L0_ffn_Ws_u': _L0_ffn_in['Ws_u'], 'L0_ffn_Ws_d': _L0_ffn_in['Ws_d'], 'L1_attn_Wa': _L1_attn_in['Wa'], 'L1_attn_Wx': _L1_attn_in['Wx'], 'L1_attn_ba': _L1_attn_in['ba'], 'L1_attn_bx': _L1_attn_in['bx'], 'L1_attn_Lam': _L1_attn_in['Lam'], 'L1_ffn_wg': _L1_ffn_in['wg'], 'L1_ffn_w1': _L1_ffn_in['w1'], 'L1_ffn_b1': _L1_ffn_in['b1'], 'L1_ffn_w2': _L1_ffn_in['w2'], 'L1_ffn_b2': _L1_ffn_in['b2']}
    _x0 = _d['L0_attn_in_features']
    _d['L0_attn_in_features'] = jax.random.normal(jax.random.fold_in(jax.random.key(seed), 1), (4, 512, 128), dtype=_x0.dtype)
    del _x0
    return _d

def reference(L0_attn_in_features, L0_attn_q_proj_weight, L0_attn_k_proj_weight, L0_attn_v_proj_weight, L0_attn_o_proj_weight, L0_ffn_gate_w, L0_ffn_gate_bias, L0_ffn_Wg, L0_ffn_Wu, L0_ffn_Wd, L0_ffn_Ws_g, L0_ffn_Ws_u, L0_ffn_Ws_d, L1_attn_Wa, L1_attn_Wx, L1_attn_ba, L1_attn_bx, L1_attn_Lam, L1_ffn_wg, L1_ffn_w1, L1_ffn_b1, L1_ffn_w2, L1_ffn_b2):

    def _L0_attn_ref(in_features, q_proj_weight, k_proj_weight, v_proj_weight, o_proj_weight):
        import jax, jax.numpy as jnp
        import numpy as np
        from math import sqrt
        D_MODEL = 128
        NUM_HEADS = 16
        MASK_VAL = -100000000.0

        def _proj_heads(x, w, h):
            d = w.shape[0] // h
            w = w.reshape(h, d, w.shape[1])
            return jnp.einsum('bsi,hdi->bhsd', x, w)
        h = NUM_HEADS
        b, s, _ = in_features.shape
        q = _proj_heads(in_features, q_proj_weight, h)
        k = _proj_heads(in_features, k_proj_weight, h)
        v = _proj_heads(in_features, v_proj_weight, h)
        d_k = q.shape[-1]
        mask = jnp.triu(jnp.full((s, s), MASK_VAL, dtype=q.dtype), k=1)[None, None]
        scores = jnp.einsum('bhqd,bhkd->bhqk', q, k) / sqrt(d_k) + mask
        attn = jax.nn.softmax(scores, axis=-1)
        out = jnp.einsum('bhqk,bhkd->bhqd', attn, v)
        out = out.transpose(0, 2, 1, 3).reshape(b, s, -1)
        return jnp.einsum('bsv,mv->bsm', out, o_proj_weight)

    def _L0_ffn_ref(hidden_states, gate_w, gate_bias, Wg, Wu, Wd, Ws_g, Ws_u, Ws_d):
        import jax, jax.numpy as jnp
        import numpy as np
        E = 16
        K = 4
        NG = 4
        TG = 2
        SCALE = 2.5
        NORM_TOPK = True
        H = 128
        I = 64
        SH_I = I * 2
        B, S = (2, 256)
        x = hidden_states
        b, s, h = x.shape
        n = b * s
        xf = x.reshape(n, h)
        logits = xf @ gate_w.T
        scores = jax.nn.sigmoid(logits)
        sfc = scores + gate_bias
        epg = E // NG
        grp = sfc.reshape(n, NG, epg)
        g_scores = jax.lax.top_k(grp, 2)[0].sum(-1)
        _, gidx = jax.lax.top_k(g_scores, TG)
        gmask = jax.nn.one_hot(gidx, NG, dtype=sfc.dtype).sum(1)
        emask = jnp.repeat(gmask, epg, axis=1)
        masked = jnp.where(emask > 0, sfc, -jnp.inf)
        _, topk_idx = jax.lax.top_k(masked, K)
        topk_w = jnp.take_along_axis(scores, topk_idx, axis=1)
        if K > 1 and NORM_TOPK:
            topk_w = topk_w / (topk_w.sum(-1, keepdims=True) + 1e-20)
        topk_w = topk_w * SCALE
        cw = (jax.nn.one_hot(topk_idx, E, dtype=topk_w.dtype) * topk_w[..., None]).sum(1)
        hg = jnp.einsum('nh,eih->nei', xf, Wg)
        hu = jnp.einsum('nh,eih->nei', xf, Wu)
        act = jax.nn.silu(hg) * hu
        y = jnp.einsum('nei,ne,ehi->nh', act, cw, Wd)
        shared = jax.nn.silu(xf @ Ws_g.T) * (xf @ Ws_u.T) @ Ws_d.T
        y = y + shared
        return (x + y.reshape(b, s, h)).astype(hidden_states.dtype)

    def _L1_attn_ref(x, Wa, Wx, ba, bx, Lam):
        import jax, jax.numpy as jnp
        import numpy as np
        B, S, D = (4, 512, 128)
        C = 8.0
        rt = jax.nn.sigmoid(jnp.einsum('bsd,hd->bsh', x, Wa) + ba)
        it = jax.nn.sigmoid(jnp.einsum('bsd,hd->bsh', x, Wx) + bx)
        log_a = -C * jax.nn.softplus(-Lam) * rt
        a = jnp.exp(log_a)
        b = jnp.sqrt(1.0 - a * a) * (it * x)

        def step(h, ab):
            a_t, b_t = ab
            h = a_t * h + b_t
            return (h, h)
        h0 = jnp.zeros((x.shape[0], x.shape[2]), dtype=x.dtype)
        _, y = jax.lax.scan(step, h0, (jnp.swapaxes(a, 0, 1), jnp.swapaxes(b, 0, 1)))
        return jnp.swapaxes(y, 0, 1)

    def _L1_ffn_ref(x, wg, w1, b1, w2, b2):
        import jax, jax.numpy as jnp
        import numpy as np
        B, Sq, M = x.shape
        E = wg.shape[1]
        S = B * Sq
        C = S // E
        xt = x.reshape(S, M)
        gates = jax.nn.softmax(xt @ wg, axis=-1)
        expert_idx = jnp.argmax(gates, axis=-1)
        mask1 = jax.nn.one_hot(expert_idx, E, dtype=xt.dtype)
        locations = jnp.cumsum(mask1, axis=0) - 1.0
        pos = jnp.sum(locations * mask1, axis=1).astype(jnp.int32)
        keep = (pos < C).astype(xt.dtype)
        gate_val = jnp.sum(gates * mask1, axis=1) * keep
        slot = expert_idx.astype(jnp.int32) * C + jnp.clip(pos, 0, C - 1)
        disp = jnp.zeros((E * C, M), dtype=xt.dtype).at[slot].add(xt * keep[:, None])
        disp = disp.reshape(E, C, M)
        h = jax.nn.relu(jnp.einsum('ecm,emh->ech', disp, w1) + b1[:, None, :])
        eo = jnp.einsum('ech,ehm->ecm', h, w2) + b2[:, None, :]
        out = eo.reshape(E * C, M)[slot] * gate_val[:, None]
        return out.reshape(B, Sq, M)
    x = L0_attn_in_features
    x = x + 0.5 * _L0_ffn_ref(_layernorm(x, axis=-1), L0_ffn_gate_w, L0_ffn_gate_bias, L0_ffn_Wg, L0_ffn_Wu, L0_ffn_Wd, L0_ffn_Ws_g, L0_ffn_Ws_u, L0_ffn_Ws_d)
    x = x + _L0_attn_ref(_layernorm(x, axis=-1), L0_attn_q_proj_weight, L0_attn_k_proj_weight, L0_attn_v_proj_weight, L0_attn_o_proj_weight)
    x = x + 0.5 * _L0_ffn_ref(_layernorm(x, axis=-1), L0_ffn_gate_w, L0_ffn_gate_bias, L0_ffn_Wg, L0_ffn_Wu, L0_ffn_Wd, L0_ffn_Ws_g, L0_ffn_Ws_u, L0_ffn_Ws_d)
    x = x + 0.5 * _L1_ffn_ref(_layernorm(x, axis=-1), L1_ffn_wg, L1_ffn_w1, L1_ffn_b1, L1_ffn_w2, L1_ffn_b2)
    x = x + _L1_attn_ref(_layernorm(x, axis=-1), L1_attn_Wa, L1_attn_Wx, L1_attn_ba, L1_attn_bx, L1_attn_Lam)
    x = x + 0.5 * _L1_ffn_ref(_layernorm(x, axis=-1), L1_ffn_wg, L1_ffn_w1, L1_ffn_b1, L1_ffn_w2, L1_ffn_b2)
    return x

_drawn_inputs = setup_inputs


def setup_inputs(seed=0):
    import zlib

    import numpy as np

    out = dict(_drawn_inputs(seed))
    spreads = {'L0_ffn_gate_bias': (0.0, 0.1), 'L1_ffn_b1': (0.0, 0.66), 'L1_ffn_b2': (0.0, 0.424)}
    factors = {'L1_attn_ba': 47.464, 'L1_attn_bx': 24.16}
    for name, (base, spread) in spreads.items():
        noise = np.random.default_rng([zlib.crc32(name.encode()), seed]).standard_normal(out[name].shape)
        drawn = base * np.exp(spread * noise) if base else spread * noise
        out[name] = jnp.asarray(drawn.astype(out[name].dtype))
    for name, factor in factors.items():
        out[name] = (out[name] * factor).astype(out[name].dtype)
    return out
```

```python
from contextlib import ExitStack

import concourse.bass as bass
from concourse import mybir

F32 = mybir.dt.float32
F32R = mybir.dt.float32r
BF16 = mybir.dt.bfloat16
U32 = mybir.dt.uint32
ALU = mybir.AluOpType
ACT = mybir.ActivationFunctionType
X = mybir.AxisListType.X
XY = mybir.AxisListType.XY

P = 128
B, S = 4, 512
TB = S // P
NT = B * TB
E0, I0, G0, TOPG, TOPK = 16, 64, 4, 2, 4
NH, DH = 16, 8
HG = NH // 4
E1, H1 = 8, 512
CAP = B * S // E1
HC = H1 // P
EPS = 1e-5
BIG = 1e30

C_ID, C_TRI, C_MASK, C_ME, C_MG, C_NI8, C_E256, C_CQ, C_CK, C_KB = 0, 128, 256, 384, 896, 928, 936, 944, 945, 946
C_N = 947
W_UNIT = (0, 1024, 2048)
W_GATE = 2304
W_N = 2320
Q_OFF, K_OFF, V_OFF, O_OFF, A_OFF, X_OFF, G_OFF, PJ_N = 0, 512, 1024, 1152, 1280, 1408, 1536, 1544
V_LAM, V_BA, V_BX, V_B1 = 0, 1, 2, 3
ST_F0, ST_AT, ST_F1, ST_M0, ST_RG, ST_M1 = range(6)


def unit_psum(n, q_side):
    if q_side:
        return [(0, 0, 4, 128), (1, 0, 4, 256), (2, 0, 2, 384), (2, 2, 2, 384), (3, 0, 2, 512), (3, 2, 2, 512)][n]
    return [(0, 0, 2, 512), (0, 2, 2, 512), (1, 0, 2, 384), (1, 2, 2, 384), (2, 0, 4, 256), (3, 0, 4, 128)][n]


def build(nc, x_in, wup, wdn, proj, w1, w2, vecs, bias0, b2, consts, out):
    ctx = ExitStack()
    with ctx:
        def sb(name, shape, dt=F32):
            return ctx.enter_context(nc.sbuf_tensor(name, shape, dt))

        def sem(name):
            return ctx.enter_context(nc.semaphore(name))

        xs = sb("xs", [P, NT, P])
        xn = sb("xn", [P, NT, P])
        stats = sb("stats", [P, 2, TB, 6])
        mv = sb("mv", [P, 2, TB, 2])
        veps = sb("veps", [P, 2, TB])
        mhalf = sb("mhalf", [P, TB])
        rstd = sb("rstd", [P, 2, TB])
        xh = [sb(f"xh{i}", [P, S], F32R) for i in range(2)]
        xl = [sb(f"xl{i}", [P, S], F32R) for i in range(2)]
        cst = sb("cst", [P, C_N])
        identb = sb("identb", [P, P], BF16)
        maskb = sb("maskb", [P, P], BF16)
        trib = sb("trib", [P, P], BF16)
        onesb = sb("onesb", [P, P], BF16)
        meb = sb("meb", [P, 512], BF16)
        mgb = sb("mgb", [P, 32], BF16)
        arena_f = sb("arena_f", [P, 8192])
        arena_r = sb("arena_r", [P, 8192], F32R)
        stage = arena_f[:, 0:4096]
        wuh = sb("wuh", [P, W_N], F32R)
        wul = sb("wul", [P, W_N], F32R)
        wds = sb("wds", [P, 9, P])
        pjh = sb("pjh", [P, PJ_N], F32R)
        pjl = sb("pjl", [P, PJ_N], F32R)
        w1h, w1l = arena_r[:, 0:4096], arena_r[:, 4096:8192]
        w2s = arena_f[:, 4096:8192].rearrange("p (c m) -> p c m", m=P)
        vec = sb("vec", [P, V_B1 + E1 * HC])
        b0s = sb("b0s", [P, E0])
        b2s = sb("b2s", [P, E1, P])
        sp_t = sb("sp_t", [P, 8])
        sil = sb("sil", [P, 2, 512])
        act = sb("act", [P, 3, 512])
        actT = sb("actT", [P, 2, 512])
        sig = sb("sig", [P, TB * E0])
        sfc = sb("sfc", [P, TB * E0])
        msk = sb("msk", [P, TB * E0])
        gt4 = sb("gt4", [P, 6, TB * G0 * 2])
        cmpg = sb("cmpg", [P, TB, G0, 2, G0], BF16)
        cmpe = sb("cmpe", [P, TB, E0, 2, E0], BF16)
        rank = sb("rank", [P, TB * E0])
        tsum = sb("tsum", [P, 3, TB])
        cw = sb("cw", [P, 2, TB, E0])
        qraw = [sb(f"qraw{i}", [P, S], F32R) for i in range(2)]
        qaug = [sb(f"qaug{i}", [P, S], F32R) for i in range(2)]
        qkh = sb("qkh", [P, S], F32R)
        krow = [sb(f"krow{i}", [P, S], F32R) for i in range(2)]
        kz = [arena_r[:, 2048 * i:2048 * i + 2048].rearrange("p (h s) -> p h s", h=4) for i in range(3)]
        va = [arena_f[:, 4096 + 2048 * i:6144 + 2048 * i].rearrange("p (t h c) -> p t h c", h=NH, c=32)
              for i in range(2)]
        mpad = [sb(f"mpad{i}", [P, TB, P]) for i in range(2)]
        pt = [arena_f[:, 1024 * i:1024 * i + 1024] for i in range(4)]
        pair = sb("pair", [P, 2048])
        ots = [pair[:, S * i:S * i + S] for i in range(2)]
        orec = sb("orec", [P, TB, 4])
        oh_, ol_ = sb("oh_", [P, S], F32R), sb("ol_", [P, S], F32R)
        otok = [pair[:, 1024 + S * i:1024 + S * i + S].rearrange("p (t h c) -> p t h c", t=TB, h=NH) for i in range(2)]

        lg, ex, wt, oh8 = (sb(n, [P, TB, E1]) for n in ("lg", "ex", "wt", "oh8"))
        t4 = sb("t4", [P, 10, TB])
        ohb = sb("ohb", [P, NT, E1], BF16)
        cum = sb("cum", [P, NT + 1, E1], BF16)
        g05 = sb("g05", [P, NT])
        idx_s, idx_g = sb("idx_s", [P, NT], U32), sb("idx_g", [P, NT], U32)
        xd = sb("xd", [P, NT, P])
        dh, dl = ([sb(f"{n}{i}", [P, CAP], F32R) for i in range(2)] for n in ("dh", "dl"))
        hT = [pair[:, 1024 * i:1024 * i + 1024].rearrange("p (c t) -> p c t", c=HC) for i in range(2)]
        eos = [sb(f"eos{i}", [P, CAP // P, P]) for i in range(2)]
        zrow = eos[0]
        rr, ii = arena_f[:, 0:2048], arena_f[:, 2048:4096]
        xf = xd[:, :, :].rearrange("p t d -> p (t d)")
        aa = xn[:, :, :].rearrange("p t d -> p (t d)")
        c8, one = sb("c8", [P, 1]), sb("one", [P, 1])

        ps = ctx.enter_context(nc.psum_tensor("ps", [P, 8, 512], F32))
        GU = [ps[:, 2 * i:2 * i + 2, :] for i in range(2)]
        TRB = [ps[:, 4 + i, :] for i in range(2)]
        YB = ps[:, 6, :]
        MB = ps[:, 7, :]
        SL = [ps[:, 2 * i:2 * i + 2, :].rearrange("p a b -> p (a b)") for i in range(3)]

        disp = [nc.dram_tensor(f"disp{m}", (E1 * CAP, P), F32, kind="Internal").ap() for m in range(2)]
        eo = [nc.dram_tensor(f"eo{m}", (E1 * CAP, P), F32, kind="Internal").ap() for m in range(2)]

        ident = cst[:, C_ID:C_ID + P]

        in_c, in_x, in_w, in_p, in_v = (sem(n) for n in ("in_c", "in_x", "in_w", "in_p", "in_v"))
        in_w1, in_w2 = sem("in_w1"), sem("in_w2")
        zeroed = sem("zeroed")
        c_cast = sem("c_cast")
        presets = sem("presets")
        w_hi, w_lo = sem("w_hi"), sem("w_lo")
        dve = sem("dve")
        ln_stat, ln_rstd, ln_xn = sem("ln_stat"), sem("ln_rstd"), sem("ln_xn")
        xt_hi, xt_lo = sem("xt_hi"), sem("xt_lo")
        misc, misc_free = sem("misc"), sem("misc_free")
        up_done, silu_done, mul_done, cw_done = sem("up_done"), sem("silu_done"), sem("mul_done"), sem("cw_done")
        tr_done, at_done, dn_done, y_read = sem("tr_done"), sem("at_done"), sem("dn_done"), sem("y_read")
        routed, sig_done = sem("routed"), sem("sig_done")
        p1_done, p2_done, pv_done = sem("p1_done"), sem("p2_done"), sem("pv_done")
        max_done, exp_done, tri_done, pv_read = sem("max_done"), sem("exp_done"), sem("tri_done"), sem("pv_read")
        kz_in = [sem(f"kz_in{i}") for i in range(3)]
        x_att = sem("x_att")
        o_hi, o_lo = sem("o_hi"), sem("o_lo")
        lg_sub, lg_exp = sem("lg_sub"), sem("lg_exp")
        oh_done, idx_done, scat = sem("oh_done"), sem("idx_done"), sem("scat")
        in_xd = [sem(f"in_xd{e}") for e in range(E1)]
        d_hi, up1, ha, hb, dn1, eo_done = (sem(n) for n in ("d_hi", "up1", "ha", "hb", "dn1", "eo_done"))
        eo_out = [sem(f"eo_out{i}") for i in range(2)]
        gat = [sem(f"gat{b}") for b in range(B)]
        x_m = sem("x_m")
        rg_mm, rg_sig, rg_a, rg_a2, rg_sq, rg_y = (sem(n) for n in ("rg_mm", "rg_sig", "rg_a", "rg_a2", "rg_sq", "rg_y"))
        lam_abs, lam_exp, lam_done = sem("lam_abs"), sem("lam_exp"), sem("lam_done")
        out_done = sem("out_done")

        nmisc = []
        plan_pe = []

        def use(*op):
            plan_pe.append(op)
            nmisc.append(op)

        def plan_ffn(st, s):
            use("T", st, 0)
            use("R", st, 0)
            nu = 3 * NT
            for i in range(nu + 3):
                if i < nu:
                    plan_pe.append(("up", s, i))
                if 2 <= i < nu + 2:
                    plan_pe.append(("tr", s, i - 2))
                if i >= 3:
                    plan_pe.append(("y", s, i - 3))
                b, o = divmod(i, 3 * TB)
                if b < B - 1 and o == 4:
                    use("T", st, b + 1)
                if b < B - 1 and o == 7:
                    use("R", st, b + 1)

        NG, NU = B * HG, 6 * B * HG
        STEPS = range(-14, NU + 17)

        def due(i):
            ops = []
            for name, every, shift, count in (("S", 24, -14, B), ("A", 24, -12, B), ("T", 24, -10, B), ("V", 24, -8, B),
                                              ("M", 6, 7, NG), ("Q", 6, -4, NG), ("K", 6, -3, NG), ("OT", 6, 17, NG),
                                              ("FT", 24, 37, B), ("PO", 24, 40, B)):
                n, rest = divmod(i - shift, every)
                if rest == 0 and 0 <= n < count:
                    ops.append((name, n))
            return ops

        slots = []

        def plan_att():
            for i in STEPS:
                for name, n in due(i):
                    if name == "T":
                        use("T", ST_AT, n)
                    elif name not in "SA":
                        use(name, n)
                if 0 <= i < NU:
                    slots.append(("P1", i))
                    plan_pe.append(("P1", i))
                if 0 <= i - 8 < NU:
                    slots.append(("P2", i - 8))
                    plan_pe.append(("P2", i - 8))
                if 0 <= i - 10 < NU:
                    plan_pe.append(("PV", i - 10))

        def plan_m(st, m):
            for b in range(B):
                use("T", st, b)
                use("R1", st, b)
                use("C", st, b)
            for e in range(E1 + 1):
                if e < E1:
                    use("XT", m, e)
                    plan_pe.append(("U1", m, e))
                if e:
                    plan_pe.append(("D1", m, e - 1))

        def plan_rg():
            for b in range(B):
                use("T", ST_RG, b)
                plan_pe.append(("RG", b))
            for b in range(B):
                use("YT", b)

        plan_ffn(ST_F0, 0)
        plan_att()
        plan_pe.append(("after_att",))
        plan_ffn(ST_F1, 1)
        plan_m(ST_M0, 0)
        plan_rg()
        plan_m(ST_M1, 1)
        at = {op: i for i, op in enumerate(nmisc)}
        C_CASTS = 5 + 3 + 2 + 3

        hi_at = {op: i for i, op in enumerate(op for op in nmisc if op[0] in "TQK")}
        block = ctx.enter_context(nc.Block())

        def tile(st, b, j):
            return xn[:, TB * b + j, :]

        @block.sync
        def _(sp):
            sp.dma_start(cst[:, :], consts).then_inc(in_c, 16)
            sp.dma_start(xs[:, :, :], x_in.rearrange("(t p) d -> p t d", p=P)).then_inc(in_x, 16)
            sp.dma_start(stage[:, 0:W_N], wup).then_inc(in_w, 16)
            sp.dma_start(b0s[:, :], bias0.partition_broadcast(P)).then_inc(in_v, 16)
            sp.dma_start(wds[:, :, :], wdn).then_inc(in_p, 16)

            sp.dma_start(vec[:, :], vecs).then_inc(in_v, 16)
            sp.dma_start(b2s[:, :, :], b2.partition_broadcast(P)).then_inc(in_v, 16)
            sp.wait_ge(presets, 2)
            for m in range(2):
                for t in range(0, NT, 2):
                    rows = disp[m][P * t:P * t + 2 * P, :].rearrange("(t p) d -> p t d", p=P)
                    sp.dma_start(rows, zrow[:, :, :]).then_inc(zeroed, 16)
            sp.wait_ge(w_lo, 1)
            sp.dma_start(stage[:, 0:PJ_N], proj).then_inc(in_w, 16)

            for i in STEPS:
                for name, g in due(i):
                    if name == "K":
                        sp.wait_ge(misc_free, at["K", g] + 1)
                        if g >= 3:
                            sp.wait_ge(p2_done, 6 * (g - 2))
                        for h in range(4):
                            r = slice(32 * h, 32 * h + 32)
                            sp.dma_start(kz[g % 3][r, h, :].bitcast(F32), krow[g % 2][r, :].bitcast(F32)).then_inc(kz_in[g % 3], 16)
            sp.wait_ge(pv_done, NU)
            sp.dma_start(stage, w1).then_inc(in_w1, 16)
            sp.dma_start(w2s, w2).then_inc(in_w2, 16)

            for m in range(2):
                for e in range(E1):
                    sp.wait_ge(scat, 16 * NT * (m + 1))
                    if m:
                        sp.wait_ge(rg_y, B)
                    n = CAP // P
                    sp.dma_start(xd[:, n * e:n * e + n, :],
                                 disp[m][CAP * e:CAP * e + CAP, :].rearrange("(t p) d -> p t d", p=P)).then_inc(in_xd[e], 16)
                for e in range(E1):
                    sp.wait_ge(eo_done, E1 * m + e + 1)
                    sp.dma_start(eo[m][CAP * e:CAP * e + CAP, :].rearrange("(t p) d -> p t d", p=P),
                                 eos[e % 2][:, :, :]).then_inc(eo_out[e % 2], 16)
            for b in range(B):
                sp.wait_ge(x_m, B + b + 1)
                sp.dma_start(out[S * b:S * b + S, :].rearrange("(t p) d -> p t d", p=P),
                             xs[:, TB * b:TB * b + TB, :]).then_inc(out_done, 16)
            sp.wait_ge(out_done, 16 * B)

        @block.gpsimd
        def _(pool):
            pool.memset(mhalf[:, :], -0.5).then_inc(presets, 1)
            pool.memset(zrow[:, :, :], 0.0).then_inc(presets, 1)
            pool.wait_ge(presets, 2)

            def power(st, b):
                L = B * st + b
                pool.wait_ge(ln_stat, L + 1)
                pool.tensor_tensor(rstd[:, L % 2, :], veps[:, L % 2, :], mhalf[:, :], ALU.pow).then_inc(ln_rstd, 1)

            def weigh(s, i):
                t, k = divmod(i, 3)
                if k == 2:
                    return
                n = 3 * NT * s + i
                pool.wait_ge(mul_done, n + 1)
                pool.wait_ge(routed, B * s + t // TB + 1)
                a = act[:, n % 3, :].rearrange("p (e i) -> p e i", i=I0)
                c = cw[:, (t // TB) % 2, t % TB, 8 * k:8 * k + 8].unsqueeze(2).broadcast_to([P, 8, I0])
                pool.tensor_tensor(a, a, c, ALU.mult).then_inc(cw_done, 1)

            def ffn(st, s):
                power(st, 0)
                for i in range(3 * NT):
                    b, o = divmod(i, 3 * TB)
                    if b < B - 1 and o == 2:
                        power(st, b + 1)
                    weigh(s, i)

            def attention():
                for i in STEPS:
                    for name, n in due(i):
                        if name == "A":
                            power(ST_AT, n)
                    j = i - 8
                    if 0 <= j < NU:
                        _, _, nh, w = unit_psum(j % 6, False)
                        pool.wait_ge(exp_done, j + 1)
                        d = pt[j % 4][:, 0:nh * w].rearrange("p (h q) -> p h q", h=nh)[:, :, 0:P]
                        pool.affine_select(out=d, in_=d, compare_op=ALU.is_ge, fill=0.0, base=0,
                                           pattern=[[0, nh], [1, P]], channel_multiplier=-1).then_inc(tri_done, 1)

            def moe(st, m):
                for b in range(B):
                    power(st, b)
                    pool.wait_ge(idx_done, B * m + b + 1)
                    if b == 0:
                        pool.wait_ge(zeroed, 16 * NT)
                    for t in range(TB * b, TB * b + TB):
                        pool.indirect_dma_start(
                            out=disp[m], out_offset=bass.IndirectOffsetOnAxis(ap=idx_s[:, t:t + 1], axis=0),
                            in_=xn[:, t, :], in_offset=None,
                            bounds_check=E1 * CAP - 1, oob_is_err=False).then_inc(scat, 16)
                for i in range(2):
                    pool.wait_ge(eo_out[i], 16 * (E1 // 2) * (m + 1))
                pool.wait_ge(up1, E1 * (m + 1))
                for b in range(B):
                    for t in range(TB * b, TB * b + TB):
                        pool.indirect_dma_start(
                            out=xd[:, t, :], out_offset=None, in_=eo[m],
                            in_offset=bass.IndirectOffsetOnAxis(ap=idx_g[:, t:t + 1], axis=0),
                            bounds_check=E1 * CAP - 1, oob_is_err=False).then_inc(gat[b], 16)

            ffn(ST_F0, 0)
            attention()
            ffn(ST_F1, 1)
            moe(ST_M0, 0)
            for b in range(B):
                power(ST_RG, b)
            moe(ST_M1, 1)

        @block.scalar
        def _(sc):
            def split_hi(dst, src, wait, value):
                sc.wait_ge(wait, value)
                sc.copy(dst, src).then_inc(w_hi, 1)

            sc.wait_ge(in_c, 16)
            for d, c in ((identb, C_ID), (maskb, C_MASK), (trib, C_TRI)):
                sc.copy(d[:, :], cst[:, c:c + P]).then_inc(c_cast, 1)
            sc.copy(meb[:, :], cst[:, C_ME:C_ME + 512]).then_inc(c_cast, 1)
            sc.copy(mgb[:, :], cst[:, C_MG:C_MG + 32]).then_inc(c_cast, 1)
            split_hi(wuh[:, :], stage[:, 0:W_N], in_w, 16)

            def hi(st, b):
                L = B * st + b
                sc.wait_ge(misc, at["T", st, b] + 1)
                sc.copy(xh[L % 2][:, :], MB).then_inc(xt_hi, 1)

            def scores(st, s, b):
                sc.wait_ge(misc, at["R", st, b] + 1)
                if b or s:
                    sc.wait_ge(routed, B * s + b)
                sc.activation(sig[:, :], MB[:, 0:TB * E0], ACT.Sigmoid).then_inc(misc_free, 1)

            def silu(s, i):
                n = 3 * NT * s + i
                w = 512 if i % 3 < 2 else P
                sc.wait_ge(up_done, n + 1)
                if n >= 2:
                    sc.wait_ge(mul_done, n - 1)
                sc.activation(sil[:, n % 2, 0:w], GU[n % 2][:, 0, 0:w], ACT.Silu).then_inc(silu_done, 1)

            def evac(s, i):
                n = 3 * NT * s + i
                w = 512 if i % 3 < 2 else P
                sc.wait_ge(tr_done, n + 1)
                if n >= 2:
                    sc.wait_ge(dn_done, n - 1)
                sc.copy(actT[:, n % 2, 0:w], TRB[n % 2][:, 0:w]).then_inc(at_done, 1)

            def ffn(st, s):
                hi(st, 0)
                scores(st, s, 0)
                nu = 3 * NT
                for i in range(nu + 2):
                    if s == 0 and i == 6:
                        split_hi(pjh[:, :], stage[:, 0:PJ_N], in_w, 32)
                    if s == 1 and i in (6, 9, 12, 15):
                        c = slice(1024 * (i // 3 - 2), 1024 * (i // 3 - 1))
                        split_hi(w1h[:, c], stage[:, c], in_w1, 16)
                    if i < nu:
                        silu(s, i)
                    if i >= 2:
                        evac(s, i - 2)
                    b, o = divmod(i, 3 * TB)
                    if b < B - 1 and o == 4:
                        hi(st, b + 1)
                    if b < B - 1 and o == 7:
                        scores(st, s, b + 1)

            def exp_unit(j):
                _, _, nh, w = unit_psum(j % 6, False)
                k = slots.index(("P2", j))
                src = SL[k % 3].rearrange("p (h q) -> p h q", h=nh)[:, :, 0:w]
                sc.wait_ge(p2_done, j + 1)
                if j >= 4:
                    sc.wait_ge(pv_done, j - 3)
                sc.activation(pt[j % 4][:, 0:nh * w].rearrange("p (h q) -> p h q", h=nh), src, ACT.Exp,
                              scale=DH ** -0.5).then_inc(exp_done, 1)

            def attention():
                for i in STEPS:
                    for name, n in due(i):
                        if name == "T":
                            hi(ST_AT, n)
                        if name == "V":
                            sc.wait_ge(misc, at["V", n] + 1)
                            if n >= 2:
                                sc.wait_ge(pv_done, 6 * HG * (n - 1))
                            sc.copy(va[n % 2][:, :, :, 0:DH],
                                    MB.rearrange("p (t h c) -> p t h c", h=NH, c=DH)).then_inc(misc_free, 1)
                        if name in "QK":
                            sc.wait_ge(misc, at[name, n] + 1)
                            if name == "Q":
                                sc.copy(qkh[:, :], MB).then_inc(xt_hi, 1)
                            else:
                                sc.activation(qkh[:, :], MB, ACT.Identity, bias=cst[:, C_KB:C_KB + 1]).then_inc(xt_hi, 1)
                        if name == "FT":
                            sc.wait_ge(misc, at[name, n] + 1)
                            sc.copy(oh_[:, :], MB).then_inc(o_hi, 1)
                    if 0 <= i - 8 < NU:
                        exp_unit(i - 8)
                    g, n = divmod(i - 11, 6)
                    if n == 5 and 0 <= g < NG:
                        sc.wait_ge(pv_done, 6 * g + 6)
                        if g >= 2:
                            sc.wait_ge(misc, at["OT", g - 2] + 1)
                        sc.copy(ots[g % 2], YB).then_inc(pv_read, 1)

            def moe(st, m):
                for b in range(B):
                    hi(st, b)
                    sc.wait_ge(lg_sub, B * m + b + 1)
                    sc.activation(ex[:, :, :], lg[:, :, :], ACT.Exp).then_inc(lg_exp, 1)

                def relu(e):
                    n = E1 * m + e
                    sc.wait_ge(up1, n + 1)
                    if n >= 2:
                        sc.wait_ge(dn1, n - 1)
                    for c in range(2):
                        ins = sc.activation(hT[e % 2][:, c, :], GU[e % 2][:, 0, CAP * c:CAP * c + CAP], ACT.Relu,
                                            bias=vec[:, V_B1 + HC * e + c:V_B1 + HC * e + c + 1])
                    ins.then_inc(ha, 1)

                for e in range(E1 + 1):
                    if e < E1:
                        sc.wait_ge(misc, at["XT", m, e] + 1)
                        sc.copy(dh[e % 2][:, :], MB[:, 0:CAP]).then_inc(d_hi, 1)
                    if e:
                        relu(e - 1)

            def recurrence():
                for b in range(B):
                    L = B * ST_RG + b
                    sc.wait_ge(misc, at["T", ST_RG, b] + 1)
                    sc.copy(xh[L % 2][:, :], MB)
                    sc.copy(xf[:, S * b:S * b + S], MB).then_inc(xt_hi, 1)
                    sc.wait_ge(rg_mm, b + 1)
                    for k, dst in ((0, rr), (1, ii)):
                        ins = sc.activation(dst[:, S * b:S * b + S], GU[b % 2][:, k, :], ACT.Sigmoid,
                                            bias=vec[:, V_BA + k:V_BA + k + 1])
                    ins.then_inc(rg_sig, 1)
                sc.wait_ge(lam_done, 1)
                sc.wait_ge(rg_sig, B)
                for b in range(B):
                    sl = slice(S * b, S * b + S)
                    sc.activation(aa[:, sl], rr[:, sl], ACT.Exp, scale=c8[:, 0:1]).then_inc(rg_a, 1)
                for b in range(B):
                    sl = slice(S * b, S * b + S)
                    sc.wait_ge(rg_a2, b + 1)
                    sc.activation(rr[:, sl], rr[:, sl], ACT.Sqrt, bias=one[:, 0:1], scale=-1.0).then_inc(rg_sq, 1)

            sc.wait_ge(lam_abs, 1)
            sc.activation(sp_t[:, 2:3], sp_t[:, 1:2], ACT.Exp, scale=-1.0).then_inc(lam_exp, 1)
            ffn(ST_F0, 0)
            attention()
            ffn(ST_F1, 1)
            moe(ST_M0, 0)
            recurrence()
            moe(ST_M1, 1)

        @block.vector
        def _(v):
            steps = [0]

            def did(ins):
                steps[0] += 1
                ins.then_inc(dve, 1)

            def settle():
                v.wait_ge(dve, steps[0])

            def link(ins):
                did(ins)
                settle()

            v.memset(arena_r[:, 0:6144].bitcast(F32), 0.0).then_inc(c_cast, 1)
            did(v.memset(arena_f[:, 4096:8192], 0.0))
            for i in range(2):
                v.memset(mpad[i][:, :, :], 0.0).then_inc(c_cast, 1)
            settle()
            for i in range(2):
                v.memset(va[i][:, :, :, DH], 1.0).then_inc(c_cast, 1)
            v.memset(onesb[:, :], 1.0).then_inc(c_cast, 1)
            v.memset(one[:, :], 1.0).then_inc(c_cast, 1)
            v.memset(cum[:, 0, :], 0.0).then_inc(c_cast, 1)
            v.wait_ge(w_hi, 1)
            v.tensor_tensor(wul[:, :], stage[:, 0:W_N], wuh[:, :].bitcast(F32), ALU.subtract).then_inc(w_lo, 1)

            def norm_stats(st, b):
                L = B * st + b
                for j in range(TB):
                    did(v.bn_stats(stats[:, L % 2, j, :], xs[:, TB * b + j, :]))
                settle()
                for j in range(TB):
                    did(v.bn_aggr(mv[:, L % 2, j, :], stats[:, L % 2, j, :]))
                settle()
                v.tensor_scalar(veps[:, L % 2, :], mv[:, L % 2, :, 1], EPS, None, ALU.add).then_inc(ln_stat, 1)

            def norm_apply(st, b):
                L = B * st + b
                v.wait_ge(ln_rstd, L + 1)
                for j in range(TB):
                    ins = v.tensor_scalar(tile(st, b, j), xs[:, TB * b + j, :], mv[:, L % 2, j, 0:1],
                                          rstd[:, L % 2, j:j + 1], ALU.subtract, ALU.mult)
                ins.then_inc(ln_xn, 1)

            def half_in(st, b):
                L = B * st + b
                v.wait_ge(ln_xn, L + 1)
                sl = slice(TB * b, TB * b + TB)
                did(v.scalar_tensor_tensor(xs[:, sl, :], xn[:, sl, :], 0.5, xs[:, sl, :], ALU.mult, ALU.add))

            def lo(st, b):
                L = B * st + b
                v.wait_ge(xt_hi, hi_at["T", st, b] + 1)
                v.tensor_tensor(xl[L % 2][:, :], MB, xh[L % 2][:, :].bitcast(F32), ALU.subtract).then_inc(misc_free, 1)

            def rank_of(cmp, vals, n, mask, dst, groups):
                other = vals.unsqueeze(2).broadcast_to([P, groups, n, n])
                own = vals.unsqueeze(3).broadcast_to([P, groups, n, n])
                did(v.tensor_tensor(cmp[:, :, :, 0, :], other, own, ALU.is_gt))
                did(v.tensor_tensor(cmp[:, :, :, 1, :], other, own, ALU.is_ge))
                settle()
                flat = cmp.rearrange("p t e a f -> p t (e a f)")
                m = mask.unsqueeze(1).broadcast_to([P, groups, 2 * n * n])
                link(v.tensor_tensor(flat, flat, m, ALU.mult))
                link(v.tensor_reduce(dst, cmp.rearrange("p t e a f -> p (t e) (a f)"), X, ALU.add))

            def route(st, s, b):
                v.wait_ge(misc_free, at["R", st, b] + 1)
                NE = TB * E0
                sf = sfc[:, :]
                link(v.tensor_tensor(sf.rearrange("p (t e) -> p t e", e=E0), sig[:, :].rearrange("p (t e) -> p t e", e=E0),
                                     b0s[:, :].unsqueeze(1).broadcast_to([P, TB, E0]), ALU.add))
                q = sf.rearrange("p (g c) -> p g c", c=4)
                ng = TB * G0
                mx, mn = gt4[:, 0, :].rearrange("p (g c) -> p g c", c=2), gt4[:, 1, :].rearrange("p (g c) -> p g c", c=2)
                t1, t2, t3, gs, grk, gmk = (gt4[:, 2 + n // 2, (n % 2) * ng:(n % 2) * ng + ng] for n in range(6))
                did(v.tensor_tensor(mx, q[:, :, 0:2], q[:, :, 2:4], ALU.max))
                link(v.tensor_tensor(mn, q[:, :, 0:2], q[:, :, 2:4], ALU.min))
                did(v.tensor_tensor(t1, mx[:, :, 0], mx[:, :, 1], ALU.max))
                did(v.tensor_tensor(t2, mx[:, :, 0], mx[:, :, 1], ALU.min))
                link(v.tensor_tensor(t3, mn[:, :, 0], mn[:, :, 1], ALU.max))
                link(v.tensor_tensor(t2, t2, t3, ALU.max))
                link(v.tensor_tensor(gs, t1, t2, ALU.add))
                rank_of(cmpg, gs.rearrange("p (t g) -> p t g", g=G0), G0, mgb[:, :], grk, TB)
                link(v.tensor_scalar(gmk, grk, float(TOPG), None, ALU.is_lt))
                gm = gmk.unsqueeze(2).broadcast_to([P, ng, 4])
                did(v.tensor_scalar(t1, gmk, -1.0, BIG, ALU.add, ALU.mult))
                mq = msk[:, :].rearrange("p (g c) -> p g c", c=4)
                link(v.tensor_tensor(mq, q, gm, ALU.mult))
                link(v.tensor_tensor(mq, mq, t1.unsqueeze(2).broadcast_to([P, ng, 4]), ALU.add))
                rank_of(cmpe, msk[:, :].rearrange("p (t e) -> p t e", e=E0), E0, meb[:, :], rank[:, :], TB)
                link(v.scalar_tensor_tensor(rank[:, :], rank[:, :], float(TOPK), sig[:, :], ALU.is_lt, ALU.mult))
                r3 = rank[:, :].rearrange("p (t e) -> p t e", e=E0)
                link(v.tensor_reduce(tsum[:, 0, :], r3, X, ALU.add))
                link(v.tensor_scalar(tsum[:, 1, :], tsum[:, 0, :], 1e-20, None, ALU.add))
                link(v.reciprocal(tsum[:, 2, :], tsum[:, 1, :]))
                if 4 * s + b >= 2:
                    v.wait_ge(cw_done, 2 * TB * (B * s + b - 1))
                v.scalar_tensor_tensor(cw[:, b % 2, :, :], r3, 2.5, tsum[:, 2, :].unsqueeze(2).broadcast_to([P, TB, E0]),
                                       ALU.mult, ALU.mult).then_inc(routed, 1)

            def mul(s, i):
                n = 3 * NT * s + i
                w = 512 if i % 3 < 2 else P
                v.wait_ge(silu_done, n + 1)
                if n >= 3:
                    v.wait_ge(tr_done, n - 2)
                v.tensor_tensor(act[:, n % 3, 0:w], sil[:, n % 2, 0:w], GU[n % 2][:, 1, 0:w], ALU.mult).then_inc(mul_done, 1)

            def add_y(s, t):
                v.wait_ge(dn_done, 3 * NT * s + 3 * t + 3)
                v.scalar_tensor_tensor(xs[:, t, :], YB[:, 0:P], 0.5, xs[:, t, :], ALU.mult, ALU.add).then_inc(y_read, 1)

            def ffn(st, s):
                norm_stats(st, 0)
                norm_apply(st, 0)
                lo(st, 0)
                half_in(st, 0)
                route(st, s, 0)
                nu = 3 * NT
                for i in range(nu + 3):
                    if s == 0 and i == 8:
                        v.wait_ge(w_hi, 2)
                        v.tensor_tensor(pjl[:, :], stage[:, 0:PJ_N], pjh[:, :].bitcast(F32), ALU.subtract).then_inc(w_lo, 1)
                    if s == 1 and i in (6, 9, 12, 15):
                        n = i // 3 - 2
                        c = slice(1024 * n, 1024 * n + 1024)
                        v.wait_ge(w_hi, 3 + n)
                        v.tensor_tensor(w1l[:, c], stage[:, c], w1h[:, c].bitcast(F32), ALU.subtract).then_inc(w_lo, 1)
                    if i < nu:
                        mul(s, i)
                    b, o = divmod(i, 3 * TB)
                    if b < B - 1 and o == 1:
                        norm_stats(st, b + 1)
                    if b < B - 1 and o == 3:
                        norm_apply(st, b + 1)
                    if b < B - 1 and o == 4:
                        lo(st, b + 1)
                        half_in(st, b + 1)
                    if b < B - 1 and o == 7:
                        route(st, s, b + 1)
                    if i >= 3 and (i - 3) % 3 == 2:
                        settle()
                        add_y(s, (i - 3) // 3)

            def max_unit(i):
                g, n = divmod(i, 6)
                q, h0, nh, w = unit_psum(n, True)
                src = SL[slots.index(("P1", i)) % 3].rearrange("p (h k) -> p h k", h=nh)[:, :, 0:w]
                v.wait_ge(p1_done, i + 1)
                if n == 0 and g >= 2:
                    v.wait_ge(misc, at["M", g - 2] + 1)
                dst = mpad[g % 2][:, q, :].rearrange("p (h c) -> p h c", h=4)[:, h0:h0 + nh, 24]
                v.tensor_reduce(dst, src, X, ALU.max, negate=True).then_inc(max_done, 1)

            def rows(name, g, dst, column):
                v.wait_ge(xt_hi, hi_at[name, g] + 1)
                v.scalar_tensor_tensor(dst, qkh[:, :].bitcast(F32), cst[:, column:column + 1], MB,
                                       ALU.mult, ALU.add).then_inc(misc_free, 1)

            def attention():
                for i in STEPS:
                    for name, n in due(i):
                        if name == "S":
                            settle()
                            norm_stats(ST_AT, n)
                        if name == "A":
                            norm_apply(ST_AT, n)
                        if name == "T":
                            lo(ST_AT, n)
                        if name == "M":
                            v.wait_ge(misc, at["M", n] + 1)
                            if n >= 2:
                                v.wait_ge(p2_done, 6 * (n - 1))
                            v.tensor_tensor(qaug[n % 2][:, :], qraw[n % 2][:, :].bitcast(F32), MB,
                                            ALU.add).then_inc(misc_free, 1)
                        if name == "Q":
                            if n >= 2:
                                v.wait_ge(p1_done, 6 * (n - 1))
                            rows("Q", n, qraw[n % 2][:, :], C_CQ)
                        if name == "K":
                            if n >= 2:
                                v.wait_ge(kz_in[(n - 2) % 3], 64 * ((n - 2) // 3 + 1))
                            rows("K", n, krow[n % 2][:, :], C_CK)
                        if name == "OT":
                            v.wait_ge(misc, at["OT", n] + 1)
                            if n % HG == 0 and n >= 2 * HG:
                                v.wait_ge(misc, at["FT", n // HG - 2] + 1)
                            o = MB.rearrange("p (t h c) -> p t h c", t=TB, c=32)
                            link(v.reciprocal(orec[:, :, :], o[:, :, :, DH]))
                            hg = n % HG
                            v.tensor_tensor(otok[(n // HG) % 2][:, :, 4 * hg:4 * hg + 4, :], o[:, :, :, 0:DH],
                                            orec[:, :, :].unsqueeze(3).broadcast_to([P, TB, 4, DH]),
                                            ALU.mult).then_inc(misc_free, 1)
                        if name == "FT":
                            v.wait_ge(o_hi, n + 1)
                            v.tensor_tensor(ol_[:, :], MB, oh_[:, :].bitcast(F32), ALU.subtract).then_inc(misc_free, 1)
                        if name == "PO":
                            v.wait_ge(misc, at["PO", n] + 1)
                            sl = slice(TB * n, TB * n + TB)
                            v.tensor_tensor(xs[:, sl, :], xs[:, sl, :], MB.rearrange("p (t d) -> p t d", d=P),
                                            ALU.add).then_inc(misc_free, 1)
                    if 0 <= i < NU:
                        max_unit(i)

            def add_batch(m, b):
                v.wait_ge(gat[b], 16 * TB * (m + 1))
                for t in range(TB * b, TB * b + TB):
                    ins = v.scalar_tensor_tensor(xs[:, t, :], xd[:, t, :], g05[:, t:t + 1], xs[:, t, :],
                                                 ALU.mult, ALU.add)
                ins.then_inc(x_m, 1)

            def moe(st, m):
                for b in range(B):
                    norm_stats(st, b)
                    norm_apply(st, b)
                    lo(st, b)
                    bl = slice(TB * b, TB * b + TB)
                    wide = [P, TB, E1]
                    mx, sm, gv, wm, pos, keep, base, slot, off, idx = (t4[:, n, :] for n in range(10))

                    def each(x):
                        return x.unsqueeze(2).broadcast_to(wide)

                    logits = MB[:, 0:TB * E1].rearrange("p (t e) -> p t e", e=E1)
                    v.wait_ge(misc, at["R1", st, b] + 1)
                    link(v.tensor_reduce(mx, logits, X, ALU.max))
                    did(v.tensor_tensor(lg[:, :, :], logits, each(mx), ALU.subtract))
                    settle()
                    v.engine_nop().then_inc(misc_free, 1)
                    v.engine_nop().then_inc(lg_sub, 1)
                    v.wait_ge(lg_exp, B * m + b + 1)
                    link(v.tensor_reduce(sm, ex[:, :, :], X, ALU.add))
                    link(v.reciprocal(sm, sm))
                    link(v.tensor_tensor(lg[:, :, :], ex[:, :, :], each(sm), ALU.mult))
                    link(v.tensor_reduce(gv, lg[:, :, :], X, ALU.max))
                    link(v.tensor_tensor(wt[:, :, :], lg[:, :, :], each(gv), ALU.is_equal))
                    ni = cst[:, C_NI8:C_NI8 + E1].unsqueeze(1).broadcast_to(wide)
                    link(v.tensor_tensor(wt[:, :, :], wt[:, :, :], ni, ALU.mult))
                    link(v.tensor_reduce(wm, wt[:, :, :], X, ALU.max))
                    did(v.tensor_tensor(oh8[:, :, :], wt[:, :, :], each(wm), ALU.is_equal))
                    link(v.tensor_tensor(ohb[:, bl, :], wt[:, :, :], each(wm), ALU.is_equal))
                    for t in range(TB * b, TB * b + TB):
                        link(v.tensor_tensor(cum[:, t + 1, :], cum[:, t, :], ohb[:, t, :], ALU.add))
                    v.engine_nop().then_inc(oh_done, 1)
                    v.wait_ge(misc, at["C", st, b] + 1)
                    before = MB[:, 0:TB * E1].rearrange("p (t e) -> p t e", e=E1)
                    link(v.tensor_tensor(wt[:, :, :], before, oh8[:, :, :], ALU.mult))
                    v.engine_nop().then_inc(misc_free, 1)
                    link(v.tensor_reduce(pos, wt[:, :, :], X, ALU.add))
                    e256 = cst[:, C_E256:C_E256 + E1].unsqueeze(1).broadcast_to(wide)
                    did(v.tensor_scalar(keep, pos, float(CAP), None, ALU.is_lt))
                    link(v.tensor_tensor(wt[:, :, :], oh8[:, :, :], e256, ALU.mult))
                    link(v.tensor_reduce(base, wt[:, :, :], X, ALU.add))
                    did(v.scalar_tensor_tensor(slot, pos, float(CAP - 1), base, ALU.min, ALU.add))
                    did(v.scalar_tensor_tensor(g05[:, bl], gv, 0.5, keep, ALU.mult, ALU.mult))
                    link(v.tensor_scalar(off, keep, -4096.0, 4096.0, ALU.mult, ALU.add))
                    link(v.tensor_tensor(idx, off, slot, ALU.add))
                    did(v.tensor_copy(idx_g[:, bl], slot))
                    link(v.tensor_copy(idx_s[:, bl], idx))
                    v.engine_nop().then_inc(idx_done, 1)

                def relu(e):
                    n = E1 * m + e
                    v.wait_ge(up1, n + 1)
                    if n >= 2:
                        v.wait_ge(dn1, n - 1)
                    for c in range(2, HC):
                        ins = v.tensor_scalar(hT[e % 2][:, c, :], GU[e % 2][:, 1, CAP * (c - 2):CAP * (c - 1)],
                                              vec[:, V_B1 + HC * e + c:V_B1 + HC * e + c + 1], 0.0, ALU.add, ALU.max)
                    ins.then_inc(hb, 1)

                def bias2(e):
                    n = E1 * m + e
                    v.wait_ge(dn1, n + 1)
                    if n >= 2:
                        v.wait_ge(eo_out[e % 2], 16 * (n // 2))
                    v.tensor_tensor(eos[e % 2][:, :, :], TRB[e % 2][:, 0:CAP].rearrange("p (t d) -> p t d", d=P),
                                    b2s[:, e, :].unsqueeze(1).broadcast_to([P, CAP // P, P]),
                                    ALU.add).then_inc(eo_done, 1)

                for e in range(E1 + 2):
                    if e < E1:
                        v.wait_ge(d_hi, E1 * m + e + 1)
                        v.tensor_tensor(dl[e % 2][:, :], MB[:, 0:CAP], dh[e % 2][:, :].bitcast(F32),
                                        ALU.subtract).then_inc(misc_free, 1)
                    if 1 <= e <= E1:
                        relu(e - 1)
                    if e >= 2:
                        bias2(e - 2)
                for b in range(B):
                    add_batch(m, b)

            def recurrence():
                for b in range(B):
                    norm_stats(ST_RG, b)
                    norm_apply(ST_RG, b)
                    lo(ST_RG, b)
                for b in range(B):
                    sl = slice(S * b, S * b + S)
                    v.wait_ge(rg_sig, b + 1)
                    did(v.tensor_tensor(ii[:, sl], ii[:, sl], xf[:, sl], ALU.mult))
                    v.wait_ge(rg_a, b + 1)
                    v.tensor_tensor(rr[:, sl], aa[:, sl], aa[:, sl], ALU.mult).then_inc(rg_a2, 1)
                settle()
                for b in range(B):
                    sl = slice(S * b, S * b + S)
                    v.wait_ge(rg_sq, b + 1)
                    link(v.tensor_tensor(ii[:, sl], ii[:, sl], rr[:, sl], ALU.mult))
                    v.tensor_tensor_scan(rr[:, sl], aa[:, sl], ii[:, sl], 0.0, ALU.mult, ALU.add).then_inc(rg_y, 1)
                for b in range(B):
                    v.wait_ge(misc, at["YT", b] + 1)
                    sl = slice(TB * b, TB * b + TB)
                    v.tensor_tensor(xs[:, sl, :], xs[:, sl, :], MB.rearrange("p (t d) -> p t d", d=P),
                                    ALU.add).then_inc(misc_free, 1)

            def softplus():
                neg, mag, u, r, z, z2, a, q = (sp_t[:, n:n + 1] for n in range(8))
                lam = vec[:, V_LAM:V_LAM + 1]
                v.wait_ge(in_v, 48)
                link(v.tensor_scalar(neg, lam, -1.0, None, ALU.mult))
                v.tensor_tensor(mag, lam, neg, ALU.max).then_inc(lam_abs, 1)
                v.wait_ge(lam_exp, 1)
                link(v.tensor_scalar(r, u, 2.0, None, ALU.add))
                link(v.reciprocal(r, r))
                link(v.tensor_tensor(z, u, r, ALU.mult))
                link(v.tensor_tensor(z2, z, z, ALU.mult))
                link(v.tensor_scalar(a, z2, 1.0 / 17, 1.0 / 15, ALU.mult, ALU.add))
                for k in (13, 11, 9, 7, 5, 3, 1):
                    link(v.tensor_scalar(a, a, z2, 1.0 / k, ALU.mult, ALU.add))
                link(v.tensor_tensor(a, a, z, ALU.mult))
                link(v.tensor_scalar(q, neg, 0.0, None, ALU.max))
                link(v.scalar_tensor_tensor(q, a, 2.0, q, ALU.mult, ALU.add))
                v.tensor_scalar(c8[:, :], q, -8.0, None, ALU.mult).then_inc(lam_done, 1)

            softplus()
            v.wait_ge(in_x, 16)
            v.wait_ge(c_cast, C_CASTS)
            ffn(ST_F0, 0)
            attention()
            v.wait_ge(misc_free, at["PO", B - 1] + 1)
            ffn(ST_F1, 1)
            v.wait_ge(y_read, 2 * NT)
            moe(ST_M0, 0)
            v.wait_ge(x_m, B)
            recurrence()
            v.wait_ge(misc_free, at["YT", B - 1] + 1)
            moe(ST_M1, 1)

        @block.tensor
        def _(pe):
            def three(dst, ah, al, bh, bl, start=True, stop=True):
                pe.matmul(dst, ah, bh, start=start, stop=False)
                pe.matmul(dst, al, bh, start=False, stop=False)
                return pe.matmul(dst, ah, bl, start=False, stop=stop)

            def free_bank(op):
                k = at[op]
                if k:
                    pe.wait_ge(misc_free, k)

            def T(st, b):
                L = B * st + b
                free_bank(("T", st, b))
                pe.wait_ge(ln_xn, L + 1)
                for j in range(TB):
                    ins = pe.transpose(MB[:, P * j:P * j + P], tile(st, b, j), ident)
                ins.then_inc(misc, 1)

            def R(st, b):
                L = B * st + b
                free_bank(("R", st, b))
                for j in range(TB):
                    sl = slice(P * j, P * j + P)
                    ins = three(MB[:, E0 * j:E0 * j + E0], xh[L % 2][:, sl], xl[L % 2][:, sl],
                                wuh[:, W_GATE:W_N], wul[:, W_GATE:W_N])
                ins.then_inc(misc, 1)

            def up(st, s, i):
                n = 3 * NT * s + i
                t, k = divmod(i, 3)
                b, j = divmod(t, TB)
                L = B * st + b
                w = 512 if k < 2 else P
                sl = slice(P * j, P * j + P)
                if n >= 2:
                    pe.wait_ge(mul_done, n - 1)
                for h in range(2):
                    c = slice(W_UNIT[k] + w * h, W_UNIT[k] + w * h + w)
                    ins = three(GU[n % 2][:, h, 0:w], xh[L % 2][:, sl], xl[L % 2][:, sl], wuh[:, c], wul[:, c])
                ins.then_inc(up_done, 1)

            def tr(s, i):
                n = 3 * NT * s + i
                k = i % 3
                t = i // 3
                if k < 2:
                    pe.wait_ge(cw_done, 2 * NT * s + 2 * t + k + 1)
                else:
                    pe.wait_ge(mul_done, n + 1)
                if n >= 2:
                    pe.wait_ge(at_done, n - 1)
                for c in range(4 if k < 2 else 1):
                    ins = pe.transpose(TRB[n % 2][:, P * c:P * c + P], act[:, n % 3, P * c:P * c + P], ident)
                ins.then_inc(tr_done, 1)

            def y(s, i):
                n = 3 * NT * s + i
                t, k = divmod(i, 3)
                pe.wait_ge(at_done, n + 1)
                if k == 0 and NT * s + t:
                    pe.wait_ge(y_read, NT * s + t)
                for c in range(4 if k < 2 else 1):
                    ins = pe.matmul(YB[:, 0:P], actT[:, n % 2, P * c:P * c + P], wds[:, 4 * k + c, :],
                                    start=(k == 0 and c == 0), stop=(k == 2))
                ins.then_inc(dn_done, 1)

            def V(b):
                L = B * ST_AT + b
                free_bank(("V", b))
                for j in range(TB):
                    sl = slice(P * j, P * j + P)
                    ins = three(MB[:, sl], xh[L % 2][:, sl], xl[L % 2][:, sl], pjh[:, V_OFF:V_OFF + P], pjl[:, V_OFF:V_OFF + P])
                ins.then_inc(misc, 1)

            def QK(name, g):
                L = B * ST_AT + g // HG
                free_bank((name, g))
                o = (Q_OFF if name == "Q" else K_OFF) + P * (g % HG)
                three(MB, pjh[:, o:o + P], pjl[:, o:o + P], xh[L % 2][:, :], xl[L % 2][:, :]).then_inc(misc, 1)

            def M(g):
                free_bank(("M", g))
                pe.wait_ge(max_done, 6 * g + 6)
                for q in range(TB):
                    ins = pe.transpose(MB[:, P * q:P * q + P], mpad[g % 2][:, q, :], ident)
                ins.then_inc(misc, 1)

            def slot(op):
                k = slots.index(op)
                if k >= 3:
                    name, n = slots[k - 3]
                    pe.wait_ge(max_done if name == "P1" else exp_done, n + 1)
                return SL[k % 3]

            def P1(i):
                g, n = divmod(i, 6)
                q, h0, nh, w = unit_psum(n, True)
                if n == 0:
                    pe.wait_ge(misc_free, at["K", g] + 1)
                    pe.wait_ge(kz_in[g % 3], 64 * (g // 3 + 1))
                dst = slot(("P1", i))
                step = 1024 // nh
                for h in range(nh):
                    o = step * h
                    pe.matmul(dst[:, o:o + w], qraw[g % 2][:, P * q:P * q + P], kz[g % 3][:, h0 + h, 0:w],
                              start=True, stop=False)
                    ins = pe.matmul(dst[:, o + w - P:o + w], identb[:, :], maskb[:, :], start=False, stop=True)
                ins.then_inc(p1_done, 1)

            def P2(i):
                g, n = divmod(i, 6)
                k, h0, nh, w = unit_psum(n, False)
                if n == 0:
                    pe.wait_ge(misc_free, at["M", g] + 1)
                dst = slot(("P2", i))
                step = 1024 // nh
                for h in range(nh):
                    ins = pe.matmul(dst[:, step * h:step * h + w], kz[g % 3][:, h0 + h, P * k:P * k + P],
                                    qaug[g % 2][:, S - w:S], start=True, stop=True)
                ins.then_inc(p2_done, 1)

            def PV(i):
                g, n = divmod(i, 6)
                b, hg = divmod(g, HG)
                k, h0, nh, w = unit_psum(n, False)
                if n == 0 and g:
                    pe.wait_ge(pv_read, g)
                if n == 0 and hg == 0:
                    pe.wait_ge(misc_free, at["V", b] + 1)
                pe.wait_ge(tri_done, i + 1)
                for h in range(nh):
                    r = 32 * (h0 + h)
                    ins = pe.matmul(YB[r:r + 32, S - w:S], va[b % 2][:, k, 4 * hg + h0 + h, :],
                                    pt[i % 4][:, w * h:w * h + w], start=(k == 0), stop=(k == TB - 1),
                                    tile_position=(0, r))
                ins.then_inc(pv_done, 1)

            def OT(g):
                free_bank(("OT", g))
                pe.wait_ge(pv_read, g + 1)
                for q in range(TB):
                    ins = pe.transpose(MB[:, P * q:P * q + P], ots[g % 2][:, P * q:P * q + P], ident)
                ins.then_inc(misc, 1)

            def FT(b):
                free_bank(("FT", b))
                for q in range(TB):
                    ins = pe.transpose(MB[:, P * q:P * q + P],
                                       otok[b % 2][:, q, :, :].rearrange("p h c -> p (h c)"), ident)
                ins.then_inc(misc, 1)

            def PO(b):
                free_bank(("PO", b))
                o = slice(O_OFF, O_OFF + P)
                for j in range(TB):
                    sl = slice(P * j, P * j + P)
                    ins = three(MB[:, sl], oh_[:, sl], ol_[:, sl], pjh[:, o], pjl[:, o])
                ins.then_inc(misc, 1)

            def R1(st, b):
                L = B * st + b
                free_bank(("R1", st, b))
                for j in range(TB):
                    sl = slice(P * j, P * j + P)
                    ins = three(MB[:, E1 * j:E1 * j + E1], xh[L % 2][:, sl], xl[L % 2][:, sl],
                                pjh[:, G_OFF:G_OFF + E1], pjl[:, G_OFF:G_OFF + E1])
                ins.then_inc(misc, 1)

            def C(st, b):
                m = 0 if st == ST_M0 else 1
                free_bank(("C", st, b))
                pe.wait_ge(oh_done, B * m + b + 1)
                n = TB * E1
                pe.matmul(MB[:, 0:n], trib[:, :], ohb[:, TB * b:TB * b + TB, :].rearrange("p t e -> p (t e)"),
                          start=True, stop=False)
                pe.matmul(MB[:, 0:n], onesb[:, :], cum[:, TB * b:TB * b + TB, :].rearrange("p t e -> p (t e)"),
                          start=False, stop=True).then_inc(misc, 1)

            def XT(m, e):
                free_bank(("XT", m, e))
                pe.wait_ge(in_xd[e], 16 * (m + 1))
                for t in range(CAP // P):
                    ins = pe.transpose(MB[:, P * t:P * t + P], xd[:, CAP // P * e + t, :], ident)
                ins.then_inc(misc, 1)

            def U1(m, e):
                n = E1 * m + e
                pe.wait_ge(misc_free, at["XT", m, e] + 1)
                if n >= 2:
                    pe.wait_ge(ha, n - 1)
                    pe.wait_ge(hb, n - 1)
                if n == 0:
                    pe.wait_ge(w_lo, 6)
                for c in range(HC):
                    o = slice(H1 * e + P * c, H1 * e + P * c + P)
                    ins = three(GU[e % 2][:, c // 2, CAP * (c % 2):CAP * (c % 2) + CAP], w1h[:, o], w1l[:, o],
                                dh[e % 2][:, :], dl[e % 2][:, :])
                ins.then_inc(up1, 1)

            def D1(m, e):
                n = E1 * m + e
                pe.wait_ge(ha, n + 1)
                pe.wait_ge(hb, n + 1)
                if n >= 2:
                    pe.wait_ge(eo_done, n - 1)
                if n == 0:
                    pe.wait_ge(in_w2, 16)
                for t in range(CAP // P):
                    for c in range(HC):
                        ins = pe.matmul(TRB[e % 2][:, P * t:P * t + P], hT[e % 2][:, c, P * t:P * t + P],
                                        w2s[:, HC * e + c, :], start=(c == 0), stop=(c == HC - 1))
                ins.then_inc(dn1, 1)

            def RG(b):
                L = B * ST_RG + b
                pe.wait_ge(misc_free, at["T", ST_RG, b] + 1)
                if b >= 2:
                    pe.wait_ge(rg_sig, b - 1)
                for k, o in ((0, A_OFF), (1, X_OFF)):
                    ins = three(GU[b % 2][:, k, :], pjh[:, o:o + P], pjl[:, o:o + P], xh[L % 2][:, :], xl[L % 2][:, :])
                ins.then_inc(rg_mm, 1)

            def YT(b):
                free_bank(("YT", b))
                pe.wait_ge(rg_y, b + 1)
                for j in range(TB):
                    c = S * b + P * j
                    ins = pe.transpose(MB[:, P * j:P * j + P], rr[:, c:c + P], ident)
                ins.then_inc(misc, 1)

            pe.wait_ge(in_c, 16)
            pe.wait_ge(c_cast, C_CASTS)
            seen = set()
            STEP = {"M": M, "P1": P1, "P2": P2, "PV": PV, "OT": OT, "FT": FT, "PO": PO, "R1": R1, "C": C, "XT": XT,
                    "U1": U1, "D1": D1, "RG": RG, "YT": YT}
            for op in plan_pe:
                if op[0] == "T":
                    T(*op[1:])
                elif op[0] == "R":
                    if "w" not in seen:
                        pe.wait_ge(w_lo, 1)
                        seen.add("w")
                    R(*op[1:])
                elif op[0] == "up":
                    up(ST_F0 if op[1] == 0 else ST_F1, *op[1:])
                elif op[0] == "tr":
                    tr(*op[1:])
                elif op[0] in "QK":
                    QK(*op)
                elif op[0] == "V":
                    if "p" not in seen:
                        pe.wait_ge(w_lo, 2)
                        pe.wait_ge(mul_done, 3 * NT)
                        pe.wait_ge(at_done, 3 * NT)
                        pe.wait_ge(y_read, NT)
                        seen.add("p")
                    V(*op[1:])
                elif op[0] == "after_att":
                    pe.wait_ge(max_done, NU)
                    pe.wait_ge(exp_done, NU)
                    pe.wait_ge(pv_read, NG)
                elif op[0] in STEP:
                    STEP[op[0]](*op[1:])
                elif op[0] == "y":
                    if "d" not in seen:
                        pe.wait_ge(in_p, 16)
                        seen.add("d")
                    y(*op[1:])


def constants(np):
    c = np.zeros((P, C_N), np.float32)
    r = np.arange(P)
    c[:, C_ID:C_ID + P] = np.eye(P)
    c[:, C_TRI:C_TRI + P] = r[:, None] < r[None, :]
    c[:, C_MASK:C_MASK + P] = np.where(r[None, :] > r[:, None], -BIG, 0)
    for n, at in ((E0, C_ME), (G0, C_MG)):
        e = np.arange(n)
        m = np.stack([e[None, :] > e[:, None], e[None, :] < e[:, None]], 1)
        c[:, at:at + 2 * n * n] = m.reshape(1, -1)
    c[:, C_NI8:C_NI8 + E1] = E1 - np.arange(E1)
    c[:, C_E256:C_E256 + E1] = CAP * np.arange(E1)
    q = r % 32
    c[:, C_CQ] = np.where(q // 8 == 1, -1, 0)
    c[:, C_CK] = np.where(q // 8 == 2, -1, 0) + (q == 24)
    c[:, C_KB] = q == 24
    return c


def kernel(**inputs):
    import numpy as np
    import concourse.bacc as bacc
    from concourse.bass_utils import run_bass_kernel_spmd as run

    a = {k: np.asarray(v) for k, v in inputs.items()}
    Wg, Wu = (a["L0_ffn_" + k].reshape(E0 * I0, P).T for k in ("Wg", "Wu"))
    half = E0 * I0 // 2
    wup = np.concatenate([Wg[:, :half], Wu[:, :half], Wg[:, half:], Wu[:, half:],
                          a["L0_ffn_Ws_g"].T, a["L0_ffn_Ws_u"].T, a["L0_ffn_gate_w"].T], 1)
    wdn = np.concatenate([a["L0_ffn_Wd"].transpose(0, 2, 1).reshape(E0 * I0, P), a["L0_ffn_Ws_d"].T], 0)
    wdn = wdn.reshape(9, P, P).transpose(1, 0, 2)

    def heads(w):
        w = w.T.reshape(P, NH, 1, DH)
        return np.concatenate([w, w, w, np.zeros_like(w)], 2).reshape(P, NH * 32)

    proj = np.concatenate([heads(a["L0_attn_q_proj_weight"]), heads(a["L0_attn_k_proj_weight"]),
                           a["L0_attn_v_proj_weight"].T, a["L0_attn_o_proj_weight"].T,
                           a["L1_attn_Wa"].T, a["L1_attn_Wx"].T, a["L1_ffn_wg"]], 1)
    w1 = a["L1_ffn_w1"].transpose(1, 0, 2).reshape(P, E1 * H1)
    w2 = a["L1_ffn_w2"].reshape(E1 * HC, P, P).transpose(1, 0, 2)
    vecs = np.concatenate([a["L1_attn_Lam"][:, None], a["L1_attn_ba"][:, None], a["L1_attn_bx"][:, None],
                           a["L1_ffn_b1"].reshape(E1 * HC, P).T], 1)
    laid = dict(x_in=a["L0_attn_in_features"].reshape(B * S, P), wup=wup, wdn=wdn, proj=proj, w1=w1, w2=w2,
                vecs=vecs, bias0=a["L0_ffn_gate_bias"], b2=a["L1_ffn_b2"], consts=constants(np))
    nc = bacc.Bacc("TRN2", target_bir_lowering=False, num_devices=1)
    arrays, args = {}, []
    for name, v in laid.items():
        v = np.ascontiguousarray(v)
        arrays[f"in_{name}"] = v
        args.append(nc.dram_tensor(f"in_{name}", v.shape, mybir.dt.from_np(v.dtype), kind="ExternalInput").ap())
    out = nc.dram_tensor("out_x", (B * S, P), F32, kind="ExternalOutput").ap()
    build(nc, *args, out)
    r = run(nc, [arrays], core_ids=[0])
    return r.results[0]["out_x"].reshape(B, S, P)
```

```python
from contextlib import ExitStack

import concourse.bass as bass
from concourse import mybir

F32 = mybir.dt.float32
F32R = mybir.dt.float32r
BF16 = mybir.dt.bfloat16
U32 = mybir.dt.uint32
ALU = mybir.AluOpType
ACT = mybir.ActivationFunctionType
X = mybir.AxisListType.X
XY = mybir.AxisListType.XY

P = 128
B, S = 4, 512
TB = S // P
NT = B * TB
E0, I0, G0, TOPG, TOPK = 16, 64, 4, 2, 4
NH, DH = 16, 8
HG = NH // 4
E1, H1 = 8, 512
CAP = B * S // E1
HC = H1 // P
ROW = P + 2
EPS = 1e-5
BIG = 1e30

C_ID, C_TRI, C_MASK, C_ME, C_MG, C_NI8, C_E256, C_CQ, C_CK, C_KB, C_TOK = 0, 128, 256, 384, 896, 928, 936, 944, 945, 946, 947
C_N = 979
W_UNIT = (0, 1024, 2048)
W_GATE = 2304
W_N = 2320
Q_OFF, K_OFF, V_OFF, O_OFF, A_OFF, X_OFF, G_OFF, PJ_N = 0, 512, 1024, 1152, 1280, 1408, 1536, 1544
V_LAM, V_BA, V_BX, V_B1 = 0, 1, 2, 3
ST_F0, ST_AT, ST_F1, ST_M0, ST_RG, ST_M1 = range(6)


def unit_psum(n, q_side):
    if q_side:
        return [(0, 0, 4, 128), (1, 0, 4, 256), (2, 0, 2, 384), (2, 2, 2, 384), (3, 0, 2, 512), (3, 2, 2, 512)][n]
    return [(0, 0, 2, 512), (0, 2, 2, 512), (1, 0, 2, 384), (1, 2, 2, 384), (2, 0, 4, 256), (3, 0, 4, 128)][n]


def build(nc, x_in, wup, wdn, proj, w1, w2, vecs, bias0, b2, consts, out):
    ctx = ExitStack()
    with ctx:
        def sb(name, shape, dt=F32):
            return ctx.enter_context(nc.sbuf_tensor(name, shape, dt))

        def sem(name):
            return ctx.enter_context(nc.semaphore(name))

        xs = sb("xs", [P, NT, P])
        xn = sb("xn", [P, NT, ROW])
        stats = sb("stats", [P, 2, TB, 6])
        mv = sb("mv", [P, 2, TB, 2])
        veps = sb("veps", [P, 2, TB])
        mhalf = sb("mhalf", [P, TB])
        rstd = sb("rstd", [P, 2, TB])
        xh = [sb(f"xh{i}", [P, S], F32R) for i in range(3)]
        xl = [sb(f"xl{i}", [P, S], F32R) for i in range(3)]
        cst = sb("cst", [P, C_N])
        identb = sb("identb", [P, P], BF16)
        maskb = sb("maskb", [P, P], BF16)
        trib = sb("trib", [P, P], BF16)
        onesb = sb("onesb", [P, P], BF16)
        meb = sb("meb", [P, 512], BF16)
        mgb = sb("mgb", [P, 32], BF16)
        arena_f = sb("arena_f", [P, 8192])
        arena_r = sb("arena_r", [P, 8192], F32R)
        stage = arena_f[:, 0:4096]
        wuh = sb("wuh", [P, W_N], F32R)
        wul = sb("wul", [P, W_N], F32R)
        wds = sb("wds", [P, 9, P])
        pjh = sb("pjh", [P, PJ_N], F32R)
        pjl = sb("pjl", [P, PJ_N], F32R)
        w1h, w1l = arena_r[:, 0:4096], arena_r[:, 4096:8192]
        w2s = arena_f[:, 4096:8192].rearrange("p (c m) -> p c m", m=P)
        vec = sb("vec", [P, V_B1 + E1 * HC])
        b0s = sb("b0s", [P, E0])
        b2s = sb("b2s", [P, E1, P])
        sp_t = sb("sp_t", [P, 8])
        sil = sb("sil", [P, 2, 512])
        act = sb("act", [P, 3, 512])
        actT = sb("actT", [P, 2, 512])
        sig = sb("sig", [P, TB * E0])
        sfc = sb("sfc", [P, TB * E0])
        msk = sb("msk", [P, TB * E0])
        gt4 = sb("gt4", [P, 6, TB * G0 * 2])
        cmpg = sb("cmpg", [P, TB, G0, 2, G0], BF16)
        cmpe = sb("cmpe", [P, TB, E0, 2, E0], BF16)
        rank = sb("rank", [P, TB * E0])
        tsum = sb("tsum", [P, 3, TB])
        cw = sb("cw", [P, 2, TB, E0])
        qraw = [sb(f"qraw{i}", [P, S], F32R) for i in range(2)]
        qaug = [sb(f"qaug{i}", [P, S], F32R) for i in range(2)]
        qkh = sb("qkh", [P, S], F32R)
        krow = [sb(f"krow{i}", [P, S], F32R) for i in range(2)]
        kz = [arena_r[:, 2048 * i:2048 * i + 2048].rearrange("p (h s) -> p h s", h=4) for i in range(3)]
        va = [arena_f[:, 4096 + 2048 * i:6144 + 2048 * i].rearrange("p (t h c) -> p t h c", h=NH, c=32)
              for i in range(2)]
        mpad = [sb(f"mpad{i}", [P, TB, P]) for i in range(2)]
        pt = [arena_f[:, 1024 * i:1024 * i + 1024] for i in range(4)]
        pair = sb("pair", [P, 2048])
        ots = [pair[:, S * i:S * i + S] for i in range(2)]
        orec = sb("orec", [P, TB, 4])
        oh_, ol_ = sb("oh_", [P, S], F32R), sb("ol_", [P, S], F32R)
        otok = [pair[:, 1024 + S * i:1024 + S * i + S].rearrange("p (t h c) -> p t h c", t=TB, h=NH) for i in range(2)]

        lg, ex, wt, oh8 = (sb(n, [P, TB, E1]) for n in ("lg", "ex", "wt", "oh8"))
        t4 = sb("t4", [P, 10, TB])
        ohb = sb("ohb", [P, NT, E1], BF16)
        cum = sb("cum", [P, NT + 1, E1], BF16)
        g05 = sb("g05", [P, NT])
        idx_s, idx_t = sb("idx_s", [P, NT], U32), sb("idx_t", [P, NT], U32)
        xd = sb("xd", [P, NT, ROW])
        yt = sb("yt", [P, NT, P])
        dh, dl = ([x[i][:, 0:CAP] for i in range(2)] for x in (xh, xl))
        hT = [pair[:, 1024 * i:1024 * i + 1024].rearrange("p (c t) -> p c t", c=HC) for i in range(2)]
        eos = [act[:, i, 0:CAP].rearrange("p (t d) -> p t d", d=P) for i in range(2)]
        empty = sb("empty", [P, ROW])
        rr, ii = arena_f[:, 0:2048], arena_f[:, 2048:4096]
        xf = yt[:, :, :].rearrange("p t d -> p (t d)")
        aa = xn[:, :, :].rearrange("p t d -> p (t d)")[:, 0:B * S]
        c8, one = sb("c8", [P, 1]), sb("one", [P, 1])

        ps = ctx.enter_context(nc.psum_tensor("ps", [P, 8, 512], F32))
        GU = [ps[:, 2 * i:2 * i + 2, :] for i in range(2)]
        TRB = [ps[:, 4 + i, :] for i in range(2)]
        YB = ps[:, 6, :]
        MB = ps[:, 7, :]
        SL = [ps[:, 2 * i:2 * i + 2, :].rearrange("p a b -> p (a b)") for i in range(3)]

        disp = [nc.dram_tensor(f"disp{m}", (E1 * CAP, ROW), F32, kind="Internal").ap() for m in range(2)]
        ytok = [nc.dram_tensor(f"ytok{m}", (B * S, P), F32, kind="Internal").ap() for m in range(2)]

        ident = cst[:, C_ID:C_ID + P]

        in_c, in_x, in_w, in_p, in_v = (sem(n) for n in ("in_c", "in_x", "in_w", "in_p", "in_v"))
        in_w1, in_w2, in_xr = sem("in_w1"), sem("in_w2"), sem("in_xr")
        zeroed = sem("zeroed")
        c_cast = sem("c_cast")
        presets = sem("presets")
        pool_own = sem("pool_own")
        w_hi, w_lo = sem("w_hi"), sem("w_lo")
        dve = sem("dve")
        ln_stat, ln_rstd, ln_xn = sem("ln_stat"), sem("ln_rstd"), sem("ln_xn")
        xt_hi, xt_lo = sem("xt_hi"), sem("xt_lo")
        misc, misc_free = sem("misc"), sem("misc_free")
        up_done, silu_done, mul_done, cw_done = sem("up_done"), sem("silu_done"), sem("mul_done"), sem("cw_done")
        tr_done, at_done, dn_done, y_read = sem("tr_done"), sem("at_done"), sem("dn_done"), sem("y_read")
        routed, sig_done = sem("routed"), sem("sig_done")
        p1_done, p2_done, pv_done = sem("p1_done"), sem("p2_done"), sem("pv_done")
        max_done, exp_done, tri_done, pv_read = sem("max_done"), sem("exp_done"), sem("tri_done"), sem("pv_read")
        kz_in = [sem(f"kz_in{i}") for i in range(3)]
        x_att = sem("x_att")
        o_hi, o_lo = sem("o_hi"), sem("o_lo")
        lg_sub, lg_exp = sem("lg_sub"), sem("lg_exp")
        oh_done, idx_done, scat = sem("oh_done"), sem("idx_done"), sem("scat")
        in_xd = [sem(f"in_xd{e}") for e in range(E1)]
        d_hi, up1, ha, hb, dn1, eo_done = (sem(n) for n in ("d_hi", "up1", "ha", "hb", "dn1", "eo_done"))
        eo_out = [sem(f"eo_out{i}") for i in range(2)]
        gat = [sem(f"gat{b}") for b in range(B)]
        tok2 = sem("tok2")
        x_m, eo_idx = sem("x_m"), sem("eo_idx")
        rg_mm, rg_sig, rg_a, rg_a2, rg_sq, rg_y = (sem(n) for n in ("rg_mm", "rg_sig", "rg_a", "rg_a2", "rg_sq", "rg_y"))
        lam_abs, lam_exp, lam_done = sem("lam_abs"), sem("lam_exp"), sem("lam_done")
        out_done = sem("out_done")

        NG, NU, NF = B * HG, 6 * B * HG, 3 * NT
        STEPS = range(NU + 10)
        side = {}

        def put(key, i, *op):
            side.setdefault((key, i), []).append(op)

        def front(key, i, st, b, steps):
            for n, name in steps:
                put(key, i + n, name, st, b)

        L0_FRONT = [(0, "S"), (2, "A"), (3, "T"), (5, "R"), (6, "r0"), (7, "r1"), (8, "r2"), (9, "r3"), (10, "r4")]
        L1_FRONT = [(0, "S"), (2, "A"), (3, "T"), (4, "R1"), (4, "m1"), (6, "m2"), (7, "C"), (8, "m3")]
        front("pre", 0, ST_F0, 0, L0_FRONT)
        for b in range(1, B):
            front("f0", 3 * TB * (b - 1), ST_F0, b, L0_FRONT)
        for i in range(-14, NU + 17):
            for name, every, shift, count in (("S", 24, -14, B), ("A", 24, -12, B), ("T", 24, -10, B), ("V", 24, -8, B),
                                              ("M", 6, 7, NG), ("Q", 6, -4, NG), ("K", 6, -3, NG), ("OT", 6, 17, NG),
                                              ("FT", 24, 37, B), ("PO", 24, 40, B)):
                n, rest = divmod(i - shift, every)
                if rest == 0 and 0 <= n < count:
                    if i < 0:
                        put("f0", NF + 2 + i, name, ST_AT, n)
                    elif i < len(STEPS):
                        put("at", i, name, ST_AT, n)
                    else:
                        put("f1", i - len(STEPS), name, ST_AT, n)
        front("at", NU - 2, ST_F1, 0, L0_FRONT[:4] + [(6, "r0"), (7, "r1"), (8, "r2"), (9, "r3"), (10, "r4")])
        for b in range(1, B):
            front("f1", 3 * TB * (b - 1), ST_F1, b, L0_FRONT)
        for b in range(B - 1):
            front("f1", 3 * TB * b + 15, ST_M0, b, L1_FRONT)
        front("m0", 0, ST_M0, B - 1, L1_FRONT)
        for b in range(B):
            front("m1", 10 * b, ST_M1, b, L1_FRONT)

        def beside(key, i):
            return side.get((key, i), ())

        KEYS = [("pre", 11), ("f0", NF + 3), ("at", len(STEPS)), ("f1", NF + 3), ("m0", 10), ("rg", 1), ("m1", 40)]
        nmisc, plan_pe, slots, norms = [], [], [], []

        def use(*op):
            plan_pe.append(op)
            nmisc.append(op)

        for key, count in KEYS:
            if key == "rg":
                for b in range(B):
                    norms.append((ST_RG, b))
                    use("T", ST_RG, b)
                    plan_pe.append(("RG", 0, b))
                for b in range(B):
                    use("YT", ST_RG, b)
                continue
            for i in range(count):
                for op in beside(key, i):
                    if op[0] == "S":
                        norms.append(op[1:])
                    if op[0] in ("T", "R", "R1", "C", "V", "Q", "K", "M", "OT", "FT", "PO"):
                        use(*op)
                if key in ("f0", "f1"):
                    if i < NF:
                        plan_pe.append(("up", int(key[1]), i))
                    if 2 <= i < NF + 2:
                        plan_pe.append(("tr", int(key[1]), i - 2))
                    if i >= 3:
                        plan_pe.append(("y", int(key[1]), i - 3))
                if key == "at":
                    if i < NU:
                        slots.append(("P1", i))
                        plan_pe.append(("P1", 0, i))
                    if 0 <= i - 8 < NU:
                        slots.append(("P2", i - 8))
                        plan_pe.append(("P2", 0, i - 8))
                    if i >= 10:
                        plan_pe.append(("PV", 0, i - 10))
            if key in ("m0", "m1"):
                for e in range(E1 + 1):
                    if e < E1:
                        use("XT", int(key[1]), e)
                        plan_pe.append(("U1", int(key[1]), e))
                    if e:
                        plan_pe.append(("D1", int(key[1]), e - 1))

        at = {op: i for i, op in enumerate(nmisc)}
        ln = {op: i for i, op in enumerate(norms)}
        part = {op: 2 if op[0] in (ST_M0, ST_M1) else op[1] % 2 for op in norms}

        C_CASTS = 5 + 2
        PRESETS = 3 + 1 + 2 + 2

        hi_at = {op: i for i, op in enumerate(op for op in nmisc if op[0] in "TQK")}
        block = ctx.enter_context(nc.Block())

        def tile(st, b, j):
            return xn[:, TB * b + j, 0:P]

        @block.sync
        def _(sp):
            xv = x_in.rearrange("(t p) d -> p t d", p=P)
            sp.dma_start(xs[:, 0:TB, :], xv[:, 0:TB, :]).then_inc(in_x, 16)
            sp.dma_start(cst[:, :], consts).then_inc(in_c, 16)
            sp.dma_start(stage[:, 0:W_N], wup).then_inc(in_w, 16)
            sp.dma_start(b0s[:, :], bias0.partition_broadcast(P)).then_inc(in_v, 16)
            sp.dma_start(vec[:, :], vecs).then_inc(in_v, 16)
            sp.dma_start(wds[:, :, :], wdn).then_inc(in_p, 16)
            sp.dma_start(xs[:, TB:NT, :], xv[:, TB:NT, :]).then_inc(in_xr, 16)
            sp.dma_start(b2s[:, :, :], b2.partition_broadcast(P)).then_inc(in_v, 16)
            sp.wait_ge(presets, PRESETS)
            for m in range(2):
                sp.dma_start(disp[m].rearrange("(t p) d -> p t d", p=P),
                             empty[:, :].unsqueeze(1).broadcast_to([P, NT, ROW])).then_inc(zeroed, 16)
                sp.dma_start(ytok[m].rearrange("(t p) d -> p t d", p=P),
                             empty[:, 0:P].unsqueeze(1).broadcast_to([P, NT, P])).then_inc(zeroed, 16)
            sp.wait_ge(w_lo, 1)
            sp.dma_start(stage[:, 0:PJ_N], proj).then_inc(in_w, 16)

            def key_rows(g):
                sp.wait_ge(misc_free, at["K", ST_AT, g] + 1)
                if g >= 3:
                    sp.wait_ge(p2_done, 6 * (g - 2))
                for h in range(4):
                    r = slice(32 * h, 32 * h + 32)
                    sp.dma_start(kz[g % 3][r, h, :].bitcast(F32), krow[g % 2][r, :].bitcast(F32)).then_inc(kz_in[g % 3], 16)

            for g in range(NG):
                key_rows(g)
            sp.wait_ge(pv_done, NU)
            sp.dma_start(stage, w1).then_inc(in_w1, 16)
            sp.dma_start(w2s, w2).then_inc(in_w2, 16)

            for m in range(2):
                for e in range(E1):
                    sp.wait_ge(scat, 16 * NT * (m + 1))
                    n = CAP // P
                    sp.dma_start(xd[:, n * e:n * e + n, :],
                                 disp[m][CAP * e:CAP * e + CAP, :].rearrange("(t p) d -> p t d", p=P)).then_inc(in_xd[e], 16)
                for i in range(2):
                    sp.wait_ge(eo_out[i], 16 * NT // 2 * (m + 1))
                for b in range(B):
                    sp.dma_start(yt[:, TB * b:TB * b + TB, :],
                                 ytok[m][S * b:S * b + S, :].rearrange("(t p) d -> p t d", p=P)).then_inc(gat[b], 16)
            for b in range(B):
                sp.wait_ge(x_m, B + b + 1)
                sp.dma_start(out[S * b:S * b + S, :].rearrange("(t p) d -> p t d", p=P),
                             xs[:, TB * b:TB * b + TB, :]).then_inc(out_done, 16)
            sp.wait_ge(out_done, 16 * B)

        @block.gpsimd
        def _(pool):
            pool.memset(mhalf[:, :], -0.5).then_inc(pool_own, 1)
            pool.memset(empty[:, :], 0.0).then_inc(pool_own, 1)
            pool.wait_ge(pool_own, 2)
            pool.memset(empty[:, P:P + 1], 2.0 * E1 * CAP).then_inc(presets, 1)

            def power(st, b):
                L = ln[st, b]
                pool.wait_ge(ln_stat, L + 1)
                pool.tensor_tensor(rstd[:, L % 2, :], veps[:, L % 2, :], mhalf[:, :], ALU.pow).then_inc(ln_rstd, 1)

            def weigh(s, i):
                t, k = divmod(i, 3)
                if k == 2:
                    return
                n = NF * s + i
                pool.wait_ge(mul_done, n + 1)
                pool.wait_ge(routed, B * s + t // TB + 1)
                a = act[:, n % 3, :].rearrange("p (e i) -> p e i", i=I0)
                c = cw[:, (t // TB) % 2, t % TB, 8 * k:8 * k + 8].unsqueeze(2).broadcast_to([P, 8, I0])
                pool.tensor_tensor(a, a, c, ALU.mult).then_inc(cw_done, 1)

            def diagonal(j):
                _, _, nh, w = unit_psum(j % 6, False)
                pool.wait_ge(exp_done, j + 1)
                d = pt[j % 4][:, 0:nh * w].rearrange("p (h q) -> p h q", h=nh)[:, :, 0:P]
                pool.affine_select(out=d, in_=d, compare_op=ALU.is_ge, fill=0.0, base=0,
                                   pattern=[[0, nh], [1, P]], channel_multiplier=-1).then_inc(tri_done, 1)

            def dispatch(st, b):
                m = 0 if st == ST_M0 else 1
                pool.wait_ge(idx_done, B * m + b + 1)
                if m == 0 and b == 0:
                    pool.wait_ge(zeroed, 64)
                for t in range(TB * b, TB * b + TB):
                    pool.indirect_dma_start(
                        out=disp[m], out_offset=bass.IndirectOffsetOnAxis(ap=idx_s[:, t:t + 1], axis=0),
                        in_=xn[:, t, :], in_offset=None,
                        bounds_check=E1 * CAP - 1, oob_is_err=False).then_inc(scat, 16)

            def collect(m):
                for e in range(E1):
                    pool.wait_ge(eo_done, E1 * m + e + 1)
                    pool.wait_ge(eo_idx, E1 * m + e + 1)
                    for t in range(CAP // P):
                        n = CAP // P * e + t
                        pool.indirect_dma_start(
                            out=ytok[m], out_offset=bass.IndirectOffsetOnAxis(ap=idx_t[:, n:n + 1], axis=0),
                            in_=eos[e % 2][:, t, :], in_offset=None,
                            bounds_check=B * S - 1, oob_is_err=False).then_inc(eo_out[e % 2], 16)

            def besides(key, i):
                for name, st, b in beside(key, i):
                    if name == "A":
                        power(st, b)
                    if name == "m3":
                        dispatch(st, b)

            for key, count in KEYS:
                if key == "rg":
                    for b in range(B):
                        power(ST_RG, b)
                    continue
                for i in range(count):
                    besides(key, i)
                    if key in ("f0", "f1") and i < NF:
                        weigh(int(key[1]), i)
                    if key == "at" and 0 <= i - 8 < NU:
                        diagonal(i - 8)
                if key == "pre":
                    pool.memset(arena_r[:, 0:6144].bitcast(F32), 0.0).then_inc(presets, 1)
                    pool.memset(arena_f[:, 4096:8192], 0.0).then_inc(pool_own, 1)
                    for i in range(2):
                        pool.memset(mpad[i][:, :, :], 0.0).then_inc(presets, 1)
                    pool.wait_ge(pool_own, 3)
                    for i in range(2):
                        pool.memset(va[i][:, :, :, DH], 1.0).then_inc(presets, 1)
                    pool.memset(onesb[:, :], 1.0).then_inc(presets, 1)
                    pool.memset(cum[:, 0, :], 0.0).then_inc(presets, 1)
                if key in ("m0", "m1"):
                    collect(int(key[1]))

        @block.scalar
        def _(sc):
            def split_hi(dst, src, wait, value):
                sc.wait_ge(wait, value)
                sc.copy(dst, src).then_inc(w_hi, 1)

            sc.wait_ge(in_c, 16)
            for d, c in ((identb, C_ID), (maskb, C_MASK), (trib, C_TRI)):
                sc.copy(d[:, :], cst[:, c:c + P]).then_inc(c_cast, 1)
            sc.copy(meb[:, :], cst[:, C_ME:C_ME + 512]).then_inc(c_cast, 1)
            sc.copy(mgb[:, :], cst[:, C_MG:C_MG + 32]).then_inc(c_cast, 1)
            split_hi(wuh[:, :], stage[:, 0:W_N], in_w, 16)

            def hi(st, b):
                L = ln[st, b]
                sc.wait_ge(misc, at["T", st, b] + 1)
                sc.copy(xh[part[st, b]][:, :], MB).then_inc(xt_hi, 1)

            def scores(st, b):
                s = 0 if st == ST_F0 else 1
                sc.wait_ge(misc, at["R", st, b] + 1)
                if b or s:
                    sc.wait_ge(routed, B * s + b)
                sc.activation(sig[:, :], MB[:, 0:TB * E0], ACT.Sigmoid).then_inc(misc_free, 1)

            def silu(s, i):
                n = 3 * NT * s + i
                w = 512 if i % 3 < 2 else P
                sc.wait_ge(up_done, n + 1)
                if n >= 2:
                    sc.wait_ge(mul_done, n - 1)
                sc.activation(sil[:, n % 2, 0:w], GU[n % 2][:, 0, 0:w], ACT.Silu).then_inc(silu_done, 1)

            def evac(s, i):
                n = 3 * NT * s + i
                w = 512 if i % 3 < 2 else P
                sc.wait_ge(tr_done, n + 1)
                if n >= 2:
                    sc.wait_ge(dn_done, n - 1)
                sc.copy(actT[:, n % 2, 0:w], TRB[n % 2][:, 0:w]).then_inc(at_done, 1)

            def exp_unit(j):
                _, _, nh, w = unit_psum(j % 6, False)
                k = slots.index(("P2", j))
                src = SL[k % 3].rearrange("p (h q) -> p h q", h=nh)[:, :, 0:w]
                sc.wait_ge(p2_done, j + 1)
                if j >= 4:
                    sc.wait_ge(pv_done, j - 3)
                sc.activation(pt[j % 4][:, 0:nh * w].rearrange("p (h q) -> p h q", h=nh), src, ACT.Exp,
                              scale=DH ** -0.5).then_inc(exp_done, 1)

            def besides(key, i):
                for name, st, n in beside(key, i):
                    op = (name, st, n)
                    if name == "T":
                        hi(st, n)
                    if name == "R":
                        scores(st, n)
                    if name == "V":
                        sc.wait_ge(misc, at[op] + 1)
                        if n == 0:
                            sc.wait_ge(presets, PRESETS)
                        if n >= 2:
                            sc.wait_ge(pv_done, 6 * HG * (n - 1))
                        sc.copy(va[n % 2][:, :, :, 0:DH],
                                MB.rearrange("p (t h c) -> p t h c", h=NH, c=DH)).then_inc(misc_free, 1)
                    if name == "Q":
                        sc.wait_ge(misc, at[op] + 1)
                        sc.copy(qkh[:, :], MB).then_inc(xt_hi, 1)
                    if name == "K":
                        sc.wait_ge(misc, at[op] + 1)
                        sc.activation(qkh[:, :], MB, ACT.Identity, bias=cst[:, C_KB:C_KB + 1]).then_inc(xt_hi, 1)
                    if name == "FT":
                        sc.wait_ge(misc, at[op] + 1)
                        sc.copy(oh_[:, :], MB).then_inc(o_hi, 1)
                    if name == "m1":
                        sc.wait_ge(lg_sub, (B if st == ST_M1 else 0) + n + 1)
                        sc.activation(ex[:, :, :], lg[:, :, :], ACT.Exp).then_inc(lg_exp, 1)

            def sums(g):
                sc.wait_ge(pv_done, 6 * g + 6)
                if g >= 2:
                    sc.wait_ge(misc, at["OT", ST_AT, g - 2] + 1)
                sc.copy(ots[g % 2], YB).then_inc(pv_read, 1)

            def moe(m):
                def relu(e):
                    n = E1 * m + e
                    sc.wait_ge(up1, n + 1)
                    if n >= 2:
                        sc.wait_ge(dn1, n - 1)
                    for c in range(2):
                        ins = sc.activation(hT[e % 2][:, c, :], GU[e % 2][:, 0, CAP * c:CAP * c + CAP], ACT.Relu,
                                            bias=vec[:, V_B1 + HC * e + c:V_B1 + HC * e + c + 1])
                    ins.then_inc(ha, 1)

                for e in range(E1 + 1):
                    if e < E1:
                        sc.wait_ge(misc, at["XT", m, e] + 1)
                        sc.copy(dh[e % 2][:, :], MB[:, 0:CAP]).then_inc(d_hi, 1)
                    if e:
                        relu(e - 1)

            def recurrence():
                for b in range(B):
                    sc.wait_ge(misc, at["T", ST_RG, b] + 1)
                    sc.copy(xh[part[ST_RG, b]][:, :], MB)
                    sc.copy(xf[:, S * b:S * b + S], MB).then_inc(xt_hi, 1)
                    sc.wait_ge(rg_mm, b + 1)
                    for k, dst in ((0, rr), (1, ii)):
                        ins = sc.activation(dst[:, S * b:S * b + S], GU[b % 2][:, k, :], ACT.Sigmoid,
                                            bias=vec[:, V_BA + k:V_BA + k + 1])
                    ins.then_inc(rg_sig, 1)
                sc.wait_ge(lam_done, 1)
                sc.wait_ge(rg_sig, B)
                for b in range(B):
                    sl = slice(S * b, S * b + S)
                    sc.activation(aa[:, sl], rr[:, sl], ACT.Exp, scale=c8[:, 0:1]).then_inc(rg_a, 1)
                for b in range(B):
                    sl = slice(S * b, S * b + S)
                    sc.wait_ge(rg_a2, b + 1)
                    sc.activation(rr[:, sl], rr[:, sl], ACT.Sqrt, bias=one[:, 0:1], scale=-1.0).then_inc(rg_sq, 1)

            for key, count in KEYS:
                if key == "rg":
                    recurrence()
                    continue
                for i in range(count):
                    besides(key, i)
                    if key == "at" and i == 8:
                        sc.wait_ge(lam_abs, 1)
                        sc.activation(sp_t[:, 2:3], sp_t[:, 1:2], ACT.Exp, scale=-1.0).then_inc(lam_exp, 1)
                    if key == "f0" and i == 9:
                        split_hi(pjh[:, :], stage[:, 0:PJ_N], in_w, 32)
                    if key == "f1" and i in (20, 23, 26, 29):
                        c = slice(1024 * (i // 3 - 6), 1024 * (i // 3 - 5))
                        split_hi(w1h[:, c], stage[:, c], in_w1, 16)
                    if key in ("f0", "f1"):
                        if i < NF:
                            silu(int(key[1]), i)
                        if 2 <= i < NF + 2:
                            evac(int(key[1]), i - 2)
                    if key == "at":
                        if 0 <= i - 8 < NU:
                            exp_unit(i - 8)
                        if i % 6 == 4 and i >= 16:
                            sums(i // 6 - 2)
                if key == "at":
                    sums(NG - 1)
                if key in ("m0", "m1"):
                    moe(int(key[1]))

        @block.vector
        def _(v):
            steps = [0]

            def did(ins):
                steps[0] += 1
                ins.then_inc(dve, 1)

            def settle():
                v.wait_ge(dve, steps[0])

            def link(ins):
                did(ins)
                settle()

            v.memset(one[:, :], 1.0).then_inc(c_cast, 1)
            v.wait_ge(in_c, 16)
            v.tensor_copy(xn[:, :, P:ROW], cst[:, C_TOK:C_N].rearrange("p (t c) -> p t c", c=2)).then_inc(c_cast, 1)
            def split_lo(dst, src, high, count):
                v.wait_ge(w_hi, count)
                v.tensor_tensor(dst, src, high.bitcast(F32), ALU.subtract).then_inc(w_lo, 1)

            def norm_stats(st, b):
                L = ln[st, b]
                for j in range(TB):
                    did(v.bn_stats(stats[:, L % 2, j, :], xs[:, TB * b + j, :]))
                settle()
                for j in range(TB):
                    did(v.bn_aggr(mv[:, L % 2, j, :], stats[:, L % 2, j, :]))
                settle()
                v.tensor_scalar(veps[:, L % 2, :], mv[:, L % 2, :, 1], EPS, None, ALU.add).then_inc(ln_stat, 1)

            def norm_apply(st, b):
                L = ln[st, b]
                v.wait_ge(ln_rstd, L + 1)
                for j in range(TB):
                    ins = v.tensor_scalar(tile(st, b, j), xs[:, TB * b + j, :], mv[:, L % 2, j, 0:1],
                                          rstd[:, L % 2, j:j + 1], ALU.subtract, ALU.mult)
                ins.then_inc(ln_xn, 1)

            def half_in(st, b):
                L = ln[st, b]
                v.wait_ge(ln_xn, L + 1)
                sl = slice(TB * b, TB * b + TB)
                did(v.scalar_tensor_tensor(xs[:, sl, :], xn[:, sl, 0:P], 0.5, xs[:, sl, :], ALU.mult, ALU.add))

            def lo(st, b):
                L = ln[st, b]
                v.wait_ge(xt_hi, hi_at["T", st, b] + 1)
                v.tensor_tensor(xl[part[st, b]][:, :], MB, xh[part[st, b]][:, :].bitcast(F32), ALU.subtract).then_inc(misc_free, 1)

            def compare(cmp, vals, n, groups):
                other = vals.unsqueeze(2).broadcast_to([P, groups, n, n])
                own = vals.unsqueeze(3).broadcast_to([P, groups, n, n])
                did(v.tensor_tensor(cmp[:, :, :, 0, :], other, own, ALU.is_gt))
                did(v.tensor_tensor(cmp[:, :, :, 1, :], other, own, ALU.is_ge))

            def tally(cmp, n, mask, dst, groups):
                flat = cmp.rearrange("p t e a f -> p t (e a f)")
                link(v.tensor_tensor(flat, flat, mask.unsqueeze(1).broadcast_to([P, groups, 2 * n * n]), ALU.mult))
                did(v.tensor_reduce(dst, cmp.rearrange("p t e a f -> p (t e) (a f)"), X, ALU.add))

            def rank_of(cmp, vals, n, mask, dst, groups):
                compare(cmp, vals, n, groups)
                settle()
                tally(cmp, n, mask, dst, groups)
                settle()

            NE, ng = TB * E0, TB * G0
            sf = sfc[:, :]
            q = sf.rearrange("p (g c) -> p g c", c=4)
            mx, mn = gt4[:, 0, :].rearrange("p (g c) -> p g c", c=2), gt4[:, 1, :].rearrange("p (g c) -> p g c", c=2)
            t1, t2, t3, gs, grk, gmk = (gt4[:, 2 + n // 2, (n % 2) * ng:(n % 2) * ng + ng] for n in range(6))
            mq = msk[:, :].rearrange("p (g c) -> p g c", c=4)
            r3 = rank[:, :].rearrange("p (t e) -> p t e", e=E0)

            def group_scores(st, b):
                v.wait_ge(misc_free, at["R", st, b] + 1)
                link(v.tensor_tensor(sf.rearrange("p (t e) -> p t e", e=E0), sig[:, :].rearrange("p (t e) -> p t e", e=E0),
                                     b0s[:, :].unsqueeze(1).broadcast_to([P, TB, E0]), ALU.add))
                did(v.tensor_tensor(mx, q[:, :, 0:2], q[:, :, 2:4], ALU.max))
                link(v.tensor_tensor(mn, q[:, :, 0:2], q[:, :, 2:4], ALU.min))
                did(v.tensor_tensor(t1, mx[:, :, 0], mx[:, :, 1], ALU.max))
                did(v.tensor_tensor(t2, mx[:, :, 0], mx[:, :, 1], ALU.min))
                link(v.tensor_tensor(t3, mn[:, :, 0], mn[:, :, 1], ALU.max))
                link(v.tensor_tensor(t2, t2, t3, ALU.max))
                did(v.tensor_tensor(gs, t1, t2, ALU.add))

            def group_mask():
                settle()
                rank_of(cmpg, gs.rearrange("p (t g) -> p t g", g=G0), G0, mgb[:, :], grk, TB)
                link(v.tensor_scalar(gmk, grk, float(TOPG), None, ALU.is_lt))
                did(v.tensor_scalar(t1, gmk, -1.0, BIG, ALU.add, ALU.mult))
                link(v.tensor_tensor(mq, q, gmk.unsqueeze(2).broadcast_to([P, ng, 4]), ALU.mult))
                did(v.tensor_tensor(mq, mq, t1.unsqueeze(2).broadcast_to([P, ng, 4]), ALU.add))

            def weights(st, b):
                nb = (0 if st == ST_F0 else B) + b
                settle()
                link(v.scalar_tensor_tensor(rank[:, :], rank[:, :], float(TOPK), sig[:, :], ALU.is_lt, ALU.mult))
                link(v.tensor_reduce(tsum[:, 0, :], r3, X, ALU.add))
                link(v.tensor_scalar(tsum[:, 1, :], tsum[:, 0, :], 1e-20, None, ALU.add))
                link(v.reciprocal(tsum[:, 2, :], tsum[:, 1, :]))
                if nb >= 2:
                    v.wait_ge(cw_done, 2 * TB * (nb - 1))
                v.scalar_tensor_tensor(cw[:, b % 2, :, :], r3, 2.5, tsum[:, 2, :].unsqueeze(2).broadcast_to([P, TB, E0]),
                                       ALU.mult, ALU.mult).then_inc(routed, 1)

            def mul(s, i):
                n = 3 * NT * s + i
                w = 512 if i % 3 < 2 else P
                v.wait_ge(silu_done, n + 1)
                if n >= 3:
                    v.wait_ge(tr_done, n - 2)
                v.tensor_tensor(act[:, n % 3, 0:w], sil[:, n % 2, 0:w], GU[n % 2][:, 1, 0:w], ALU.mult).then_inc(mul_done, 1)

            def add_y(s, t):
                v.wait_ge(dn_done, 3 * NT * s + 3 * t + 3)
                v.scalar_tensor_tensor(xs[:, t, :], YB[:, 0:P], 0.5, xs[:, t, :], ALU.mult, ALU.add).then_inc(y_read, 1)

            def max_unit(i):
                g, n = divmod(i, 6)
                q, h0, nh, w = unit_psum(n, True)
                src = SL[slots.index(("P1", i)) % 3].rearrange("p (h k) -> p h k", h=nh)[:, :, 0:w]
                v.wait_ge(p1_done, i + 1)
                if n == 0 and g >= 2:
                    v.wait_ge(misc, at["M", ST_AT, g - 2] + 1)
                dst = mpad[g % 2][:, q, :].rearrange("p (h c) -> p h c", h=4)[:, h0:h0 + nh, 24]
                v.tensor_reduce(dst, src, X, ALU.max, negate=True).then_inc(max_done, 1)

            def rows(name, g, dst, column):
                v.wait_ge(xt_hi, hi_at[name, ST_AT, g] + 1)
                v.scalar_tensor_tensor(dst, qkh[:, :].bitcast(F32), cst[:, column:column + 1], MB,
                                       ALU.mult, ALU.add).then_inc(misc_free, 1)

            def besides(key, i):
                for name, st, n in beside(key, i):
                    op = (name, st, n)
                    if name == "S":
                        if st == ST_F0 and n == 1:
                            v.wait_ge(in_xr, 16)
                        settle_xs(st, n)
                        norm_stats(st, n)
                    if name == "A":
                        norm_apply(st, n)
                    if name == "T":
                        lo(st, n)
                        if st in (ST_F0, ST_F1):
                            half_in(st, n)
                    if name == "r0":
                        group_scores(st, n)
                    if name == "r1":
                        group_mask()
                    if name == "r2":
                        settle()
                        compare(cmpe, msk[:, :].rearrange("p (t e) -> p t e", e=E0), E0, TB)
                    if name == "r3":
                        settle()
                        tally(cmpe, E0, meb[:, :], rank[:, :], TB)
                    if name == "r4":
                        weights(st, n)
                    if name == "m1":
                        gates(st, n)
                    if name == "m2":
                        first_choice(st, n)
                    if name == "m3":
                        positions(st, n)
                    if name == "M":
                        v.wait_ge(misc, at[op] + 1)
                        if n >= 2:
                            v.wait_ge(p2_done, 6 * (n - 1))
                        v.tensor_tensor(qaug[n % 2][:, :], qraw[n % 2][:, :].bitcast(F32), MB,
                                        ALU.add).then_inc(misc_free, 1)
                    if name == "Q":
                        if n >= 2:
                            v.wait_ge(p1_done, 6 * (n - 1))
                        rows("Q", n, qraw[n % 2][:, :], C_CQ)
                    if name == "K":
                        if n >= 2:
                            v.wait_ge(kz_in[(n - 2) % 3], 64 * ((n - 2) // 3 + 1))
                        rows("K", n, krow[n % 2][:, :], C_CK)
                    if name == "OT":
                        v.wait_ge(misc, at[op] + 1)
                        if n % HG == 0 and n >= 2 * HG:
                            v.wait_ge(misc, at["FT", ST_AT, n // HG - 2] + 1)
                        o = MB.rearrange("p (t h c) -> p t h c", t=TB, c=32)
                        link(v.reciprocal(orec[:, :, :], o[:, :, :, DH]))
                        hg = n % HG
                        v.tensor_tensor(otok[(n // HG) % 2][:, :, 4 * hg:4 * hg + 4, :], o[:, :, :, 0:DH],
                                        orec[:, :, :].unsqueeze(3).broadcast_to([P, TB, 4, DH]),
                                        ALU.mult).then_inc(misc_free, 1)
                    if name == "FT":
                        v.wait_ge(o_hi, n + 1)
                        v.tensor_tensor(ol_[:, :], MB, oh_[:, :].bitcast(F32), ALU.subtract).then_inc(misc_free, 1)
                    if name == "PO":
                        v.wait_ge(misc, at[op] + 1)
                        sl = slice(TB * n, TB * n + TB)
                        v.tensor_tensor(xs[:, sl, :], xs[:, sl, :], MB.rearrange("p (t d) -> p t d", d=P),
                                        ALU.add).then_inc(misc_free, 1)

            def settle_xs(st, b):
                if st == ST_AT:
                    v.wait_ge(y_read, TB * (b + 1))
                if st == ST_F1:
                    v.wait_ge(misc_free, at["PO", ST_AT, b] + 1)
                if st == ST_M0:
                    v.wait_ge(y_read, NT + TB * (b + 1))
                if st == ST_RG:
                    v.wait_ge(x_m, b + 1)
                if st == ST_M1:
                    v.wait_ge(misc_free, at["YT", ST_RG, b] + 1)

            def add_batch(m, b):
                v.wait_ge(gat[b], 16 * (m + 1))
                for t in range(TB * b, TB * b + TB):
                    ins = v.scalar_tensor_tensor(xs[:, t, :], yt[:, t, :], g05[:, t:t + 1], xs[:, t, :],
                                                 ALU.mult, ALU.add)
                ins.then_inc(x_m, 1)

            wide = [P, TB, E1]
            t_mx, t_sm, t_gv, t_wm, t_pos, t_keep, t_base, t_slot, t_off, t_idx = (t4[:, n, :] for n in range(10))

            def each(x):
                return x.unsqueeze(2).broadcast_to(wide)

            def gates(st, b):
                logits = MB[:, 0:TB * E1].rearrange("p (t e) -> p t e", e=E1)
                v.wait_ge(misc, at["R1", st, b] + 1)
                link(v.tensor_reduce(t_mx, logits, X, ALU.max))
                link(v.tensor_tensor(lg[:, :, :], logits, each(t_mx), ALU.subtract))
                v.engine_nop().then_inc(misc_free, 1)
                v.engine_nop().then_inc(lg_sub, 1)

            def first_choice(st, b):
                m = 0 if st == ST_M0 else 1
                bl = slice(TB * b, TB * b + TB)
                v.wait_ge(lg_exp, B * m + b + 1)
                link(v.tensor_reduce(t_sm, ex[:, :, :], X, ALU.add))
                link(v.reciprocal(t_sm, t_sm))
                link(v.tensor_tensor(lg[:, :, :], ex[:, :, :], each(t_sm), ALU.mult))
                link(v.tensor_reduce(t_gv, lg[:, :, :], X, ALU.max))
                link(v.tensor_tensor(wt[:, :, :], lg[:, :, :], each(t_gv), ALU.is_equal))
                ni = cst[:, C_NI8:C_NI8 + E1].unsqueeze(1).broadcast_to(wide)
                link(v.tensor_tensor(wt[:, :, :], wt[:, :, :], ni, ALU.mult))
                link(v.tensor_reduce(t_wm, wt[:, :, :], X, ALU.max))
                did(v.tensor_tensor(oh8[:, :, :], wt[:, :, :], each(t_wm), ALU.is_equal))
                link(v.tensor_tensor(ohb[:, bl, :], wt[:, :, :], each(t_wm), ALU.is_equal))
                for t in range(TB * b, TB * b + TB):
                    link(v.tensor_tensor(cum[:, t + 1, :], cum[:, t, :], ohb[:, t, :], ALU.add))
                v.engine_nop().then_inc(oh_done, 1)

            def positions(st, b):
                bl = slice(TB * b, TB * b + TB)
                v.wait_ge(misc, at["C", st, b] + 1)
                before = MB[:, 0:TB * E1].rearrange("p (t e) -> p t e", e=E1)
                link(v.tensor_tensor(wt[:, :, :], before, oh8[:, :, :], ALU.mult))
                v.engine_nop().then_inc(misc_free, 1)
                link(v.tensor_reduce(t_pos, wt[:, :, :], X, ALU.add))
                e256 = cst[:, C_E256:C_E256 + E1].unsqueeze(1).broadcast_to(wide)
                did(v.tensor_scalar(t_keep, t_pos, float(CAP), None, ALU.is_lt))
                link(v.tensor_tensor(wt[:, :, :], oh8[:, :, :], e256, ALU.mult))
                did(v.tensor_reduce(t_base, wt[:, :, :], X, ALU.add))
                did(v.tensor_scalar(t_off, t_keep, -4096.0, 4096.0, ALU.mult, ALU.add))
                did(v.scalar_tensor_tensor(g05[:, bl], t_gv, 0.5, t_keep, ALU.mult, ALU.mult))
                settle()
                link(v.tensor_tensor(t_slot, t_pos, t_base, ALU.add))
                link(v.tensor_tensor(t_idx, t_off, t_slot, ALU.add))
                v.tensor_copy(idx_s[:, bl], t_idx).then_inc(idx_done, 1)

            def moe(m):
                def relu(e):
                    n = E1 * m + e
                    v.wait_ge(up1, n + 1)
                    if n >= 2:
                        v.wait_ge(dn1, n - 1)
                    for c in range(2, HC):
                        ins = v.tensor_scalar(hT[e % 2][:, c, :], GU[e % 2][:, 1, CAP * (c - 2):CAP * (c - 1)],
                                              vec[:, V_B1 + HC * e + c:V_B1 + HC * e + c + 1], 0.0, ALU.add, ALU.max)
                    ins.then_inc(hb, 1)

                def bias2(e):
                    n = E1 * m + e
                    v.wait_ge(dn1, n + 1)
                    if n >= 2:
                        v.wait_ge(eo_out[e % 2], 32 * (n // 2))
                    v.tensor_tensor(eos[e % 2][:, :, :], TRB[e % 2][:, 0:CAP].rearrange("p (t d) -> p t d", d=P),
                                    b2s[:, e, :].unsqueeze(1).broadcast_to([P, CAP // P, P]),
                                    ALU.add).then_inc(eo_done, 1)

                for e in range(E1 + 2):
                    if e < E1:
                        n = slice(CAP // P * e, CAP // P * (e + 1))
                        v.wait_ge(in_xd[e], 16 * (m + 1))
                        v.tensor_copy(idx_t[:, n], xd[:, n, P]).then_inc(eo_idx, 1)
                        v.wait_ge(d_hi, E1 * m + e + 1)
                        v.tensor_tensor(dl[e % 2][:, :], MB[:, 0:CAP], dh[e % 2][:, :].bitcast(F32),
                                        ALU.subtract).then_inc(misc_free, 1)
                    if 1 <= e <= E1:
                        relu(e - 1)
                    if e >= 2:
                        bias2(e - 2)
                for b in range(B):
                    add_batch(m, b)

            def recurrence():
                for b in range(B):
                    settle_xs(ST_RG, b)
                    norm_stats(ST_RG, b)
                    norm_apply(ST_RG, b)
                    lo(ST_RG, b)
                for b in range(B):
                    sl = slice(S * b, S * b + S)
                    v.wait_ge(rg_sig, b + 1)
                    did(v.tensor_tensor(ii[:, sl], ii[:, sl], xf[:, sl], ALU.mult))
                    v.wait_ge(rg_a, b + 1)
                    v.tensor_tensor(rr[:, sl], aa[:, sl], aa[:, sl], ALU.mult).then_inc(rg_a2, 1)
                settle()
                for b in range(B):
                    sl = slice(S * b, S * b + S)
                    v.wait_ge(rg_sq, b + 1)
                    link(v.tensor_tensor(ii[:, sl], ii[:, sl], rr[:, sl], ALU.mult))
                    v.tensor_tensor_scan(rr[:, sl], aa[:, sl], ii[:, sl], 0.0, ALU.mult, ALU.add).then_inc(rg_y, 1)
                for b in range(B):
                    v.wait_ge(misc, at["YT", ST_RG, b] + 1)
                    sl = slice(TB * b, TB * b + TB)
                    v.tensor_tensor(xs[:, sl, :], xs[:, sl, :], MB.rearrange("p (t d) -> p t d", d=P),
                                    ALU.add).then_inc(misc_free, 1)

            neg, mag, u, r, z, z2, a, q8 = (sp_t[:, n:n + 1] for n in range(8))
            lam = vec[:, V_LAM:V_LAM + 1]

            def magnitude():
                v.wait_ge(in_v, 48)
                link(v.tensor_scalar(neg, lam, -1.0, None, ALU.mult))
                v.tensor_tensor(mag, lam, neg, ALU.max).then_inc(lam_abs, 1)

            def softplus():
                v.wait_ge(lam_exp, 1)
                link(v.tensor_scalar(r, u, 2.0, None, ALU.add))
                link(v.reciprocal(r, r))
                link(v.tensor_tensor(z, u, r, ALU.mult))
                link(v.tensor_tensor(z2, z, z, ALU.mult))
                link(v.tensor_scalar(a, z2, 1.0 / 17, 1.0 / 15, ALU.mult, ALU.add))
                for k in (13, 11, 9, 7, 5, 3, 1):
                    link(v.tensor_scalar(a, a, z2, 1.0 / k, ALU.mult, ALU.add))
                link(v.tensor_tensor(a, a, z, ALU.mult))
                link(v.tensor_scalar(q8, neg, 0.0, None, ALU.max))
                link(v.scalar_tensor_tensor(q8, a, 2.0, q8, ALU.mult, ALU.add))
                v.tensor_scalar(c8[:, :], q8, -8.0, None, ALU.mult).then_inc(lam_done, 1)

            v.wait_ge(in_x, 16)
            besides("pre", 0)
            besides("pre", 2)
            besides("pre", 3)
            split_lo(wul[:, :], stage[:, 0:W_N], wuh[:, :], 1)
            magnitude()
            v.wait_ge(c_cast, C_CASTS)
            for i in range(4, 11):
                besides("pre", i)
            for key, count in KEYS[1:]:
                if key == "rg":
                    recurrence()
                    continue
                if key == "m1":
                    v.tensor_copy(xn[:, :, P:ROW], cst[:, C_TOK:C_N].rearrange("p (t c) -> p t c", c=2)).then_inc(tok2, 1)
                    v.wait_ge(tok2, 1)
                for i in range(count):
                    besides(key, i)
                    if key == "f0" and i == 11:
                        split_lo(pjl[:, :], stage[:, 0:PJ_N], pjh[:, :], 2)
                    if key == "f1" and i in (21, 24, 27, 30):
                        n = i // 3 - 7
                        c = slice(1024 * n, 1024 * n + 1024)
                        split_lo(w1l[:, c], stage[:, c], w1h[:, c], 3 + n)
                    if key in ("f0", "f1"):
                        if i < NF:
                            mul(int(key[1]), i)
                        if i >= 3 and i % 3 == 2:
                            settle()
                            add_y(int(key[1]), i // 3 - 1)
                    if key == "at" and i < NU:
                        max_unit(i)
                    if key == "at" and i == 16:
                        softplus()
                if key in ("m0", "m1"):
                    moe(int(key[1]))

        @block.tensor
        def _(pe):
            def three(dst, ah, al, bh, bl, start=True, stop=True):
                pe.matmul(dst, ah, bh, start=start, stop=False)
                pe.matmul(dst, al, bh, start=False, stop=False)
                return pe.matmul(dst, ah, bl, start=False, stop=stop)

            def free_bank(op):
                k = at[op]
                if k:
                    pe.wait_ge(misc_free, k)

            def T(st, b):
                L = ln[st, b]
                free_bank(("T", st, b))
                pe.wait_ge(ln_xn, L + 1)
                for j in range(TB):
                    ins = pe.transpose(MB[:, P * j:P * j + P], tile(st, b, j), ident)
                ins.then_inc(misc, 1)

            def R(st, b):
                L = ln[st, b]
                free_bank(("R", st, b))
                for j in range(TB):
                    sl = slice(P * j, P * j + P)
                    ins = three(MB[:, E0 * j:E0 * j + E0], xh[part[st, b]][:, sl], xl[part[st, b]][:, sl],
                                wuh[:, W_GATE:W_N], wul[:, W_GATE:W_N])
                ins.then_inc(misc, 1)

            def up(s, i):
                st = ST_F1 if s else ST_F0
                n = 3 * NT * s + i
                t, k = divmod(i, 3)
                b, j = divmod(t, TB)
                L = ln[st, b]
                w = 512 if k < 2 else P
                sl = slice(P * j, P * j + P)
                if n >= 2:
                    pe.wait_ge(mul_done, n - 1)
                if s == 1 and i < 2:
                    pe.wait_ge(max_done, NU)
                    pe.wait_ge(exp_done, NU)
                for h in range(2):
                    c = slice(W_UNIT[k] + w * h, W_UNIT[k] + w * h + w)
                    ins = three(GU[n % 2][:, h, 0:w], xh[part[st, b]][:, sl], xl[part[st, b]][:, sl], wuh[:, c], wul[:, c])
                ins.then_inc(up_done, 1)

            def tr(s, i):
                n = 3 * NT * s + i
                k = i % 3
                t = i // 3
                if k < 2:
                    pe.wait_ge(cw_done, 2 * NT * s + 2 * t + k + 1)
                else:
                    pe.wait_ge(mul_done, n + 1)
                if n >= 2:
                    pe.wait_ge(at_done, n - 1)
                for c in range(4 if k < 2 else 1):
                    ins = pe.transpose(TRB[n % 2][:, P * c:P * c + P], act[:, n % 3, P * c:P * c + P], ident)
                ins.then_inc(tr_done, 1)

            def y(s, i):
                n = 3 * NT * s + i
                t, k = divmod(i, 3)
                pe.wait_ge(at_done, n + 1)
                if k == 0 and NT * s + t:
                    pe.wait_ge(y_read, NT * s + t)
                if k == 0 and s == 1 and t == 0:
                    pe.wait_ge(pv_read, NG)
                for c in range(4 if k < 2 else 1):
                    ins = pe.matmul(YB[:, 0:P], actT[:, n % 2, P * c:P * c + P], wds[:, 4 * k + c, :],
                                    start=(k == 0 and c == 0), stop=(k == 2))
                ins.then_inc(dn_done, 1)

            def V(st, b):
                free_bank(("V", st, b))
                for j in range(TB):
                    sl = slice(P * j, P * j + P)
                    ins = three(MB[:, sl], xh[part[st, b]][:, sl], xl[part[st, b]][:, sl], pjh[:, V_OFF:V_OFF + P], pjl[:, V_OFF:V_OFF + P])
                ins.then_inc(misc, 1)

            def QK(name, st, g):
                b = g // HG
                free_bank((name, st, g))
                o = (Q_OFF if name == "Q" else K_OFF) + P * (g % HG)
                three(MB, pjh[:, o:o + P], pjl[:, o:o + P], xh[part[st, b]][:, :], xl[part[st, b]][:, :]).then_inc(misc, 1)

            def M(st, g):
                free_bank(("M", st, g))
                pe.wait_ge(max_done, 6 * g + 6)
                for q in range(TB):
                    ins = pe.transpose(MB[:, P * q:P * q + P], mpad[g % 2][:, q, :], ident)
                ins.then_inc(misc, 1)

            def slot(op):
                k = slots.index(op)
                if k >= 3:
                    name, n = slots[k - 3]
                    pe.wait_ge(max_done if name == "P1" else exp_done, n + 1)
                return SL[k % 3]

            def P1(_, i):
                g, n = divmod(i, 6)
                q, h0, nh, w = unit_psum(n, True)
                if i == 0:
                    pe.wait_ge(mul_done, NF)
                    pe.wait_ge(at_done, NF)
                    pe.wait_ge(y_read, NT)
                if n == 0:
                    pe.wait_ge(misc_free, at["K", ST_AT, g] + 1)
                    pe.wait_ge(kz_in[g % 3], 64 * (g // 3 + 1))
                dst = slot(("P1", i))
                step = 1024 // nh
                for h in range(nh):
                    o = step * h
                    pe.matmul(dst[:, o:o + w], qraw[g % 2][:, P * q:P * q + P], kz[g % 3][:, h0 + h, 0:w],
                              start=True, stop=False)
                    ins = pe.matmul(dst[:, o + w - P:o + w], identb[:, :], maskb[:, :], start=False, stop=True)
                ins.then_inc(p1_done, 1)

            def P2(_, i):
                g, n = divmod(i, 6)
                k, h0, nh, w = unit_psum(n, False)
                if n == 0:
                    pe.wait_ge(misc_free, at["M", ST_AT, g] + 1)
                dst = slot(("P2", i))
                step = 1024 // nh
                for h in range(nh):
                    ins = pe.matmul(dst[:, step * h:step * h + w], kz[g % 3][:, h0 + h, P * k:P * k + P],
                                    qaug[g % 2][:, S - w:S], start=True, stop=True)
                ins.then_inc(p2_done, 1)

            def PV(_, i):
                g, n = divmod(i, 6)
                b, hg = divmod(g, HG)
                k, h0, nh, w = unit_psum(n, False)
                if n == 0 and g:
                    pe.wait_ge(pv_read, g)
                if n == 0 and hg == 0:
                    pe.wait_ge(misc_free, at["V", ST_AT, b] + 1)
                pe.wait_ge(tri_done, i + 1)
                for h in range(nh):
                    r = 32 * (h0 + h)
                    ins = pe.matmul(YB[r:r + 32, S - w:S], va[b % 2][:, k, 4 * hg + h0 + h, :],
                                    pt[i % 4][:, w * h:w * h + w], start=(k == 0), stop=(k == TB - 1),
                                    tile_position=(0, r))
                ins.then_inc(pv_done, 1)

            def OT(st, g):
                free_bank(("OT", st, g))
                pe.wait_ge(pv_read, g + 1)
                for q in range(TB):
                    ins = pe.transpose(MB[:, P * q:P * q + P], ots[g % 2][:, P * q:P * q + P], ident)
                ins.then_inc(misc, 1)

            def FT(st, b):
                free_bank(("FT", st, b))
                for q in range(TB):
                    ins = pe.transpose(MB[:, P * q:P * q + P],
                                       otok[b % 2][:, q, :, :].rearrange("p h c -> p (h c)"), ident)
                ins.then_inc(misc, 1)

            def PO(st, b):
                free_bank(("PO", st, b))
                o = slice(O_OFF, O_OFF + P)
                for j in range(TB):
                    sl = slice(P * j, P * j + P)
                    ins = three(MB[:, sl], oh_[:, sl], ol_[:, sl], pjh[:, o], pjl[:, o])
                ins.then_inc(misc, 1)

            def R1(st, b):
                L = ln[st, b]
                free_bank(("R1", st, b))
                for j in range(TB):
                    sl = slice(P * j, P * j + P)
                    ins = three(MB[:, E1 * j:E1 * j + E1], xh[part[st, b]][:, sl], xl[part[st, b]][:, sl],
                                pjh[:, G_OFF:G_OFF + E1], pjl[:, G_OFF:G_OFF + E1])
                ins.then_inc(misc, 1)

            def C(st, b):
                m = 0 if st == ST_M0 else 1
                free_bank(("C", st, b))
                pe.wait_ge(oh_done, B * m + b + 1)
                n = TB * E1
                pe.matmul(MB[:, 0:n], trib[:, :], ohb[:, TB * b:TB * b + TB, :].rearrange("p t e -> p (t e)"),
                          start=True, stop=False)
                pe.matmul(MB[:, 0:n], onesb[:, :], cum[:, TB * b:TB * b + TB, :].rearrange("p t e -> p (t e)"),
                          start=False, stop=True).then_inc(misc, 1)

            def XT(m, e):
                free_bank(("XT", m, e))
                pe.wait_ge(in_xd[e], 16 * (m + 1))
                for t in range(CAP // P):
                    ins = pe.transpose(MB[:, P * t:P * t + P], xd[:, CAP // P * e + t, 0:P], ident)
                ins.then_inc(misc, 1)

            def U1(m, e):
                n = E1 * m + e
                pe.wait_ge(misc_free, at["XT", m, e] + 1)
                if n >= 2:
                    pe.wait_ge(ha, n - 1)
                    pe.wait_ge(hb, n - 1)
                if n == 0:
                    pe.wait_ge(w_lo, 6)
                for c in range(HC):
                    o = slice(H1 * e + P * c, H1 * e + P * c + P)
                    ins = three(GU[e % 2][:, c // 2, CAP * (c % 2):CAP * (c % 2) + CAP], w1h[:, o], w1l[:, o],
                                dh[e % 2][:, :], dl[e % 2][:, :])
                ins.then_inc(up1, 1)

            def D1(m, e):
                n = E1 * m + e
                pe.wait_ge(ha, n + 1)
                pe.wait_ge(hb, n + 1)
                if n >= 2:
                    pe.wait_ge(eo_done, n - 1)
                if n == 0:
                    pe.wait_ge(in_w2, 16)
                for t in range(CAP // P):
                    for c in range(HC):
                        ins = pe.matmul(TRB[e % 2][:, P * t:P * t + P], hT[e % 2][:, c, P * t:P * t + P],
                                        w2s[:, HC * e + c, :], start=(c == 0), stop=(c == HC - 1))
                ins.then_inc(dn1, 1)

            def RG(_, b):
                st = ST_RG
                pe.wait_ge(misc_free, at["T", ST_RG, b] + 1)
                if b >= 2:
                    pe.wait_ge(rg_sig, b - 1)
                for k, o in ((0, A_OFF), (1, X_OFF)):
                    ins = three(GU[b % 2][:, k, :], pjh[:, o:o + P], pjl[:, o:o + P], xh[part[st, b]][:, :], xl[part[st, b]][:, :])
                ins.then_inc(rg_mm, 1)

            def YT(st, b):
                free_bank(("YT", ST_RG, b))
                pe.wait_ge(rg_y, b + 1)
                for j in range(TB):
                    c = S * b + P * j
                    ins = pe.transpose(MB[:, P * j:P * j + P], rr[:, c:c + P], ident)
                ins.then_inc(misc, 1)

            pe.wait_ge(in_c, 16)
            STEP = {"T": T, "R": R, "up": up, "tr": tr, "y": y, "V": V, "M": M, "P1": P1, "P2": P2, "PV": PV, "OT": OT,
                    "FT": FT, "PO": PO, "R1": R1, "C": C, "XT": XT, "U1": U1, "D1": D1, "RG": RG, "YT": YT}
            for name, st, n in plan_pe:
                if name == "R" and (st, n) == (ST_F0, 0):
                    pe.wait_ge(w_lo, 1)
                if name == "y" and (st, n) == (0, 0):
                    pe.wait_ge(in_p, 16)
                if name == "V" and n == 0:
                    pe.wait_ge(w_lo, 2)
                    pe.wait_ge(c_cast, C_CASTS)
                    pe.wait_ge(presets, PRESETS)
                if name in ("Q", "K"):
                    QK(name, st, n)
                else:
                    STEP[name](st, n)


def constants(np):
    c = np.zeros((P, C_N), np.float32)
    r = np.arange(P)
    c[:, C_ID:C_ID + P] = np.eye(P)
    c[:, C_TRI:C_TRI + P] = r[:, None] < r[None, :]
    c[:, C_MASK:C_MASK + P] = np.where(r[None, :] > r[:, None], -BIG, 0)
    for n, at in ((E0, C_ME), (G0, C_MG)):
        e = np.arange(n)
        m = np.stack([e[None, :] > e[:, None], e[None, :] < e[:, None]], 1)
        c[:, at:at + 2 * n * n] = m.reshape(1, -1)
    c[:, C_NI8:C_NI8 + E1] = E1 - np.arange(E1)
    c[:, C_E256:C_E256 + E1] = CAP * np.arange(E1)
    q = r % 32
    c[:, C_CQ] = np.where(q // 8 == 1, -1, 0)
    c[:, C_CK] = np.where(q // 8 == 2, -1, 0) + (q == 24)
    c[:, C_KB] = q == 24
    c[:, C_TOK:C_N:2] = r[:, None] + P * np.arange(NT)
    return c


def kernel(**inputs):
    import numpy as np
    import concourse.bacc as bacc
    from concourse.bass_utils import run_bass_kernel_spmd as run

    a = {k: np.asarray(v) for k, v in inputs.items()}
    Wg, Wu = (a["L0_ffn_" + k].reshape(E0 * I0, P).T for k in ("Wg", "Wu"))
    half = E0 * I0 // 2
    wup = np.concatenate([Wg[:, :half], Wu[:, :half], Wg[:, half:], Wu[:, half:],
                          a["L0_ffn_Ws_g"].T, a["L0_ffn_Ws_u"].T, a["L0_ffn_gate_w"].T], 1)
    wdn = np.concatenate([a["L0_ffn_Wd"].transpose(0, 2, 1).reshape(E0 * I0, P), a["L0_ffn_Ws_d"].T], 0)
    wdn = wdn.reshape(9, P, P).transpose(1, 0, 2)

    def heads(w):
        w = w.T.reshape(P, NH, 1, DH)
        return np.concatenate([w, w, w, np.zeros_like(w)], 2).reshape(P, NH * 32)

    proj = np.concatenate([heads(a["L0_attn_q_proj_weight"]), heads(a["L0_attn_k_proj_weight"]),
                           a["L0_attn_v_proj_weight"].T, a["L0_attn_o_proj_weight"].T,
                           a["L1_attn_Wa"].T, a["L1_attn_Wx"].T, a["L1_ffn_wg"]], 1)
    w1 = a["L1_ffn_w1"].transpose(1, 0, 2).reshape(P, E1 * H1)
    w2 = a["L1_ffn_w2"].reshape(E1 * HC, P, P).transpose(1, 0, 2)
    vecs = np.concatenate([a["L1_attn_Lam"][:, None], a["L1_attn_ba"][:, None], a["L1_attn_bx"][:, None],
                           a["L1_ffn_b1"].reshape(E1 * HC, P).T], 1)
    laid = dict(x_in=a["L0_attn_in_features"].reshape(B * S, P), wup=wup, wdn=wdn, proj=proj, w1=w1, w2=w2,
                vecs=vecs, bias0=a["L0_ffn_gate_bias"], b2=a["L1_ffn_b2"], consts=constants(np))
    nc = bacc.Bacc("TRN2", target_bir_lowering=False, num_devices=1)
    arrays, args = {}, []
    for name, v in laid.items():
        v = np.ascontiguousarray(v)
        arrays[f"in_{name}"] = v
        args.append(nc.dram_tensor(f"in_{name}", v.shape, mybir.dt.from_np(v.dtype), kind="ExternalInput").ap())
    out = nc.dram_tensor("out_x", (B * S, P), F32, kind="ExternalOutput").ap()
    build(nc, *args, out)
    r = run(nc, [arrays], core_ids=[0])
    return r.results[0]["out_x"].reshape(B, S, P)
```

```python
from contextlib import ExitStack

import concourse.bass as bass
from concourse import mybir

F32 = mybir.dt.float32
F32R = mybir.dt.float32r
BF16 = mybir.dt.bfloat16
U32 = mybir.dt.uint32
ALU = mybir.AluOpType
ACT = mybir.ActivationFunctionType
X = mybir.AxisListType.X

P = 128
B, S = 4, 512
TB = S // P
NT = B * TB
E0, I0, G0, TOPG, TOPK = 16, 64, 4, 2, 4
NH, DH = 16, 8
HG = NH // 4
E1, H1 = 8, 512
CAP = B * S // E1
HC = H1 // P
R_TOK, R_GATE, R_MEAN, R_RSTD, ROW = P, P + 1, P + 2, P + 3, P + 4
EPS = 1e-5
BIG = 1e30

C_ID, C_TRI, C_MASK, C_MG, C_NI8, C_E256, C_CQ, C_CK, C_KB, C_TOK = 0, 128, 256, 384, 416, 424, 432, 433, 434, 435
C_N = C_TOK + NT
W_UNIT = (0, 1024, 2048)
W_GATE = 2304
W_N = 2320
W_PARTS = ((2048, 2320), (0, 1024), (1024, 2048))
Q_OFF, K_OFF, V_OFF, O_OFF, A_OFF, X_OFF, G_OFF, PJ_N = 0, 512, 1024, 1152, 1280, 1408, 1536, 1544
V_LAM, V_BA, V_BX, V_B1 = 0, 1, 2, 3
ST_F0, ST_AT, ST_F1, ST_M0, ST_RG, ST_M1 = range(6)


Q_UNITS = ([(0, 0, 4, P)] + [(1, h, 2, 2 * P) for h in (0, 2)] + [(2, h, 1, 3 * P) for h in range(4)] +
           [(3, h, 1, 4 * P) for h in range(4)])
K_UNITS = ([(0, h, 1, 4 * P) for h in range(4)] + [(1, h, 1, 3 * P) for h in range(4)] +
           [(2, h, 2, 2 * P) for h in (0, 2)] + [(3, 0, 4, P)])
UN = len(K_UNITS)
K_LAST = [max(n for n, u in enumerate(K_UNITS) if u[0] == k) for k in range(TB)]


def build(nc, x_in, wup, wdn, proj, w1, w2, vecs, bias0, b2, consts, out):
    ctx = ExitStack()
    with ctx:
        def sb(name, shape, dt=F32):
            return ctx.enter_context(nc.sbuf_tensor(name, shape, dt))

        def sem(name):
            return ctx.enter_context(nc.semaphore(name))

        xs = sb("xs", [P, NT, ROW])
        xn = sb("xn", [P, NT, P])
        stats = sb("stats", [P, 2, TB, 6])
        veps = sb("veps", [P, 2, TB])
        mhalf = sb("mhalf", [P, TB])
        xh = [sb(f"xh{i}", [P, S], F32R) for i in range(3)]
        xl = [sb(f"xl{i}", [P, S], F32R) for i in range(3)]
        cst = sb("cst", [P, C_N])
        identb = sb("identb", [P, P], BF16)
        maskb = sb("maskb", [P, P], BF16)
        trib = sb("trib", [P, P], BF16)
        onesb = sb("onesb", [P, P], BF16)
        mgb = sb("mgb", [P, 32], BF16)
        arena_f = sb("arena_f", [P, 8192])
        arena_r = sb("arena_r", [P, 8192], F32R)
        stage = arena_f[:, 0:4096]
        wuh = sb("wuh", [P, W_N], F32R)
        wul = sb("wul", [P, W_N], F32R)
        wds = sb("wds", [P, 9, P])
        pjh = sb("pjh", [P, PJ_N], F32R)
        pjl = sb("pjl", [P, PJ_N], F32R)
        w1h, w1l = arena_r[:, 0:4096], arena_r[:, 4096:8192]
        w2s = arena_f[:, 4096:8192].rearrange("p (c m) -> p c m", m=P)
        vec = sb("vec", [P, V_B1 + E1 * HC])
        b0s = sb("b0s", [P, E0])
        b2s = sb("b2s", [P, E1, P])
        sp_t = sb("sp_t", [P, 8])
        sil = sb("sil", [P, 2, 512])
        act = sb("act", [P, 3, 512])
        actT = sb("actT", [P, 2, 512])
        sig = sb("sig", [P, TB * E0])
        sfc = sb("sfc", [P, TB * E0])
        msk = sb("msk", [P, TB, E0 + 8 - TOPK])
        left = sb("left", [P, TB, E0 + 8 - TOPK])
        best = sb("best", [P, TB, 8])
        gt4 = sb("gt4", [P, 6, TB * G0 * 2])
        cmpg = sb("cmpg", [P, TB, G0, 2, G0], BF16)
        rank = sb("rank", [P, TB * E0])
        tsum = sb("tsum", [P, 3, TB])
        cw = sb("cw", [P, 2, TB, E0])
        qraw = [sb(f"qraw{i}", [P, S], F32R) for i in range(2)]
        qaug = [sb(f"qaug{i}", [P, S], F32R) for i in range(2)]
        qkh = sb("qkh", [P, S], F32R)
        krow = [sb(f"krow{i}", [P, S], F32R) for i in range(2)]
        kz = [arena_r[:, 2048 * i:2048 * i + 2048].rearrange("p (h s) -> p h s", h=4) for i in range(3)]
        va = [arena_f[:, 4096 + 2048 * i:6144 + 2048 * i].rearrange("p (t h c) -> p t h c", h=NH, c=32)
              for i in range(2)]
        mpad = [sb(f"mpad{i}", [P, TB, P]) for i in range(2)]
        pt = [arena_f[:, S * i:S * i + S] for i in range(8)]
        pair = sb("pair", [P, 2048])
        ots = [pair[:, S * i:S * i + S] for i in range(2)]
        orec = sb("orec", [P, TB, 4])
        oh_, ol_ = sb("oh_", [P, S], F32R), sb("ol_", [P, S], F32R)
        otok = [pair[:, 1024 + S * i:1024 + S * i + S].rearrange("p (t h c) -> p t h c", t=TB, h=NH) for i in range(2)]

        lg, ex, wt, we = (sb(n, [P, TB, E1]) for n in ("lg", "ex", "wt", "we"))
        t4 = sb("t4", [P, 7, TB])
        ohb = sb("ohb", [P, NT, E1], BF16)
        idx_s, idx_t = sb("idx_s", [P, NT], U32), sb("idx_t", [P, NT], U32)
        xd = sb("xd", [P, NT, ROW])
        xe = [sil[:, i, 0:CAP].rearrange("p (t d) -> p t d", d=P) for i in range(2)]
        dh, dl = ([x[i][:, 0:CAP] for i in range(2)] for x in (xh, xl))
        hT = [pair[:, 1024 * i:1024 * i + 1024].rearrange("p (c t) -> p c t", c=HC) for i in range(2)]
        eos = [act[:, i, 0:CAP].rearrange("p (t d) -> p t d", d=P) for i in range(2)]
        empty = sb("empty", [P, ROW])
        rr, ii = arena_f[:, 0:2048], arena_f[:, 2048:4096]
        xf = sb("xf", [P, B * S])
        aa = xn[:, :, :].rearrange("p t d -> p (t d)")
        c8, one = sb("c8", [P, 1]), sb("one", [P, 1])

        ps = ctx.enter_context(nc.psum_tensor("ps", [P, 8, 512], F32))
        GU = [ps[:, 2 * i:2 * i + 2, :] for i in range(2)]
        TRB = [ps[:, 4 + i, :] for i in range(2)]
        YB = ps[:, 6, :]
        MB = ps[:, 7, :]
        SL = [ps[:, i, :] for i in range(6)]

        disp = [nc.dram_tensor(f"disp{m}", (E1 * CAP, ROW), F32, kind="Internal").ap() for m in range(2)]
        x_mid = nc.dram_tensor("x_mid", (B * S, P), F32, kind="Internal").ap()
        tok_out = [x_mid, out]

        ident = cst[:, C_ID:C_ID + P]

        def bank(op):
            return MB if at[op] < first_rg or op[0] == "XT" else ps[:, 7 - (at[op] - first_rg) % 4, :]


        in_c, in_x, in_w, in_p, in_v = (sem(n) for n in ("in_c", "in_x", "in_w", "in_p", "in_v"))
        in_b = sem("in_b")
        in_wup = [sem(f"in_wup{n}") for n in range(3)]
        in_w1, in_w2, in_xr = sem("in_w1"), sem("in_w2"), sem("in_xr")
        zeroed = sem("zeroed")
        c_cast = sem("c_cast")
        presets = sem("presets")
        pool_own = sem("pool_own")
        w_hi, w_lo = sem("w_hi"), sem("w_lo")
        dve = sem("dve")
        ln_stat, ln_rstd, ln_xn = sem("ln_stat"), sem("ln_rstd"), sem("ln_xn")
        xt_hi, xt_lo = sem("xt_hi"), sem("xt_lo")
        misc, misc_free = sem("misc"), sem("misc_free")
        up_done, silu_done, mul_done, cw_done = sem("up_done"), sem("silu_done"), sem("mul_done"), sem("cw_done")
        tr_done, at_done, dn_done, y_read = sem("tr_done"), sem("at_done"), sem("dn_done"), sem("y_read")
        routed, sig_done = sem("routed"), sem("sig_done")
        p1_done, p2_done, pv_done = sem("p1_done"), sem("p2_done"), sem("pv_done")
        max_done, exp_done, tri_done, pv_read = sem("max_done"), sem("exp_done"), sem("tri_done"), sem("pv_read")
        kz_in = [sem(f"kz_in{i}") for i in range(3)]
        x_att = sem("x_att")
        o_hi, o_lo = sem("o_hi"), sem("o_lo")
        lg_sub, lg_exp = sem("lg_sub"), sem("lg_exp")
        oh_done, idx_done, scat = sem("oh_done"), sem("idx_done"), sem("scat")
        in_xd = [sem(f"in_xd{e}") for e in range(E1)]
        d_hi, up1, ha, hb, dn1, eo_done = (sem(n) for n in ("d_hi", "up1", "ha", "hb", "dn1", "eo_done"))
        eo_out = [sem(f"eo_out{i}") for i in range(2)]
        gat = [sem(f"gat{b}") for b in range(B)]
        eo_idx, xe_done, kept = sem("eo_idx"), sem("xe_done"), sem("kept")
        rg_mm, rg_sig, rg_a, rg_a2, rg_sq, rg_y = (sem(n) for n in ("rg_mm", "rg_sig", "rg_a", "rg_a2", "rg_sq", "rg_y"))
        lam_abs, lam_exp, lam_done = sem("lam_abs"), sem("lam_exp"), sem("lam_done")

        NG, NU, NF = B * HG, UN * B * HG, 3 * NT
        P_LAG, V_LAG = 14, 18
        STEPS = range(NU + V_LAG)
        side = {}

        def put(key, i, *op):
            side.setdefault((key, i), []).append(op)

        def front(key, i, st, b, steps):
            for n, name in steps:
                put(key, i + n, name, st, b)

        L0_FRONT = [(1, "S"), (3, "A"), (4, "T"), (5, "R"), (7, "r0"), (8, "r1"), (9, "r2"), (9, "r3"), (10, "r4")]
        L1_FRONT = [(0, "S"), (2, "A"), (3, "T"), (4, "R1"), (5, "m1"), (6, "C"), (7, "m2"), (7, "m3")]
        front("pre", 0, ST_F0, 0, [(0, "S"), (2, "A"), (3, "T"), (5, "R"),
                                   (6, "r0"), (7, "r1"), (8, "r2"), (9, "r3"), (10, "r4")])
        for b in range(1, B):
            front("f0", 3 * TB * (b - 1), ST_F0, b, L0_FRONT)
        for i in range(-30, NU + V_LAG + 20):
            for name, every, shift, count in (("S", UN * HG, -30, B), ("A", UN * HG, -26, B), ("T", UN * HG, -23, B),
                                              ("V", UN * HG, -15, B), ("M", UN, P_LAG - 2, NG), ("Q", UN, -6, NG),
                                              ("K", UN, -8, NG), ("OT", UN, V_LAG + 12, NG),
                                              ("FT", UN * HG, V_LAG + 48, B), ("PO", UN * HG, V_LAG + 52, B)):
                n, rest = divmod(i - shift, every)
                if rest == 0 and 0 <= n < count:
                    if i < 0:
                        put("f0", NF + 2 + i // 2, name, ST_AT, n)
                    elif i < len(STEPS):
                        put("at", i, name, ST_AT, n)
                    else:
                        put("f1", (i - len(STEPS)) // 2, name, ST_AT, n)
        front("at", NU - 60, ST_F1, 0, [(3 * n, name) for n, (_, name) in enumerate(L0_FRONT)])
        for b in range(1, B):
            front("f1", 3 * TB * (b - 1), ST_F1, b, L0_FRONT)
        for b in range(B - 1):
            front("f1", 3 * TB * b + 15, ST_M0, b, [(0, "S"), (2, "A"), (3, "T"), (4, "R1"), (5, "m1"), (7, "C"),
                                                    (7, "m2"), (8, "m3")])
            for j in range(TB):
                put(*(("f1", 3 * TB * b + 23 + j) if b < B - 2 else ("m0", 1)), "D", ST_M0, TB * b + j)
        front("m0", 0, ST_M0, B - 1, L1_FRONT)
        for j in range(TB):
            put("m0", 7, "D", ST_M0, NT - TB + j)
        RG_ORDER = ("S0 S1 A0 T0 A1 S2 T1 G0 A2 S3 T2 G1 A3 T3 G2 G3 I0 I1 I2 E0 E1 E2 E3 I3 H0 H1 Y0 H2 Y1 s0 H3 "
                    "s1 Y2 a0 t0 Y3 a1 s2 t1 r0 a2 m0 c0 s3 n0 p0 t2 r1 m1 a3 c1 n1 p1 t3 r2 m2 c2 n2 p2 "
                    "r3 m3 c3 n3 p3").split()
        NAMES = {"Y": "YT", "s": "S", "a": "A", "t": "T", "r": "R1", "m": "m1", "c": "C", "n": "m2", "p": "m3"}
        for i, (name, b) in enumerate(RG_ORDER):
            put("rg", i, NAMES.get(name, name), ST_M1 if name.islower() else ST_RG, int(b))
            if name == "p":
                for t in range(TB * int(b), TB * int(b) + TB):
                    put("rg", i, "D", ST_M1, t)

        def beside(key, i):
            return side.get((key, i), ())

        KEYS = [("pre", 11), ("f0", NF + 3), ("at", len(STEPS)), ("f1", NF + 3), ("m0", 8), ("rg", len(RG_ORDER)),
                ("m1", 0)]
        nmisc, plan_pe, slots, norms = [], [], [], []

        def use(*op):
            plan_pe.append(op)
            nmisc.append(op)

        for key, count in KEYS:
            for i in range(count):
                if key == "at" and i < NU:
                    slots.append(("P1", i))
                    plan_pe.append(("P1", 0, i))
                for op in beside(key, i):
                    if op[0] == "G":
                        plan_pe.append(op)
                    if op[0] == "S":
                        norms.append(op[1:])
                    if op[0] in ("T", "R", "R1", "C", "V", "Q", "K", "M", "OT", "FT", "PO", "YT"):
                        use(*op)
                if key in ("f0", "f1"):
                    if i < NF:
                        plan_pe.append(("up", int(key[1]), i))
                    if 2 <= i < NF + 2:
                        plan_pe.append(("tr", int(key[1]), i - 2))
                    if i >= 3:
                        plan_pe.append(("y", int(key[1]), i - 3))
                if key == "at":
                    if 0 <= i - P_LAG < NU:
                        slots.append(("P2", i - P_LAG))
                        plan_pe.append(("P2", 0, i - P_LAG))
                    g, n = divmod(i - V_LAG, UN)
                    if i >= V_LAG and n in K_LAST:
                        plan_pe.append(("PV", 0, TB * g + K_LAST.index(n)))
            if key in ("m0", "m1"):
                for e in range(-1, E1 + 1):
                    if e + 1 < E1:
                        use("XT", int(key[1]), e + 1)
                    if 0 <= e < E1:
                        plan_pe.append(("U1", int(key[1]), e))
                    if e >= 1:
                        plan_pe.append(("D1", int(key[1]), e - 1))

        at = {op: i for i, op in enumerate(nmisc)}
        first_rg = at["T", ST_RG, 0]
        ln = {op: i for i, op in enumerate(norms)}
        part = {op: 2 if op[0] == ST_M0 else op[1] % 2 for op in norms}

        C_CASTS = 4 + 3
        PRESETS = 1 + 1 + 2 + 2 + 1

        hi_at = {op: i for i, op in enumerate(op for op in nmisc if op[0] in "TQK")}
        block = ctx.enter_context(nc.Block())

        def tile(st, b, j):
            return xn[:, TB * b + j, :]

        def sum_unit(j):
            return TB * (j // UN) + K_UNITS[j % UN][0]

        def router_tiles(st, b):
            return slice(TB * b, TB * b + TB)

        def router_step(st, b):
            return b if st == ST_M0 else B + b

        @block.sync
        def _(sp):
            xv = x_in.rearrange("(t p) d -> p t d", p=P)
            sp.dma_start(xs[:, 0:TB, 0:P], xv[:, 0:TB, :]).then_inc(in_x, 16)
            sp.dma_start(cst[:, :], consts).then_inc(in_c, 16)
            sp.dma_start(b0s[:, :], bias0.partition_broadcast(P)).then_inc(in_b, 16)
            for n, (first, end) in enumerate(W_PARTS):
                sp.dma_start(stage[:, first:end], wup[:, first:end]).then_inc(in_wup[n], 16)
            sp.dma_start(vec[:, :], vecs).then_inc(in_v, 16)
            sp.dma_start(wds[:, :, :], wdn).then_inc(in_p, 16)
            sp.dma_start(xs[:, TB:NT, 0:P], xv[:, TB:NT, :]).then_inc(in_xr, 16)
            sp.dma_start(b2s[:, :, :], b2.partition_broadcast(P)).then_inc(in_v, 16)
            sp.wait_ge(presets, PRESETS)
            for m in range(2):
                sp.dma_start(disp[m].rearrange("(t p) d -> p t d", p=P),
                             empty[:, :].unsqueeze(1).broadcast_to([P, NT, ROW])).then_inc(zeroed, 16)
            sp.wait_ge(w_lo, 3)
            sp.dma_start(stage[:, 0:PJ_N], proj).then_inc(in_w, 16)

            def key_rows(g):
                sp.wait_ge(misc_free, at["K", ST_AT, g] + 1)
                if g >= 3:
                    sp.wait_ge(p2_done, UN * (g - 2))
                for h in range(4):
                    r = slice(32 * h, 32 * h + 32)
                    sp.dma_start(kz[g % 3][r, h, :].bitcast(F32), krow[g % 2][r, :].bitcast(F32)).then_inc(kz_in[g % 3], 16)

            for g in range(NG):
                key_rows(g)
            sp.wait_ge(pv_done, TB * NG)
            sp.dma_start(stage, w1).then_inc(in_w1, 16)
            sp.dma_start(w2s, w2).then_inc(in_w2, 16)

            def by_token(dram, b):
                return dram[S * b:S * b + S, :].rearrange("(t p) d -> p t d", p=P)

            for m in range(2):
                for b in range(B):
                    if m == 0:
                        sp.wait_ge(y_read, NT + TB * (b + 1))
                    else:
                        sp.wait_ge(misc_free, at["YT", ST_RG, b] + 1)
                    sp.dma_start(by_token(tok_out[m], b), xs[:, TB * b:TB * b + TB, 0:P]).then_inc(kept, 16)
                for e in range(E1):
                    sp.wait_ge(scat, 16 * NT * (m + 1))
                    n = CAP // P
                    sp.dma_start(xd[:, n * e:n * e + n, :],
                                 disp[m][CAP * e:CAP * e + CAP, :].rearrange("(t p) d -> p t d", p=P)).then_inc(in_xd[e], 16)
                for i in range(2):
                    sp.wait_ge(eo_out[i], 16 * NT // 2 * (m + 1))
                if m == 0:
                    for b in range(B):
                        sp.dma_start(xs[:, TB * b:TB * b + TB, 0:P], by_token(x_mid, b)).then_inc(gat[b], 16)
            sp.wait_ge(kept, 16 * 2 * B)

        @block.gpsimd
        def _(pool):
            pool.memset(mhalf[:, :], -0.5).then_inc(pool_own, 1)
            pool.memset(empty[:, :], 0.0).then_inc(pool_own, 1)
            pool.wait_ge(pool_own, 2)
            pool.memset(empty[:, R_TOK:R_TOK + 1], 2.0 * E1 * CAP).then_inc(presets, 1)

            def power(st, b):
                L = ln[st, b]
                pool.wait_ge(ln_stat, L + 1)
                pool.tensor_tensor(xs[:, TB * b:TB * b + TB, R_RSTD], veps[:, L % 2, :], mhalf[:, :],
                                   ALU.pow).then_inc(ln_rstd, 1)

            def square(b):
                sl = slice(S * b, S * b + S)
                pool.wait_ge(rg_a, b + 1)
                pool.tensor_tensor(rr[:, sl], aa[:, sl], aa[:, sl], ALU.mult).then_inc(rg_a2, 1)

            def weigh(s, i):
                t, k = divmod(i, 3)
                if k == 2:
                    return
                n = NF * s + i
                pool.wait_ge(mul_done, n + 1)
                pool.wait_ge(routed, B * s + t // TB + 1)
                a = act[:, n % 3, :].rearrange("p (e i) -> p e i", i=I0)
                c = cw[:, (t // TB) % 2, t % TB, 8 * k:8 * k + 8].unsqueeze(2).broadcast_to([P, 8, I0])
                pool.tensor_tensor(a, a, c, ALU.mult).then_inc(cw_done, 1)

            def diagonal(j):
                _, _, nh, w = K_UNITS[j % UN]
                pool.wait_ge(exp_done, j + 1)
                d = pt[j % 8][:, 0:nh * w].rearrange("p (h q) -> p h q", h=nh)[:, :, 0:P]
                pool.affine_select(out=d, in_=d, compare_op=ALU.is_ge, fill=0.0, base=0,
                                   pattern=[[0, nh], [1, P]], channel_multiplier=-1).then_inc(tri_done, 1)

            def dispatch(st, t):
                m = 0 if st == ST_M0 else 1
                pool.wait_ge(idx_done, router_step(st, t // TB) + 1)
                if m == 0 and t == 0:
                    pool.wait_ge(zeroed, 32)
                pool.indirect_dma_start(
                    out=disp[m], out_offset=bass.IndirectOffsetOnAxis(ap=idx_s[:, t:t + 1], axis=0),
                    in_=xs[:, t, :], in_offset=None,
                    bounds_check=E1 * CAP - 1, oob_is_err=False).then_inc(scat, 16)

            def collect(m):
                pool.wait_ge(kept, 16 * B * (m + 1))
                for e in range(E1):
                    pool.wait_ge(eo_done, E1 * m + e + 1)
                    pool.wait_ge(eo_idx, E1 * m + e + 1)
                    for t in range(CAP // P):
                        n = CAP // P * e + t
                        pool.indirect_dma_start(
                            out=tok_out[m], out_offset=bass.IndirectOffsetOnAxis(ap=idx_t[:, n:n + 1], axis=0),
                            in_=eos[e % 2][:, t, :], in_offset=None,
                            bounds_check=B * S - 1, oob_is_err=False).then_inc(eo_out[e % 2], 16)

            def besides(key, i):
                for name, st, b in beside(key, i):
                    if name == "S":
                        power(st, b)
                    if name == "D":
                        dispatch(st, b)
                    if name == "E":
                        square(b)

            for key, count in KEYS:
                for i in range(count):
                    besides(key, i)
                    if key in ("f0", "f1") and i < NF:
                        weigh(int(key[1]), i)
                    if key == "at" and 0 <= i - P_LAG < NU:
                        diagonal(i - P_LAG)
                if key == "pre":
                    pool.memset(arena_r[:, 0:6144].bitcast(F32), 0.0).then_inc(presets, 1)
                    pool.memset(arena_f[:, 4096:8192], 0.0).then_inc(pool_own, 1)
                    for i in range(2):
                        pool.memset(mpad[i][:, :, :], 0.0).then_inc(presets, 1)
                    pool.wait_ge(pool_own, 3)
                    for i in range(2):
                        pool.memset(va[i][:, :, :, DH], 1.0).then_inc(presets, 1)
                    pool.memset(onesb[:, :], 1.0).then_inc(presets, 1)
                if key in ("m0", "m1"):
                    collect(int(key[1]))

        @block.scalar
        def _(sc):
            def split_hi(dst, src, wait, value):
                sc.wait_ge(wait, value)
                sc.copy(dst, src).then_inc(w_hi, 1)

            sc.wait_ge(in_c, 16)
            for d, c in ((identb, C_ID), (maskb, C_MASK), (trib, C_TRI)):
                sc.copy(d[:, :], cst[:, c:c + P]).then_inc(c_cast, 1)
            sc.copy(mgb[:, :], cst[:, C_MG:C_MG + 32]).then_inc(c_cast, 1)
            for n, (first, end) in enumerate(W_PARTS[:2]):
                split_hi(wuh[:, first:end], stage[:, first:end], in_wup[n], 16)

            def hi(st, b):
                L = ln[st, b]
                sc.wait_ge(misc, at["T", st, b] + 1)
                rows_t = bank(("T", st, b))
                ins = sc.copy(xh[part[st, b]][:, :], rows_t)
                if st == ST_RG:
                    ins = sc.copy(xf[:, S * b:S * b + S], rows_t)
                ins.then_inc(xt_hi, 1)

            def scores(st, b):
                s = 0 if st == ST_F0 else 1
                sc.wait_ge(misc, at["R", st, b] + 1)
                if b or s:
                    sc.wait_ge(routed, B * s + b)
                sc.activation(sig[:, :], MB[:, 0:TB * E0], ACT.Sigmoid).then_inc(misc_free, 1)

            def silu(s, i):
                n = 3 * NT * s + i
                w = 512 if i % 3 < 2 else P
                sc.wait_ge(up_done, n + 1)
                if n >= 2:
                    sc.wait_ge(mul_done, n - 1)
                sc.activation(sil[:, n % 2, 0:w], GU[n % 2][:, 0, 0:w], ACT.Silu).then_inc(silu_done, 1)

            def evac(s, i):
                n = 3 * NT * s + i
                w = 512 if i % 3 < 2 else P
                sc.wait_ge(tr_done, n + 1)
                if n >= 2:
                    sc.wait_ge(dn_done, n - 1)
                sc.copy(actT[:, n % 2, 0:w], TRB[n % 2][:, 0:w]).then_inc(at_done, 1)

            def exp_unit(j):
                _, _, nh, w = K_UNITS[j % UN]
                k = slots.index(("P2", j))
                src = SL[k % 6].rearrange("p (h q) -> p h q", h=nh)[:, :, 0:w]
                sc.wait_ge(p2_done, j + 1)
                if j >= 8:
                    sc.wait_ge(pv_done, sum_unit(j - 8) + 1)
                sc.activation(pt[j % 8][:, 0:nh * w].rearrange("p (h q) -> p h q", h=nh), src, ACT.Exp,
                              scale=DH ** -0.5).then_inc(exp_done, 1)

            def besides(key, i):
                for name, st, n in beside(key, i):
                    op = (name, st, n)
                    if name == "T":
                        hi(st, n)
                    if name == "R":
                        scores(st, n)
                    if name == "V":
                        sc.wait_ge(misc, at[op] + 1)
                        if n == 0:
                            sc.wait_ge(presets, PRESETS)
                        if n >= 2:
                            sc.wait_ge(pv_done, TB * HG * (n - 1))
                        sc.copy(va[n % 2][:, :, :, 0:DH],
                                MB.rearrange("p (t h c) -> p t h c", h=NH, c=DH)).then_inc(misc_free, 1)
                    if name == "Q":
                        sc.wait_ge(misc, at[op] + 1)
                        sc.copy(qkh[:, :], MB).then_inc(xt_hi, 1)
                    if name == "K":
                        sc.wait_ge(misc, at[op] + 1)
                        sc.activation(qkh[:, :], MB, ACT.Identity, bias=cst[:, C_KB:C_KB + 1]).then_inc(xt_hi, 1)
                    if name == "FT":
                        sc.wait_ge(misc, at[op] + 1)
                        sc.copy(oh_[:, :], MB).then_inc(o_hi, 1)
                    if name == "m1":
                        bl = router_tiles(st, n)
                        w = bl.stop - bl.start
                        sc.wait_ge(lg_sub, router_step(st, n) + 1)
                        sc.activation(ex[:, 0:w, :], lg[:, 0:w, :], ACT.Exp).then_inc(lg_exp, 1)
                    if name == "G":
                        sc.wait_ge(rg_mm, n + 1)
                        for k, dst in ((0, rr), (1, ii)):
                            ins = sc.activation(dst[:, S * n:S * n + S], GU[n % 2][:, k, :], ACT.Sigmoid,
                                                bias=vec[:, V_BA + k:V_BA + k + 1])
                        ins.then_inc(rg_sig, 1)
                    if name == "E":
                        sl = slice(S * n, S * n + S)
                        if n == 0:
                            sc.wait_ge(lam_done, 1)
                            sc.wait_ge(rg_sig, B)
                            sc.wait_ge(misc, at["T", ST_RG, B - 1] + 1)
                        sc.activation(aa[:, sl], rr[:, sl], ACT.Exp, scale=c8[:, 0:1]).then_inc(rg_a, 1)
                    if name == "H":
                        sl = slice(S * n, S * n + S)
                        sc.wait_ge(rg_a2, n + 1)
                        sc.activation(rr[:, sl], rr[:, sl], ACT.Sqrt, bias=one[:, 0:1], scale=-1.0).then_inc(rg_sq, 1)

            def sums(g):
                sc.wait_ge(pv_done, TB * g + TB)
                if g >= 2:
                    sc.wait_ge(misc, at["OT", ST_AT, g - 2] + 1)
                sc.copy(ots[g % 2], YB).then_inc(pv_read, 1)

            def moe(m):
                def relu(e):
                    n = E1 * m + e
                    sc.wait_ge(up1, n + 1)
                    if n >= 2:
                        sc.wait_ge(dn1, n - 1)
                    for c in range(2):
                        ins = sc.activation(hT[e % 2][:, c, :], GU[e % 2][:, 0, CAP * c:CAP * c + CAP], ACT.Relu,
                                            bias=vec[:, V_B1 + HC * e + c:V_B1 + HC * e + c + 1])
                    ins.then_inc(ha, 1)

                for e in range(-1, E1):
                    if e + 1 < E1:
                        sc.wait_ge(misc, at["XT", m, e + 1] + 1)
                        sc.copy(dh[(e + 1) % 2][:, :], MB[:, 0:CAP]).then_inc(d_hi, 1)
                    if e >= 0:
                        relu(e)

            for key, count in KEYS:
                for i in range(count):
                    besides(key, i)
                    if key == "pre" and i == 4:
                        first, end = W_PARTS[2]
                        split_hi(wuh[:, first:end], stage[:, first:end], in_wup[2], 16)
                    if key == "at" and i == 8:
                        sc.wait_ge(lam_abs, 1)
                        sc.activation(sp_t[:, 2:3], sp_t[:, 1:2], ACT.Exp, scale=-1.0).then_inc(lam_exp, 1)
                    if key == "f0" and i == 9:
                        split_hi(pjh[:, :], stage[:, 0:PJ_N], in_w, 16)
                    if key == "f1" and i in (20, 23, 26, 29):
                        c = slice(1024 * (i // 3 - 6), 1024 * (i // 3 - 5))
                        split_hi(w1h[:, c], stage[:, c], in_w1, 16)
                    if key in ("f0", "f1"):
                        if i < NF:
                            silu(int(key[1]), i)
                        if 2 <= i < NF + 2:
                            evac(int(key[1]), i - 2)
                    if key == "at":
                        if 0 <= i - P_LAG < NU:
                            exp_unit(i - P_LAG)
                        if i >= V_LAG and (i - V_LAG) % UN == UN - 1:
                            sums((i - V_LAG) // UN)
                if key in ("m0", "m1"):
                    moe(int(key[1]))

        @block.vector
        def _(v):
            steps = [0]

            def did(ins):
                steps[0] += 1
                ins.then_inc(dve, 1)

            def settle():
                v.wait_ge(dve, steps[0])

            def link(ins):
                did(ins)
                settle()

            v.memset(one[:, :], 1.0).then_inc(c_cast, 1)
            v.memset(msk[:, :, E0:], 2.0 * BIG).then_inc(c_cast, 1)
            v.wait_ge(in_c, 16)
            v.tensor_copy(xs[:, :, R_TOK], cst[:, C_TOK:C_TOK + NT]).then_inc(c_cast, 1)

            def split_lo(dst, src, high, count):
                v.wait_ge(w_hi, count)
                v.tensor_tensor(dst, src, high.bitcast(F32), ALU.subtract).then_inc(w_lo, 1)

            def norm_stats(st, b):
                L = ln[st, b]
                for j in range(TB):
                    did(v.bn_stats(stats[:, L % 2, j, :], xs[:, TB * b + j, 0:P]))
                settle()
                for j in range(TB):
                    did(v.bn_aggr(xs[:, TB * b + j, R_MEAN:ROW], stats[:, L % 2, j, :]))
                settle()
                if L >= 2:
                    v.wait_ge(ln_rstd, L - 1)
                v.tensor_scalar(veps[:, L % 2, :], xs[:, TB * b:TB * b + TB, R_RSTD], EPS, None,
                                ALU.add).then_inc(ln_stat, 1)

            def norm_apply(st, b):
                v.wait_ge(ln_rstd, ln[st, b] + 1)
                for j in range(TB):
                    x = xs[:, TB * b + j, :]
                    ins = v.tensor_scalar(tile(st, b, j), x[:, 0:P], x[:, R_MEAN:R_RSTD],
                                          x[:, R_RSTD:ROW], ALU.subtract, ALU.mult)
                ins.then_inc(ln_xn, 1)

            def half_in(st, b):
                L = ln[st, b]
                v.wait_ge(ln_xn, L + 1)
                sl = slice(TB * b, TB * b + TB)
                did(v.scalar_tensor_tensor(xs[:, sl, 0:P], xn[:, sl, :], 0.5, xs[:, sl, 0:P], ALU.mult, ALU.add))

            def lo(st, b):
                L = ln[st, b]
                v.wait_ge(xt_hi, hi_at["T", st, b] + 1)
                v.tensor_tensor(xl[part[st, b]][:, :], bank(("T", st, b)), xh[part[st, b]][:, :].bitcast(F32),
                                ALU.subtract).then_inc(misc_free, 1)

            def compare(cmp, vals, n, groups):
                other = vals.unsqueeze(2).broadcast_to([P, groups, n, n])
                own = vals.unsqueeze(3).broadcast_to([P, groups, n, n])
                did(v.tensor_tensor(cmp[:, :, :, 0, :], other, own, ALU.is_gt))
                did(v.tensor_tensor(cmp[:, :, :, 1, :], other, own, ALU.is_ge))

            def tally(cmp, n, mask, dst, groups):
                flat = cmp.rearrange("p t e a f -> p t (e a f)")
                link(v.tensor_tensor(flat, flat, mask.unsqueeze(1).broadcast_to([P, groups, 2 * n * n]), ALU.mult))
                did(v.tensor_reduce(dst, cmp.rearrange("p t e a f -> p (t e) (a f)"), X, ALU.add))

            def rank_of(cmp, vals, n, mask, dst, groups):
                compare(cmp, vals, n, groups)
                settle()
                tally(cmp, n, mask, dst, groups)
                settle()

            NE, ng = TB * E0, TB * G0
            sf = sfc[:, :]
            q = sf.rearrange("p (g c) -> p g c", c=4)
            mx, mn = gt4[:, 0, :].rearrange("p (g c) -> p g c", c=2), gt4[:, 1, :].rearrange("p (g c) -> p g c", c=2)
            t1, t2, t3, gs, grk, gmk = (gt4[:, 2 + n // 2, (n % 2) * ng:(n % 2) * ng + ng] for n in range(6))
            r3 = rank[:, :].rearrange("p (t e) -> p t e", e=E0)

            def group_scores(st, b):
                v.wait_ge(misc_free, at["R", st, b] + 1)
                link(v.tensor_tensor(sf.rearrange("p (t e) -> p t e", e=E0), sig[:, :].rearrange("p (t e) -> p t e", e=E0),
                                     b0s[:, :].unsqueeze(1).broadcast_to([P, TB, E0]), ALU.add))
                did(v.tensor_tensor(mx, q[:, :, 0:2], q[:, :, 2:4], ALU.max))
                link(v.tensor_tensor(mn, q[:, :, 0:2], q[:, :, 2:4], ALU.min))
                did(v.tensor_tensor(t1, mx[:, :, 0], mx[:, :, 1], ALU.max))
                did(v.tensor_tensor(t2, mx[:, :, 0], mx[:, :, 1], ALU.min))
                link(v.tensor_tensor(t3, mn[:, :, 0], mn[:, :, 1], ALU.max))
                link(v.tensor_tensor(t2, t2, t3, ALU.max))
                did(v.tensor_tensor(gs, t1, t2, ALU.add))

            def group_mask():
                settle()
                rank_of(cmpg, gs.rearrange("p (t g) -> p t g", g=G0), G0, mgb[:, :], grk, TB)
                link(v.tensor_scalar(gmk, grk, float(TOPG), None, ALU.is_lt))
                did(v.tensor_scalar(t1, gmk, -1.0, BIG, ALU.add, ALU.mult))
                ms = msk[:, :, 0:E0].rearrange("p t (g c) -> p t g c", c=4)

                def by_group(x):
                    return x.rearrange("p (t g) -> p t g", g=G0).unsqueeze(3).broadcast_to([P, TB, G0, 4])

                link(v.tensor_tensor(ms, sf.rearrange("p (t g c) -> p t g c", g=G0, c=4), by_group(gmk), ALU.mult))
                did(v.tensor_tensor(ms, ms, by_group(t1), ALU.add))

            def weights(st, b):
                nb = (0 if st == ST_F0 else B) + b
                settle()
                link(v.scalar_tensor_tensor(r3, left[:, :, 0:E0], -2.0 * BIG, sig[:, :].rearrange("p (t e) -> p t e", e=E0),
                                            ALU.is_equal, ALU.mult))
                link(v.tensor_reduce(tsum[:, 0, :], r3, X, ALU.add))
                link(v.tensor_scalar(tsum[:, 1, :], tsum[:, 0, :], 1e-20, None, ALU.add))
                link(v.reciprocal(tsum[:, 2, :], tsum[:, 1, :]))
                if nb >= 2:
                    v.wait_ge(cw_done, 2 * TB * (nb - 1))
                v.scalar_tensor_tensor(cw[:, b % 2, :, :], r3, 2.5, tsum[:, 2, :].unsqueeze(2).broadcast_to([P, TB, E0]),
                                       ALU.mult, ALU.mult).then_inc(routed, 1)

            def mul(s, i):
                n = 3 * NT * s + i
                w = 512 if i % 3 < 2 else P
                v.wait_ge(silu_done, n + 1)
                if n >= 3:
                    v.wait_ge(tr_done, n - 2)
                v.tensor_tensor(act[:, n % 3, 0:w], sil[:, n % 2, 0:w], GU[n % 2][:, 1, 0:w], ALU.mult).then_inc(mul_done, 1)

            def add_y(s, t):
                v.wait_ge(dn_done, 3 * NT * s + 3 * t + 3)
                v.scalar_tensor_tensor(xs[:, t, 0:P], YB[:, 0:P], 0.5, xs[:, t, 0:P], ALU.mult, ALU.add).then_inc(y_read, 1)

            def max_unit(i):
                g, n = divmod(i, UN)
                q, h0, nh, w = Q_UNITS[n]
                src = SL[slots.index(("P1", i)) % 6].rearrange("p (h k) -> p h k", h=nh)[:, :, 0:w]
                v.wait_ge(p1_done, i + 1)
                if n == 0 and g >= 2:
                    v.wait_ge(misc, at["M", ST_AT, g - 2] + 1)
                dst = mpad[g % 2][:, q, :].rearrange("p (h c) -> p h c", h=4)[:, h0:h0 + nh, 24]
                v.tensor_reduce(dst, src, X, ALU.max, negate=True).then_inc(max_done, 1)

            def rows(name, g, dst, column):
                v.wait_ge(xt_hi, hi_at[name, ST_AT, g] + 1)
                v.scalar_tensor_tensor(dst, qkh[:, :].bitcast(F32), cst[:, column:column + 1], MB,
                                       ALU.mult, ALU.add).then_inc(misc_free, 1)

            def besides(key, i):
                for name, st, n in beside(key, i):
                    op = (name, st, n)
                    if name == "S":
                        if st == ST_F0 and n == 1:
                            v.wait_ge(in_xr, 16)
                        settle_xs(st, n)
                        norm_stats(st, n)
                    if name == "A":
                        norm_apply(st, n)
                    if name == "T":
                        lo(st, n)
                        if st in (ST_F0, ST_F1) and (st, n) != (ST_F0, 0):
                            half_in(st, n)
                    if name == "r0":
                        group_scores(st, n)
                    if name == "r1":
                        group_mask()
                    if name == "r2":
                        settle()
                        for t in range(TB):
                            did(v.max(best[:, t, :], msk[:, t, :]))
                    if name == "r3":
                        settle()
                        for t in range(TB):
                            did(v.match_replace(left[:, t, :], best[:, t, :], msk[:, t, :], -2.0 * BIG))
                    if name == "r4":
                        weights(st, n)
                    if name == "m1":
                        first_choice(st, n)
                    if name == "m2":
                        gates(st, n)
                    if name == "m3":
                        positions(st, n)
                    if name == "M":
                        v.wait_ge(misc, at[op] + 1)
                        if n >= 2:
                            v.wait_ge(p2_done, UN * (n - 1))
                        v.tensor_tensor(qaug[n % 2][:, :], qraw[n % 2][:, :].bitcast(F32), MB,
                                        ALU.add).then_inc(misc_free, 1)
                    if name == "Q":
                        if n >= 2:
                            v.wait_ge(p1_done, UN * (n - 1))
                        rows("Q", n, qraw[n % 2][:, :], C_CQ)
                    if name == "K":
                        if n >= 2:
                            v.wait_ge(kz_in[(n - 2) % 3], 64 * ((n - 2) // 3 + 1))
                        rows("K", n, krow[n % 2][:, :], C_CK)
                    if name == "OT":
                        v.wait_ge(misc, at[op] + 1)
                        if n % HG == 0 and n >= 2 * HG:
                            v.wait_ge(misc, at["FT", ST_AT, n // HG - 2] + 1)
                        o = MB.rearrange("p (t h c) -> p t h c", t=TB, c=32)
                        link(v.reciprocal(orec[:, :, :], o[:, :, :, DH]))
                        hg = n % HG
                        v.tensor_tensor(otok[(n // HG) % 2][:, :, 4 * hg:4 * hg + 4, :], o[:, :, :, 0:DH],
                                        orec[:, :, :].unsqueeze(3).broadcast_to([P, TB, 4, DH]),
                                        ALU.mult).then_inc(misc_free, 1)
                    if name == "FT":
                        v.wait_ge(o_hi, n + 1)
                        v.tensor_tensor(ol_[:, :], MB, oh_[:, :].bitcast(F32), ALU.subtract).then_inc(misc_free, 1)
                    if name in ("PO", "YT"):
                        v.wait_ge(misc, at[op] + 1)
                        sl = slice(TB * n, TB * n + TB)
                        v.tensor_tensor(xs[:, sl, 0:P], xs[:, sl, 0:P], bank(op).rearrange("p (t d) -> p t d", d=P),
                                        ALU.add).then_inc(misc_free, 1)
                    if name == "I":
                        sl = slice(S * n, S * n + S)
                        v.wait_ge(rg_sig, n + 1)
                        did(v.tensor_tensor(ii[:, sl], ii[:, sl], xf[:, sl], ALU.mult))
                    if name == "H":
                        sl = slice(S * n, S * n + S)
                        if n == 0:
                            settle()
                        v.wait_ge(rg_sq, n + 1)
                        link(v.tensor_tensor(ii[:, sl], ii[:, sl], rr[:, sl], ALU.mult))
                        v.tensor_tensor_scan(rr[:, sl], aa[:, sl], ii[:, sl], 0.0, ALU.mult, ALU.add).then_inc(rg_y, 1)

            def settle_xs(st, b):
                if st == ST_AT:
                    v.wait_ge(y_read, TB * (b + 1))
                if st == ST_F1:
                    v.wait_ge(misc_free, at["PO", ST_AT, b] + 1)
                if st == ST_M0:
                    v.wait_ge(y_read, NT + TB * (b + 1))
                if st == ST_RG:
                    v.wait_ge(gat[b], 16)
                if st == ST_M1:
                    v.wait_ge(misc_free, at["YT", ST_RG, b] + 1)

            t_mx, t_sm, t_wm, t_pos, t_base, t_slot, t_off = (t4[:, n, :] for n in range(7))

            def router(st, b):
                bl = router_tiles(st, b)
                w = bl.stop - bl.start
                return bl, w, [P, w, E1], lambda x: x[:, 0:w].unsqueeze(2).broadcast_to([P, w, E1])

            def first_choice(st, b):
                bl, w, wide, each = router(st, b)
                logits = bank(("R1", st, b))[:, 0:w * E1].rearrange("p (t e) -> p t e", e=E1)
                v.wait_ge(misc, at["R1", st, b] + 1)
                link(v.tensor_reduce(t_mx[:, 0:w], logits, X, ALU.max))
                v.tensor_tensor(lg[:, 0:w, :], logits, each(t_mx), ALU.subtract).then_inc(lg_sub, 1)
                v.wait_ge(lg_sub, router_step(st, b) + 1)
                v.engine_nop().then_inc(misc_free, 1)
                ni = cst[:, C_NI8:C_NI8 + E1].unsqueeze(1).broadcast_to(wide)
                link(v.scalar_tensor_tensor(wt[:, 0:w, :], lg[:, 0:w, :], 0.0, ni, ALU.is_ge, ALU.mult))
                link(v.tensor_reduce(t_wm[:, 0:w], wt[:, 0:w, :], X, ALU.max))
                v.tensor_tensor(ohb[:, bl, :], wt[:, 0:w, :], each(t_wm), ALU.is_equal).then_inc(oh_done, 1)
                v.wait_ge(oh_done, router_step(st, b) + 1)
                e256 = cst[:, C_E256:C_E256 + E1].unsqueeze(1).broadcast_to(wide)
                link(v.tensor_tensor(we[:, 0:w, :], ohb[:, bl, :], e256, ALU.mult))
                did(v.tensor_reduce(t_base[:, 0:w], we[:, 0:w, :], X, ALU.add))

            def gates(st, b):
                bl, w, wide, each = router(st, b)
                v.wait_ge(lg_exp, router_step(st, b) + 1)
                link(v.tensor_reduce(t_sm[:, 0:w], ex[:, 0:w, :], X, ALU.add))
                link(v.reciprocal(t_sm[:, 0:w], t_sm[:, 0:w]))
                did(v.tensor_scalar(xs[:, bl, R_GATE], t_sm[:, 0:w], 0.5, None, ALU.mult))

            def positions(st, b):
                bl, w, wide, each = router(st, b)
                v.wait_ge(misc, at["C", st, b] + 1)
                before = bank(("C", st, b))[:, 0:w * E1].rearrange("p (t e) -> p t e", e=E1)
                link(v.tensor_tensor(wt[:, 0:w, :], before, ohb[:, bl, :], ALU.mult))
                v.engine_nop().then_inc(misc_free, 1)
                link(v.tensor_reduce(t_pos[:, 0:w], wt[:, 0:w, :], X, ALU.add))
                did(v.tensor_tensor(t_slot[:, 0:w], t_pos[:, 0:w], t_base[:, 0:w], ALU.add))
                link(v.tensor_scalar(t_off[:, 0:w], t_pos[:, 0:w], float(CAP), 2.0 * E1 * CAP, ALU.is_ge, ALU.mult))
                v.tensor_tensor(idx_s[:, bl], t_off[:, 0:w], t_slot[:, 0:w], ALU.add).then_inc(idx_done, 1)

            def moe(m):
                def relu(e):
                    n = E1 * m + e
                    v.wait_ge(up1, n + 1)
                    if n >= 2:
                        v.wait_ge(dn1, n - 1)
                    for c in range(2, HC):
                        ins = v.tensor_scalar(hT[e % 2][:, c, :], GU[e % 2][:, 1, CAP * (c - 2):CAP * (c - 1)],
                                              vec[:, V_B1 + HC * e + c:V_B1 + HC * e + c + 1], 0.0, ALU.add, ALU.max)
                    ins.then_inc(hb, 1)

                def result(e):
                    n = E1 * m + e
                    v.wait_ge(dn1, n + 1)
                    if n >= 2:
                        v.wait_ge(eo_out[e % 2], 32 * (n // 2))
                    for t in range(CAP // P):
                        x = xd[:, CAP // P * e + t, :]
                        ins = v.scalar_tensor_tensor(eos[e % 2][:, t, :], TRB[e % 2][:, P * t:P * t + P],
                                                     x[:, R_GATE:R_MEAN], x[:, 0:P], ALU.mult, ALU.add)
                    ins.then_inc(eo_done, 1)

                def rows_in(e):
                    n = slice(CAP // P * e, CAP // P * (e + 1))
                    v.wait_ge(in_xd[e], 16 * (m + 1))
                    if E1 * m + e >= 2:
                        v.wait_ge(misc, at["XT", m - (e < 2), (e - 2) % E1] + 1)
                    for t in range(CAP // P):
                        x = xd[:, CAP // P * e + t, :]
                        ins = v.tensor_scalar(xe[e % 2][:, t, :], x[:, 0:P], x[:, R_MEAN:R_RSTD], x[:, R_RSTD:ROW],
                                              ALU.subtract, ALU.mult)
                    ins.then_inc(xe_done, 1)
                    v.tensor_copy(idx_t[:, n], xd[:, n, R_TOK]).then_inc(eo_idx, 1)
                    for t in range(CAP // P):
                        x = xd[:, CAP // P * e + t, :]
                        did(v.scalar_tensor_tensor(x[:, 0:P], b2s[:, e, :], x[:, R_GATE:R_MEAN], x[:, 0:P],
                                                   ALU.mult, ALU.add))

                rows_in(0)
                for e in range(-1, E1 + 2):
                    if e + 1 < E1:
                        v.wait_ge(d_hi, E1 * m + e + 2)
                        v.tensor_tensor(dl[(e + 1) % 2][:, :], MB[:, 0:CAP], dh[(e + 1) % 2][:, :].bitcast(F32),
                                        ALU.subtract).then_inc(misc_free, 1)
                    if e + 2 < E1:
                        rows_in(e + 2)
                    if e >= 2:
                        settle()
                        result(e - 2)
                    if 0 <= e < E1:
                        relu(e)

            neg, mag, u, r, z, z2, a, q8 = (sp_t[:, n:n + 1] for n in range(8))
            lam = vec[:, V_LAM:V_LAM + 1]

            def magnitude():
                v.wait_ge(in_v, 32)
                link(v.tensor_scalar(neg, lam, -1.0, None, ALU.mult))
                v.tensor_tensor(mag, lam, neg, ALU.max).then_inc(lam_abs, 1)

            def softplus():
                v.wait_ge(lam_exp, 1)
                link(v.tensor_scalar(r, u, 2.0, None, ALU.add))
                link(v.reciprocal(r, r))
                link(v.tensor_tensor(z, u, r, ALU.mult))
                link(v.tensor_tensor(z2, z, z, ALU.mult))
                link(v.tensor_scalar(a, z2, 1.0 / 17, 1.0 / 15, ALU.mult, ALU.add))
                for k in (13, 11, 9, 7, 5, 3, 1):
                    link(v.tensor_scalar(a, a, z2, 1.0 / k, ALU.mult, ALU.add))
                link(v.tensor_tensor(a, a, z, ALU.mult))
                link(v.tensor_scalar(q8, neg, 0.0, None, ALU.max))
                link(v.scalar_tensor_tensor(q8, a, 2.0, q8, ALU.mult, ALU.add))
                v.tensor_scalar(c8[:, :], q8, -8.0, None, ALU.mult).then_inc(lam_done, 1)

            v.wait_ge(in_x, 16)
            besides("pre", 0)
            besides("pre", 2)
            for n, (first, end) in enumerate(W_PARTS):
                split_lo(wul[:, first:end], stage[:, first:end], wuh[:, first:end], n + 1)
                if n == 0:
                    besides("pre", 3)
            v.wait_ge(c_cast, C_CASTS)
            v.wait_ge(in_b, 16)
            for i in range(4, 11):
                if i >= 9:
                    mul(0, i - 9)
                besides("pre", i)
            for key, count in KEYS[1:]:
                for i in range(count):
                    if key == "at" and i < NU:
                        max_unit(i)
                    besides(key, i)
                    if key == "f0" and i == 2:
                        half_in(ST_F0, 0)
                        magnitude()
                    if key == "f0" and i == 11:
                        split_lo(pjl[:, :], stage[:, 0:PJ_N], pjh[:, :], 4)
                    if key == "f1" and i in (21, 24, 27, 30):
                        n = i // 3 - 7
                        c = slice(1024 * n, 1024 * n + 1024)
                        split_lo(w1l[:, c], stage[:, c], w1h[:, c], 5 + n)
                    if key in ("f0", "f1"):
                        if i < NF and (key, i) not in (("f0", 0), ("f0", 1)):
                            mul(int(key[1]), i)
                        if i >= 3 and i % 3 == 2:
                            settle()
                            add_y(int(key[1]), i // 3 - 1)
                if key == "m0":
                    softplus()
                if key in ("m0", "m1"):
                    moe(int(key[1]))

        @block.tensor
        def _(pe):
            def three(dst, ah, al, bh, bl, start=True, stop=True):
                pe.matmul(dst, ah, bh, start=start, stop=False)
                pe.matmul(dst, al, bh, start=False, stop=False)
                return pe.matmul(dst, ah, bl, start=False, stop=stop)

            def free_bank(op):
                k = at[op]
                if k == first_rg:
                    pe.wait_ge(eo_done, E1)
                if k >= first_rg + 4 and op[0] != "XT":
                    pe.wait_ge(misc_free, k - 3)
                elif k:
                    pe.wait_ge(misc_free, k)

            def T(st, b):
                L = ln[st, b]
                free_bank(("T", st, b))
                pe.wait_ge(ln_xn, L + 1)
                for j in range(TB):
                    ins = pe.transpose(bank(("T", st, b))[:, P * j:P * j + P], tile(st, b, j), ident)
                ins.then_inc(misc, 1)

            def R(st, b):
                L = ln[st, b]
                free_bank(("R", st, b))
                for j in range(TB):
                    sl = slice(P * j, P * j + P)
                    ins = three(MB[:, E0 * j:E0 * j + E0], xh[part[st, b]][:, sl], xl[part[st, b]][:, sl],
                                wuh[:, W_GATE:W_N], wul[:, W_GATE:W_N])
                ins.then_inc(misc, 1)

            def up(s, i):
                st = ST_F1 if s else ST_F0
                n = 3 * NT * s + i
                t, k = divmod(i, 3)
                b, j = divmod(t, TB)
                L = ln[st, b]
                w = 512 if k < 2 else P
                sl = slice(P * j, P * j + P)
                if n >= 2:
                    pe.wait_ge(mul_done, n - 1)
                if s == 1 and i < 2:
                    pe.wait_ge(max_done, NU)
                    pe.wait_ge(exp_done, NU)
                for h in range(2):
                    c = slice(W_UNIT[k] + w * h, W_UNIT[k] + w * h + w)
                    ins = three(GU[n % 2][:, h, 0:w], xh[part[st, b]][:, sl], xl[part[st, b]][:, sl], wuh[:, c], wul[:, c])
                ins.then_inc(up_done, 1)

            def tr(s, i):
                n = 3 * NT * s + i
                k = i % 3
                t = i // 3
                if k < 2:
                    pe.wait_ge(cw_done, 2 * NT * s + 2 * t + k + 1)
                else:
                    pe.wait_ge(mul_done, n + 1)
                if n >= 2:
                    pe.wait_ge(at_done, n - 1)
                for c in range(4 if k < 2 else 1):
                    ins = pe.transpose(TRB[n % 2][:, P * c:P * c + P], act[:, n % 3, P * c:P * c + P], ident)
                ins.then_inc(tr_done, 1)

            def y(s, i):
                n = 3 * NT * s + i
                t, k = divmod(i, 3)
                pe.wait_ge(at_done, n + 1)
                if k == 0 and NT * s + t:
                    pe.wait_ge(y_read, NT * s + t)
                if k == 0 and s == 1 and t == 0:
                    pe.wait_ge(pv_read, NG)
                for c in range(4 if k < 2 else 1):
                    ins = pe.matmul(YB[:, 0:P], actT[:, n % 2, P * c:P * c + P], wds[:, 4 * k + c, :],
                                    start=(k == 0 and c == 0), stop=(k == 2))
                ins.then_inc(dn_done, 1)

            def V(st, b):
                free_bank(("V", st, b))
                for j in range(TB):
                    sl = slice(P * j, P * j + P)
                    ins = three(MB[:, sl], xh[part[st, b]][:, sl], xl[part[st, b]][:, sl],
                                pjh[:, V_OFF:V_OFF + P], pjl[:, V_OFF:V_OFF + P])
                ins.then_inc(misc, 1)

            def QK(name, st, g):
                b = g // HG
                free_bank((name, st, g))
                o = (Q_OFF if name == "Q" else K_OFF) + P * (g % HG)
                three(MB, pjh[:, o:o + P], pjl[:, o:o + P], xh[part[st, b]][:, :], xl[part[st, b]][:, :]).then_inc(misc, 1)

            def M(st, g):
                free_bank(("M", st, g))
                pe.wait_ge(max_done, UN * (g + 1))
                for q in range(TB):
                    ins = pe.transpose(MB[:, P * q:P * q + P], mpad[g % 2][:, q, :], ident)
                ins.then_inc(misc, 1)

            def slot(op):
                k = slots.index(op)
                if k >= 6:
                    name, n = slots[k - 6]
                    pe.wait_ge(max_done if name == "P1" else exp_done, n + 1)
                return SL[k % 6]

            def P1(_, i):
                g, n = divmod(i, UN)
                q, h0, nh, w = Q_UNITS[n]
                if i == 0:
                    pe.wait_ge(mul_done, NF)
                    pe.wait_ge(at_done, NF)
                    pe.wait_ge(y_read, NT)
                if n == 0:
                    pe.wait_ge(misc_free, at["Q", ST_AT, g] + 1)
                    pe.wait_ge(kz_in[g % 3], 64 * (g // 3 + 1))
                dst = slot(("P1", i))
                step = S // nh
                for h in range(nh):
                    o = step * h
                    pe.matmul(dst[:, o:o + w], qraw[g % 2][:, P * q:P * q + P], kz[g % 3][:, h0 + h, 0:w],
                              start=True, stop=False)
                    ins = pe.matmul(dst[:, o + w - P:o + w], identb[:, :], maskb[:, :], start=False, stop=True)
                ins.then_inc(p1_done, 1)

            def P2(_, i):
                g, n = divmod(i, UN)
                k, h0, nh, w = K_UNITS[n]
                if n == 0:
                    pe.wait_ge(misc_free, at["M", ST_AT, g] + 1)
                dst = slot(("P2", i))
                step = S // nh
                for h in range(nh):
                    ins = pe.matmul(dst[:, step * h:step * h + w], kz[g % 3][:, h0 + h, P * k:P * k + P],
                                    qaug[g % 2][:, S - w:S], start=True, stop=True)
                ins.then_inc(p2_done, 1)

            def PV(_, i):
                g, k = divmod(i, TB)
                b, hg = divmod(g, HG)
                w = S - P * k
                if k == 0 and g:
                    pe.wait_ge(pv_read, g)
                if k == 0 and hg == 0:
                    pe.wait_ge(misc_free, at["V", ST_AT, b] + 1)
                pe.wait_ge(tri_done, UN * g + K_LAST[k] + 1)
                for n, (tile_, h0, nh, _) in enumerate(K_UNITS):
                    for h in range(nh if tile_ == k else 0):
                        r = 32 * (h0 + h)
                        ins = pe.matmul(YB[r:r + 32, P * k:S], va[b % 2][:, k, 4 * hg + h0 + h, :],
                                        pt[(UN * g + n) % 8][:, w * h:w * h + w], start=(k == 0), stop=(k == TB - 1),
                                        tile_position=(0, r))
                ins.then_inc(pv_done, 1)

            def OT(st, g):
                free_bank(("OT", st, g))
                pe.wait_ge(pv_read, g + 1)
                for q in range(TB):
                    ins = pe.transpose(MB[:, P * q:P * q + P], ots[g % 2][:, P * q:P * q + P], ident)
                ins.then_inc(misc, 1)

            def FT(st, b):
                free_bank(("FT", st, b))
                for q in range(TB):
                    ins = pe.transpose(MB[:, P * q:P * q + P],
                                       otok[b % 2][:, q, :, :].rearrange("p h c -> p (h c)"), ident)
                ins.then_inc(misc, 1)

            def PO(st, b):
                free_bank(("PO", st, b))
                o = slice(O_OFF, O_OFF + P)
                for j in range(TB):
                    sl = slice(P * j, P * j + P)
                    ins = three(MB[:, sl], oh_[:, sl], ol_[:, sl], pjh[:, o], pjl[:, o])
                ins.then_inc(misc, 1)

            def R1(st, b):
                L = ln[st, b]
                free_bank(("R1", st, b))
                tiles = router_tiles(st, b)
                pe.wait_ge(misc_free, at["T", st, tiles.stop // TB - 1] + 1)
                for t in range(tiles.start, tiles.stop):
                    n = part[st, t // TB]
                    sl = slice(P * (t % TB), P * (t % TB) + P)
                    o = E1 * (t - tiles.start)
                    ins = three(bank(("R1", st, b))[:, o:o + E1], xh[n][:, sl], xl[n][:, sl],
                                pjh[:, G_OFF:G_OFF + E1], pjl[:, G_OFF:G_OFF + E1])
                ins.then_inc(misc, 1)

            def C(st, b):
                free_bank(("C", st, b))
                pe.wait_ge(oh_done, router_step(st, b) + 1)
                tiles = router_tiles(st, b)
                w = tiles.stop - tiles.start
                sums = bank(("C", st, b))
                pe.matmul(sums[:, 0:w * E1], trib[:, :], ohb[:, tiles, :].rearrange("p t e -> p (t e)"),
                          start=True, stop=False)
                for t in range(tiles.stop - 1):
                    first = max(t + 1 - tiles.start, 0)
                    ins = pe.matmul(sums[:, first * E1:w * E1], onesb[:, :],
                                    ohb[:, t, :].unsqueeze(1).broadcast_to([P, w - first, E1]),
                                    start=False, stop=(t == tiles.stop - 2))
                ins.then_inc(misc, 1)

            def XT(m, e):
                free_bank(("XT", m, e))
                pe.wait_ge(xe_done, E1 * m + e + 1)
                for t in range(CAP // P):
                    ins = pe.transpose(MB[:, P * t:P * t + P], xe[e % 2][:, t, :], ident)
                ins.then_inc(misc, 1)

            def U1(m, e):
                n = E1 * m + e
                pe.wait_ge(misc_free, at["XT", m, e] + 1)
                if n >= 2:
                    pe.wait_ge(ha, n - 1)
                    pe.wait_ge(hb, n - 1)
                if n == 0:
                    pe.wait_ge(w_lo, 8)
                for c in range(HC):
                    o = slice(H1 * e + P * c, H1 * e + P * c + P)
                    ins = three(GU[e % 2][:, c // 2, CAP * (c % 2):CAP * (c % 2) + CAP], w1h[:, o], w1l[:, o],
                                dh[e % 2][:, :], dl[e % 2][:, :])
                ins.then_inc(up1, 1)

            def D1(m, e):
                n = E1 * m + e
                pe.wait_ge(ha, n + 1)
                pe.wait_ge(hb, n + 1)
                if n >= 2:
                    pe.wait_ge(eo_done, n - 1)
                if n == 0:
                    pe.wait_ge(in_w2, 16)
                for t in range(CAP // P):
                    for c in range(HC):
                        ins = pe.matmul(TRB[e % 2][:, P * t:P * t + P], hT[e % 2][:, c, P * t:P * t + P],
                                        w2s[:, HC * e + c, :], start=(c == 0), stop=(c == HC - 1))
                ins.then_inc(dn1, 1)

            def G(st, b):
                pe.wait_ge(misc_free, at["T", ST_RG, b] + 1)
                if b >= 2:
                    pe.wait_ge(rg_sig, b - 1)
                for k, o in ((0, A_OFF), (1, X_OFF)):
                    ins = three(GU[b % 2][:, k, :], pjh[:, o:o + P], pjl[:, o:o + P],
                                xh[part[st, b]][:, :], xl[part[st, b]][:, :])
                ins.then_inc(rg_mm, 1)

            def YT(st, b):
                free_bank(("YT", ST_RG, b))
                pe.wait_ge(rg_y, b + 1)
                for j in range(TB):
                    c = S * b + P * j
                    ins = pe.transpose(bank(("YT", st, b))[:, P * j:P * j + P], rr[:, c:c + P], ident)
                ins.then_inc(misc, 1)

            pe.wait_ge(in_c, 16)
            STEP = {"T": T, "R": R, "up": up, "tr": tr, "y": y, "V": V, "M": M, "P1": P1, "P2": P2, "PV": PV, "OT": OT,
                    "FT": FT, "PO": PO, "R1": R1, "C": C, "XT": XT, "U1": U1, "D1": D1, "G": G, "YT": YT}
            for name, st, n in plan_pe:
                if name == "R" and (st, n) == (ST_F0, 0):
                    pe.wait_ge(w_lo, 1)
                if name == "y" and (st, n) == (0, 0):
                    pe.wait_ge(in_p, 16)
                if name == "up" and st == 0 and n < 2:
                    pe.wait_ge(w_lo, 2 + n)
                if name == "V" and n == 0:
                    pe.wait_ge(w_lo, 4)
                    pe.wait_ge(c_cast, C_CASTS)
                    pe.wait_ge(presets, PRESETS)
                if name in ("Q", "K"):
                    QK(name, st, n)
                else:
                    STEP[name](st, n)


def constants(np):
    c = np.zeros((P, C_N), np.float32)
    r = np.arange(P)
    c[:, C_ID:C_ID + P] = np.eye(P)
    c[:, C_TRI:C_TRI + P] = r[:, None] < r[None, :]
    c[:, C_MASK:C_MASK + P] = np.where(r[None, :] > r[:, None], -BIG, 0)
    e = np.arange(G0)
    m = np.stack([e[None, :] > e[:, None], e[None, :] < e[:, None]], 1)
    c[:, C_MG:C_MG + 2 * G0 * G0] = m.reshape(1, -1)
    c[:, C_NI8:C_NI8 + E1] = E1 - np.arange(E1)
    c[:, C_E256:C_E256 + E1] = CAP * np.arange(E1)
    q = r % 32
    c[:, C_CQ] = np.where(q // 8 == 1, -1, 0)
    c[:, C_CK] = np.where(q // 8 == 2, -1, 0) + (q == 24)
    c[:, C_KB] = q == 24
    c[:, C_TOK:C_N] = r[:, None] + P * np.arange(NT)
    return c


def kernel(**inputs):
    import numpy as np
    import concourse.bacc as bacc
    from concourse.bass_utils import run_bass_kernel_spmd as run

    a = {k: np.asarray(v) for k, v in inputs.items()}
    Wg, Wu = (a["L0_ffn_" + k].reshape(E0 * I0, P).T for k in ("Wg", "Wu"))
    half = E0 * I0 // 2
    wup = np.concatenate([Wg[:, :half], Wu[:, :half], Wg[:, half:], Wu[:, half:],
                          a["L0_ffn_Ws_g"].T, a["L0_ffn_Ws_u"].T, a["L0_ffn_gate_w"].T], 1)
    wdn = np.concatenate([a["L0_ffn_Wd"].transpose(0, 2, 1).reshape(E0 * I0, P), a["L0_ffn_Ws_d"].T], 0)
    wdn = wdn.reshape(9, P, P).transpose(1, 0, 2)

    def heads(w):
        w = w.T.reshape(P, NH, 1, DH)
        return np.concatenate([w, w, w, np.zeros_like(w)], 2).reshape(P, NH * 32)

    proj = np.concatenate([heads(a["L0_attn_q_proj_weight"]), heads(a["L0_attn_k_proj_weight"]),
                           a["L0_attn_v_proj_weight"].T, a["L0_attn_o_proj_weight"].T,
                           a["L1_attn_Wa"].T, a["L1_attn_Wx"].T, a["L1_ffn_wg"]], 1)
    w1 = a["L1_ffn_w1"].transpose(1, 0, 2).reshape(P, E1 * H1)
    w2 = a["L1_ffn_w2"].reshape(E1 * HC, P, P).transpose(1, 0, 2)
    vecs = np.concatenate([a["L1_attn_Lam"][:, None], a["L1_attn_ba"][:, None], a["L1_attn_bx"][:, None],
                           a["L1_ffn_b1"].reshape(E1 * HC, P).T], 1)
    laid = dict(x_in=a["L0_attn_in_features"].reshape(B * S, P), wup=wup, wdn=wdn, proj=proj, w1=w1, w2=w2,
                vecs=vecs, bias0=a["L0_ffn_gate_bias"], b2=a["L1_ffn_b2"], consts=constants(np))
    nc = bacc.Bacc("TRN2", target_bir_lowering=False, num_devices=1)
    arrays, args = {}, []
    for name, v in laid.items():
        v = np.ascontiguousarray(v)
        arrays[f"in_{name}"] = v
        args.append(nc.dram_tensor(f"in_{name}", v.shape, mybir.dt.from_np(v.dtype), kind="ExternalInput").ap())
    out = nc.dram_tensor("out_x", (B * S, P), F32, kind="ExternalOutput").ap()
    build(nc, *args, out)
    r = run(nc, [arrays], core_ids=[0])
    return r.results[0]["out_x"].reshape(B, S, P)
```
